# Optimizing a Trainium2 kernel written in Bass

```python
import numpy as np
import jax
import jax.numpy as jnp

def _softmax(x, axis=-1):
    return jax.nn.softmax(x, axis=axis)

def _gelu(x):
    return jax.nn.gelu(x, approximate=True)

def _silu(x):
    return jax.nn.silu(x)

def _sigmoid(x):
    return jax.nn.sigmoid(x)

def _layernorm(x, axis=-1, eps=1e-05):
    m = jnp.mean(x, axis=axis, keepdims=True)
    v = jnp.var(x, axis=axis, keepdims=True)
    return (x - m) / jnp.sqrt(v + eps)

def _scatter_add(tgt, idx, src, axis=0):
    return tgt.at[idx].add(src)

def _segment_sum(src, seg, n):
    return jax.ops.segment_sum(src, seg, n)
kernel_name = 'mk_xattn_ffn_d4_seqx_r8_a6e208'

def setup_inputs(seed: int=0):
    np.random.seed(seed)
    _w = jnp.asarray

    def _rec_inputs():
        import jax
        import jax.numpy as jnp
        _rk = jax.random.key(seed)
        x = -0.0002928 + 1 * jax.random.normal(jax.random.fold_in(_rk, 1), (32, 128, 128), jnp.float32)
        _lenS = 128 - jax.random.randint(jax.random.fold_in(_rk, 7), (32,), 0, max(1, 128 // 4) + 1, jnp.int32)
        _lenS2 = 128 - jax.random.randint(jax.random.fold_in(_rk, 8), (32,), 0, max(1, 128 // 4) + 1, jnp.int32)
        _ctx_768P = jax.random.normal(jax.random.fold_in(_rk, 11), (32, 16, 96), jnp.float32)
        _ctx_768c = jax.random.dirichlet(jax.random.fold_in(_rk, 511), 0.3 * jnp.ones((16,), jnp.float32), (32, 128))
        _ctx_768t = jnp.einsum('bsk,bkd->bsd', _ctx_768c, _ctx_768P)
        _ctx_768t = _ctx_768t * jax.lax.rsqrt(jnp.mean(jnp.square(_ctx_768t)) + 1e-12) * 0.953939
        ctx_768 = 2.09791e-05 + 1.00001 * (_ctx_768t + 0.3 * jax.random.normal(jax.random.fold_in(_rk, 611), (32, 128, 96), jnp.float32))
        _validS = jnp.arange(128)[None, :] < _lenS[:, None]
        _validS2 = jnp.arange(128)[None, :] < _lenS2[:, None]
        _causal = jnp.tril(jnp.ones((128, 128), dtype=bool))
        mask_BxS_bk0 = jnp.logical_not(jnp.broadcast_to(_validS[:, :], (32, 128)))
        return (x, ctx_768, mask_BxS_bk0)
    x, ctx_768, mask_BxS_bk0 = _rec_inputs()

    def _L0_xattn_setup():
        import jax, jax.numpy as jnp
        import numpy as np
        N_HEADS = 16
        EMBED_DIM = 128
        CROSS_DIM = 96
        HEAD_DIM = EMBED_DIM // N_HEADS
        key = jax.random.key(seed)
        ks = jax.random.split(key, 12)
        B, SQ, SKV = (2, 256, 256)
        s_in = 1.0 / np.sqrt(EMBED_DIM)
        s_cross = 1.0 / np.sqrt(CROSS_DIM)
        return {'x': jax.random.normal(ks[0], (B, SQ, EMBED_DIM), jnp.float32), 'y': jax.random.normal(ks[1], (B, SKV, CROSS_DIM), jnp.float32), 'wq': jax.random.normal(ks[2], (EMBED_DIM, EMBED_DIM), jnp.float32) * s_in, 'bq': jax.random.normal(ks[3], (EMBED_DIM,), jnp.float32) * s_in, 'wk': jax.random.normal(ks[4], (EMBED_DIM, CROSS_DIM), jnp.float32) * s_cross, 'bk': jax.random.normal(ks[5], (EMBED_DIM,), jnp.float32) * s_cross, 'wv': jax.random.normal(ks[6], (EMBED_DIM, CROSS_DIM), jnp.float32) * s_cross, 'bv': jax.random.normal(ks[7], (EMBED_DIM,), jnp.float32) * s_cross, 'wo': jax.random.normal(ks[8], (EMBED_DIM, EMBED_DIM), jnp.float32) * s_in, 'bo': jax.random.normal(ks[9], (EMBED_DIM,), jnp.float32) * s_in}
    _L0_xattn_all = _L0_xattn_setup()
    _L0_xattn_in = {k: v for k, v in _L0_xattn_all.items() if k in ('wq', 'bq', 'wk', 'bk', 'wv', 'bv', 'wo', 'bo')}
    del _L0_xattn_all

    def _L0_ffn_setup():
        import jax, jax.numpy as jnp
        import numpy as np
        D = 128
        N_EXP = 8
        TOP_K = 1
        key = jax.random.key(seed)
        ks = jax.random.split(key, 7)
        s = 0.02
        return {'x': jax.random.normal(ks[0], (4, 256, D), jnp.float32), 'gate_w': jax.random.normal(ks[1], (D, N_EXP), jnp.float32) * s, 'gate_b': jnp.zeros((N_EXP,), jnp.float32), 'w1': jax.random.normal(ks[2], (N_EXP, D, 4 * D), jnp.float32) * s, 'b1': jnp.zeros((N_EXP, 4 * D), jnp.float32), 'w2': jax.random.normal(ks[3], (N_EXP, 4 * D, D), jnp.float32) * s, 'b2': jnp.zeros((N_EXP, D), jnp.float32)}
    _L0_ffn_all = _L0_ffn_setup()
    _L0_ffn_in = {k: v for k, v in _L0_ffn_all.items() if k in ('gate_w', 'gate_b', 'w1', 'b1', 'w2', 'b2')}
    del _L0_ffn_all

    def _L1_xattn_setup():
        import jax, jax.numpy as jnp
        import numpy as np
        IMG_DIM, TXT_DIM, HID = (128, 96, 128)
        B, LQ, LK = (8, 256, 256)
        key = jax.random.key(seed)
        ks = jax.random.split(key, 8)
        s_img = 1.0 / np.sqrt(IMG_DIM)
        s_txt = 1.0 / np.sqrt(TXT_DIM)
        return {'image_features': jax.random.normal(ks[0], (B, LQ, IMG_DIM), jnp.float32), 'text_features': jax.random.normal(ks[1], (B, LK, TXT_DIM), jnp.float32), 'Wq': jax.random.uniform(ks[2], (IMG_DIM, HID), jnp.float32, -s_img, s_img), 'bq': jax.random.uniform(ks[3], (HID,), jnp.float32, -s_img, s_img), 'Wk': jax.random.uniform(ks[4], (TXT_DIM, HID), jnp.float32, -s_txt, s_txt), 'bk': jax.random.uniform(ks[5], (HID,), jnp.float32, -s_txt, s_txt), 'Wv': jax.random.uniform(ks[6], (TXT_DIM, HID), jnp.float32, -s_txt, s_txt), 'bv': jax.random.uniform(ks[7], (HID,), jnp.float32, -s_txt, s_txt)}
    _L1_xattn_all = _L1_xattn_setup()
    _L1_xattn_in = {k: v for k, v in _L1_xattn_all.items() if k in ('Wq', 'bq', 'Wk', 'bk', 'Wv', 'bv')}
    del _L1_xattn_all

    def _L1_ffn_setup():
        import jax, jax.numpy as jnp
        import numpy as np
        B, L, D = (2, 256, 128)
        E = 15
        H = D * 1
        K = 3
        T = 1.0
        key = jax.random.key(seed)
        ks = jax.random.split(key, 12)
        s = 0.02
        return {'x': jax.random.normal(ks[0], (B, L, D), dtype=jnp.float32), 'router_W': jax.random.normal(ks[1], (D, E), dtype=jnp.float32) * s, 'router_b': jnp.zeros((E,), dtype=jnp.float32), 'sW1': jax.random.normal(ks[2], (D, H), dtype=jnp.float32) * s, 'sb1': jnp.zeros((H,), dtype=jnp.float32), 'sW2': jax.random.normal(ks[3], (H, D), dtype=jnp.float32) * s, 'sb2': jnp.zeros((D,), dtype=jnp.float32), 'eW1': jax.random.normal(ks[4], (E, D, H), dtype=jnp.float32) * s, 'eb1': jnp.zeros((E, H), dtype=jnp.float32), 'eW2': jax.random.normal(ks[5], (E, H, D), dtype=jnp.float32) * s, 'eb2': jnp.zeros((E, D), dtype=jnp.float32)}
    _L1_ffn_all = _L1_ffn_setup()
    _L1_ffn_in = {k: v for k, v in _L1_ffn_all.items() if k in ('router_W', 'router_b', 'sW1', 'sb1', 'sW2', 'sb2', 'eW1', 'eb1', 'eW2', 'eb2')}
    del _L1_ffn_all

    def _L2_xattn_setup():
        import jax, jax.numpy as jnp
        import numpy as np
        NUM_HEADS = 16
        key = jax.random.key(seed)
        k1, k2, k3, k4, k5 = jax.random.split(key, 5)
        B, N, C = (4, 256, 128)
        N2, Cy = (128, 96)
        x = jax.random.normal(k1, (B, N, C), dtype=jnp.float32)
        y = jax.random.normal(k2, (B, N2, Cy), dtype=jnp.float32)
        pad_mask = jax.random.randint(k3, (B, N), 0, 2).astype(jnp.bool_)
        Wq = jax.random.normal(k4, (C, C), dtype=jnp.float32) * C ** (-0.5)
        Wkv = jax.random.normal(k5, (2 * C, Cy), dtype=jnp.float32) * Cy ** (-0.5)
        return {'x': x, 'y': y, 'pad_mask': pad_mask, 'Wq': Wq, 'Wkv': Wkv}
    _L2_xattn_all = _L2_xattn_setup()
    _L2_xattn_in = {k: v for k, v in _L2_xattn_all.items() if k in ('Wq', 'Wkv')}
    del _L2_xattn_all

    def _L2_ffn_setup():
        import jax, jax.numpy as jnp
        import numpy as np
        DIM = 128
        NQ = 16
        NKV = 4
        HD = DIM // NQ
        HID = 256
        E = 8
        B, S = (1, 128)
        EPS = 1e-06

        def rmsnorm(x, w):
            ms = jnp.mean(x * x, axis=-1, keepdims=True)
            return w * (x * jax.lax.rsqrt(ms + EPS))

        def rope_tables(seq_len, head_dim):
            inv_freq = 1.0 / 10000.0 ** (jnp.arange(0, head_dim, 2, dtype=jnp.float32) / head_dim)
            t = jnp.arange(seq_len, dtype=jnp.float32)
            freqs = jnp.einsum('i,j->ij', t, inv_freq)
            return (jnp.cos(freqs), jnp.sin(freqs))

        def apply_rope(x, cos, sin):
            c = cos[None, :, None, :]
            s = sin[None, :, None, :]
            half = x.shape[-1] // 2
            x1, x2 = (x[..., :half], x[..., half:])
            return jnp.concatenate([x1 * c - x2 * s, x1 * s + x2 * c], axis=-1)

        def _forward(x, ln1_w, ln2_w, Wq, bq, Wk, bk, Wv, bv, qn_w, kn_w, Wg, bg, Wo, bo, Wr, br, W1, b1, W2, b2):
            batch, seq, _ = x.shape
            cos, sin = rope_tables(seq, HD)
            h = rmsnorm(x, ln1_w)
            q = (h @ Wq + bq).reshape(batch, seq, NQ, HD)
            k = (h @ Wk + bk).reshape(batch, seq, NKV, HD)
            v = (h @ Wv + bv).reshape(batch, seq, NKV, HD)
            q = rmsnorm(apply_rope(q, cos, sin), qn_w)
            k = rmsnorm(apply_rope(k, cos, sin), kn_w)
            rep = NQ // NKV
            k = jnp.repeat(k, rep, axis=2)
            v = jnp.repeat(v, rep, axis=2)
            scores = jnp.einsum('bthd,bshd->bhts', q, k) / np.sqrt(HD)
            causal = jnp.tril(jnp.ones((seq, seq), dtype=bool))
            scores = jnp.where(causal[None, None], scores, -jnp.inf)
            attn = jax.nn.softmax(scores, axis=-1)
            out = jnp.einsum('bhts,bshd->bthd', attn, v)
            gate = jax.nn.sigmoid(out @ Wg + bg)
            out = (out * gate).reshape(batch, seq, DIM)
            x = x + out @ Wo + bo
            h2 = rmsnorm(x, ln2_w)
            logits = h2 @ Wr + br
            top1 = jnp.argmax(logits, axis=-1).reshape(-1)
            xt = h2.reshape(-1, DIM)
            u = jnp.einsum('td,edf->tef', xt, W1) + b1
            u1, u2 = (u[..., :HID], u[..., HID:])
            act = u1 * jax.nn.sigmoid(u2)
            y_all = jnp.einsum('teh,ehd->ted', act, W2) + b2
            y = jnp.take_along_axis(y_all, top1[:, None, None], axis=1)[:, 0, :]
            return x + y.reshape(batch, seq, DIM)
        key = jax.random.key(seed)
        ks = jax.random.split(key, 20)
        sc = lambda fan_in: 1.0 / np.sqrt(fan_in)
        d = {}
        d['x'] = jax.random.normal(ks[0], (B, S, DIM), dtype=jnp.float32)
        d['ln1_w'] = jnp.ones((DIM,), jnp.float32)
        d['ln2_w'] = jnp.ones((DIM,), jnp.float32)
        d['Wq'] = jax.random.normal(ks[1], (DIM, DIM), jnp.float32) * sc(DIM)
        d['bq'] = jnp.zeros((DIM,), jnp.float32)
        d['Wk'] = jax.random.normal(ks[2], (DIM, HD * NKV), jnp.float32) * sc(DIM)
        d['bk'] = jnp.zeros((HD * NKV,), jnp.float32)
        d['Wv'] = jax.random.normal(ks[3], (DIM, HD * NKV), jnp.float32) * sc(DIM)
        d['bv'] = jnp.zeros((HD * NKV,), jnp.float32)
        d['qn_w'] = jnp.ones((HD,), jnp.float32)
        d['kn_w'] = jnp.ones((HD,), jnp.float32)
        d['Wg'] = jax.random.normal(ks[4], (HD, HD), jnp.float32) * sc(HD)
        d['bg'] = jnp.zeros((HD,), jnp.float32)
        d['Wo'] = jax.random.normal(ks[5], (DIM, DIM), jnp.float32) * sc(DIM)
        d['bo'] = jnp.zeros((DIM,), jnp.float32)
        d['Wr'] = jax.random.normal(ks[6], (DIM, E), jnp.float32) * sc(DIM)
        d['br'] = jnp.zeros((E,), jnp.float32)
        d['W1'] = jax.random.normal(ks[7], (E, DIM, 2 * HID), jnp.float32) * sc(DIM)
        d['b1'] = jnp.zeros((E, 2 * HID), jnp.float32)
        d['W2'] = jax.random.normal(ks[8], (E, HID, DIM), jnp.float32) * sc(HID)
        d['b2'] = jnp.zeros((E, DIM), jnp.float32)
        return d
    _L2_ffn_all = _L2_ffn_setup()
    _L2_ffn_in = {k: v for k, v in _L2_ffn_all.items() if k in ('ln1_w', 'ln2_w', 'Wq', 'bq', 'Wk', 'bk', 'Wv', 'bv', 'qn_w', 'kn_w', 'Wg', 'bg', 'Wo', 'bo', 'Wr', 'br', 'W1', 'b1', 'W2', 'b2')}
    del _L2_ffn_all

    def _L3_xattn_setup():
        import jax, jax.numpy as jnp
        import numpy as np
        HEADS = 8
        DIM_HEAD = 64
        QUERY_DIM = 128
        CONTEXT_DIM = 96
        INNER = HEADS * DIM_HEAD
        key = jax.random.key(seed)
        ks = jax.random.split(key, 7)
        B, Sq, Skv = (4, 512, 128)
        x = jax.random.normal(ks[0], (B, Sq, QUERY_DIM), dtype=jnp.float32)
        context = jax.random.normal(ks[1], (B, Skv, CONTEXT_DIM), dtype=jnp.float32)
        Wq = jax.random.normal(ks[2], (QUERY_DIM, INNER), dtype=jnp.float32) * QUERY_DIM ** (-0.5)
        Wk = jax.random.normal(ks[3], (CONTEXT_DIM, INNER), dtype=jnp.float32) * CONTEXT_DIM ** (-0.5)
        Wv = jax.random.normal(ks[4], (CONTEXT_DIM, INNER), dtype=jnp.float32) * CONTEXT_DIM ** (-0.5)
        Wo = jax.random.normal(ks[5], (INNER, QUERY_DIM), dtype=jnp.float32) * INNER ** (-0.5)
        bo = jax.random.normal(ks[6], (QUERY_DIM,), dtype=jnp.float32) * 0.01
        return {'x': x, 'context': context, 'Wq': Wq, 'Wk': Wk, 'Wv': Wv, 'Wo': Wo, 'bo': bo}
    _L3_xattn_all = _L3_xattn_setup()
    _L3_xattn_in = {k: v for k, v in _L3_xattn_all.items() if k in ('Wq', 'Wk', 'Wv', 'Wo', 'bo')}
    del _L3_xattn_all

    def _L3_ffn_setup():
        import jax, jax.numpy as jnp
        import numpy as np
        H = 128
        E = 8
        B, S = (4, 256)
        key = jax.random.key(seed)
        k1, k2, k3, k4 = jax.random.split(key, 4)
        x = jax.random.normal(k1, (B, S, H), dtype=jnp.float32)
        wg = jax.random.normal(k2, (H, E), dtype=jnp.float32) * 0.02
        W = jax.random.normal(k3, (E, H, H), dtype=jnp.float32) * 0.02
        b = jax.random.normal(k4, (E, H), dtype=jnp.float32) * 0.02
        return {'x': x, 'wg': wg, 'W': W, 'b': b}
    _L3_ffn_all = _L3_ffn_setup()
    _L3_ffn_in = {k: v for k, v in _L3_ffn_all.items() if k in ('wg', 'W', 'b')}
    del _L3_ffn_all
    return {'x': x, 'ctx_768': ctx_768, 'mask_BxS_bk0': mask_BxS_bk0, 'L0_xattn_wq': _L0_xattn_in['wq'], 'L0_xattn_bq': _L0_xattn_in['bq'], 'L0_xattn_wk': _L0_xattn_in['wk'], 'L0_xattn_bk': _L0_xattn_in['bk'], 'L0_xattn_wv': _L0_xattn_in['wv'], 'L0_xattn_bv': _L0_xattn_in['bv'], 'L0_xattn_wo': _L0_xattn_in['wo'], 'L0_xattn_bo': _L0_xattn_in['bo'], 'L0_ffn_gate_w': _L0_ffn_in['gate_w'], 'L0_ffn_gate_b': _L0_ffn_in['gate_b'], 'L0_ffn_w1': _L0_ffn_in['w1'], 'L0_ffn_b1': _L0_ffn_in['b1'], 'L0_ffn_w2': _L0_ffn_in['w2'], 'L0_ffn_b2': _L0_ffn_in['b2'], 'L1_xattn_Wq': _L1_xattn_in['Wq'], 'L1_xattn_bq': _L1_xattn_in['bq'], 'L1_xattn_Wk': _L1_xattn_in['Wk'], 'L1_xattn_bk': _L1_xattn_in['bk'], 'L1_xattn_Wv': _L1_xattn_in['Wv'], 'L1_xattn_bv': _L1_xattn_in['bv'], 'L1_ffn_router_W': _L1_ffn_in['router_W'], 'L1_ffn_router_b': _L1_ffn_in['router_b'], 'L1_ffn_sW1': _L1_ffn_in['sW1'], 'L1_ffn_sb1': _L1_ffn_in['sb1'], 'L1_ffn_sW2': _L1_ffn_in['sW2'], 'L1_ffn_sb2': _L1_ffn_in['sb2'], 'L1_ffn_eW1': _L1_ffn_in['eW1'], 'L1_ffn_eb1': _L1_ffn_in['eb1'], 'L1_ffn_eW2': _L1_ffn_in['eW2'], 'L1_ffn_eb2': _L1_ffn_in['eb2'], 'L2_xattn_Wq': _L2_xattn_in['Wq'], 'L2_xattn_Wkv': _L2_xattn_in['Wkv'], 'L2_ffn_ln1_w': _L2_ffn_in['ln1_w'], 'L2_ffn_ln2_w': _L2_ffn_in['ln2_w'], 'L2_ffn_Wq': _L2_ffn_in['Wq'], 'L2_ffn_bq': _L2_ffn_in['bq'], 'L2_ffn_Wk': _L2_ffn_in['Wk'], 'L2_ffn_bk': _L2_ffn_in['bk'], 'L2_ffn_Wv': _L2_ffn_in['Wv'], 'L2_ffn_bv': _L2_ffn_in['bv'], 'L2_ffn_qn_w': _L2_ffn_in['qn_w'], 'L2_ffn_kn_w': _L2_ffn_in['kn_w'], 'L2_ffn_Wg': _L2_ffn_in['Wg'], 'L2_ffn_bg': _L2_ffn_in['bg'], 'L2_ffn_Wo': _L2_ffn_in['Wo'], 'L2_ffn_bo': _L2_ffn_in['bo'], 'L2_ffn_Wr': _L2_ffn_in['Wr'], 'L2_ffn_br': _L2_ffn_in['br'], 'L2_ffn_W1': _L2_ffn_in['W1'], 'L2_ffn_b1': _L2_ffn_in['b1'], 'L2_ffn_W2': _L2_ffn_in['W2'], 'L2_ffn_b2': _L2_ffn_in['b2'], 'L3_xattn_Wq': _L3_xattn_in['Wq'], 'L3_xattn_Wk': _L3_xattn_in['Wk'], 'L3_xattn_Wv': _L3_xattn_in['Wv'], 'L3_xattn_Wo': _L3_xattn_in['Wo'], 'L3_xattn_bo': _L3_xattn_in['bo'], 'L3_ffn_wg': _L3_ffn_in['wg'], 'L3_ffn_W': _L3_ffn_in['W'], 'L3_ffn_b': _L3_ffn_in['b']}

def reference(x, ctx_768, mask_BxS_bk0, L0_xattn_wq, L0_xattn_bq, L0_xattn_wk, L0_xattn_bk, L0_xattn_wv, L0_xattn_bv, L0_xattn_wo, L0_xattn_bo, L0_ffn_gate_w, L0_ffn_gate_b, L0_ffn_w1, L0_ffn_b1, L0_ffn_w2, L0_ffn_b2, L1_xattn_Wq, L1_xattn_bq, L1_xattn_Wk, L1_xattn_bk, L1_xattn_Wv, L1_xattn_bv, L1_ffn_router_W, L1_ffn_router_b, L1_ffn_sW1, L1_ffn_sb1, L1_ffn_sW2, L1_ffn_sb2, L1_ffn_eW1, L1_ffn_eb1, L1_ffn_eW2, L1_ffn_eb2, L2_xattn_Wq, L2_xattn_Wkv, L2_ffn_ln1_w, L2_ffn_ln2_w, L2_ffn_Wq, L2_ffn_bq, L2_ffn_Wk, L2_ffn_bk, L2_ffn_Wv, L2_ffn_bv, L2_ffn_qn_w, L2_ffn_kn_w, L2_ffn_Wg, L2_ffn_bg, L2_ffn_Wo, L2_ffn_bo, L2_ffn_Wr, L2_ffn_br, L2_ffn_W1, L2_ffn_b1, L2_ffn_W2, L2_ffn_b2, L3_xattn_Wq, L3_xattn_Wk, L3_xattn_Wv, L3_xattn_Wo, L3_xattn_bo, L3_ffn_wg, L3_ffn_W, L3_ffn_b):
    import jax
    import jax.numpy as jnp

    def _L0_xattn_ref(x, y, wq, bq, wk, bk, wv, bv, wo, bo):
        import jax, jax.numpy as jnp
        import numpy as np
        N_HEADS = 16
        EMBED_DIM = 128
        CROSS_DIM = 96
        HEAD_DIM = EMBED_DIM // N_HEADS
        B, SQ, E = x.shape
        q = x @ wq.T + bq
        k = y @ wk.T + bk
        v = y @ wv.T + bv
        q = q.reshape(B, SQ, N_HEADS, HEAD_DIM).transpose(0, 2, 1, 3)
        k = k.reshape(B, -1, N_HEADS, HEAD_DIM).transpose(0, 2, 1, 3)
        v = v.reshape(B, -1, N_HEADS, HEAD_DIM).transpose(0, 2, 1, 3)
        scale = 1.0 / jnp.sqrt(jnp.asarray(HEAD_DIM, x.dtype))
        score = jnp.einsum('bhqd,bhkd->bhqk', q, k) * scale
        attn = jax.nn.softmax(score, axis=-1)
        out = jnp.einsum('bhqk,bhkd->bhqd', attn, v)
        out = out.transpose(0, 2, 1, 3).reshape(B, SQ, E)
        return out @ wo.T + bo

    def _L0_ffn_ref(x, gate_w, gate_b, w1, b1, w2, b2):
        import jax, jax.numpy as jnp
        import numpy as np
        D = 128
        N_EXP = 8
        TOP_K = 1
        b, s, d = x.shape
        xf = x.reshape(-1, d)
        logits = xf @ gate_w + gate_b
        pb = jax.nn.softmax(logits, axis=-1)
        _, idx = jax.lax.top_k(pb, TOP_K)
        sel = jnp.any(idx[:, :, None] == jnp.arange(N_EXP)[None, None, :], axis=1)
        weights = pb * sel

        def expert_step(acc, params):
            w1e, b1e, w2e, b2e, wgt = params
            h = jax.nn.gelu(xf @ w1e + b1e, approximate=False)
            y = h @ w2e + b2e
            return (acc + wgt[:, None] * y, None)
        out0 = jnp.zeros_like(xf)
        out, _ = jax.lax.scan(expert_step, out0, (w1, b1, w2, b2, weights.T))
        return out.reshape(b, s, d)

    def _L1_xattn_ref(image_features, text_features, Wq, bq, Wk, bk, Wv, bv):
        import jax, jax.numpy as jnp
        import numpy as np
        IMG_DIM, TXT_DIM, HID = (128, 96, 128)
        B, LQ, LK = (8, 256, 256)
        query = jnp.einsum('bqi,ih->bqh', image_features, Wq) + bq
        key = jnp.einsum('bkt,th->bkh', text_features, Wk) + bk
        value = jnp.einsum('bkt,th->bkh', text_features, Wv) + bv
        scale = 1.0 / jnp.sqrt(jnp.asarray(HID, query.dtype))
        scores = jnp.einsum('bqh,bkh->bqk', query, key) * scale
        weights = jax.nn.softmax(scores, axis=-1)
        attended = jnp.einsum('bqk,bkh->bqh', weights, value)
        return attended

    def _L1_ffn_ref(x, router_W, router_b, sW1, sb1, sW2, sb2, eW1, eb1, eW2, eb2):
        import jax, jax.numpy as jnp
        import numpy as np
        B, L, D = (2, 256, 128)
        E = 15
        H = D * 1
        K = 3
        T = 1.0
        b, l, d = x.shape
        n = b * l
        xt = x.reshape(n, d)
        shared = jax.nn.relu(xt @ sW1 + sb1) @ sW2 + sb2
        logits = xt @ router_W + router_b
        probs = jax.nn.softmax(logits / T, axis=-1)
        top_p, top_i = jax.lax.top_k(probs, K)
        cw = jnp.zeros((n, E), dtype=probs.dtype)
        cw = cw.at[jnp.arange(n)[:, None], top_i].set(top_p)
        h = jax.nn.relu(jnp.einsum('nd,edh->neh', xt, eW1) + eb1)
        ye = jnp.einsum('neh,ehd->ned', h, eW2) + eb2
        routed = jnp.einsum('ned,ne->nd', ye, cw)
        return (shared + routed).reshape(b, l, d)

    def _L2_xattn_ref(x, y, pad_mask, Wq, Wkv):
        import jax, jax.numpy as jnp
        import numpy as np
        NUM_HEADS = 16
        B, N, C = x.shape
        N2 = y.shape[1]
        H = NUM_HEADS
        d = C // H
        scale = d ** (-0.5)
        q = (x @ Wq.T).reshape(B, N, H, d).transpose(0, 2, 1, 3)
        kv = (y @ Wkv.T).reshape(B, N2, 2, H, d).transpose(2, 0, 3, 1, 4)
        k, v = (kv[0], kv[1])
        attn = jnp.einsum('bhnd,bhmd->bhnm', q * scale, k)
        attn = jnp.where(pad_mask[:, None, :, None], attn, jnp.float32(-1000000000.0))
        attn = jax.nn.softmax(attn, axis=-1)
        out = jnp.einsum('bhnm,bhmd->bhnd', attn, v)
        return out.transpose(0, 2, 1, 3).reshape(B, N, C)

    def _L2_ffn_ref(x, ln1_w, ln2_w, Wq, bq, Wk, bk, Wv, bv, qn_w, kn_w, Wg, bg, Wo, bo, Wr, br, W1, b1, W2, b2):
        import jax, jax.numpy as jnp
        import numpy as np
        DIM = 128
        NQ = 16
        NKV = 4
        HD = DIM // NQ
        HID = 256
        E = 8
        B, S = (1, 128)
        EPS = 1e-06

        def rmsnorm(x, w):
            ms = jnp.mean(x * x, axis=-1, keepdims=True)
            return w * (x * jax.lax.rsqrt(ms + EPS))

        def rope_tables(seq_len, head_dim):
            inv_freq = 1.0 / 10000.0 ** (jnp.arange(0, head_dim, 2, dtype=jnp.float32) / head_dim)
            t = jnp.arange(seq_len, dtype=jnp.float32)
            freqs = jnp.einsum('i,j->ij', t, inv_freq)
            return (jnp.cos(freqs), jnp.sin(freqs))

        def apply_rope(x, cos, sin):
            c = cos[None, :, None, :]
            s = sin[None, :, None, :]
            half = x.shape[-1] // 2
            x1, x2 = (x[..., :half], x[..., half:])
            return jnp.concatenate([x1 * c - x2 * s, x1 * s + x2 * c], axis=-1)

        def _forward(x, ln1_w, ln2_w, Wq, bq, Wk, bk, Wv, bv, qn_w, kn_w, Wg, bg, Wo, bo, Wr, br, W1, b1, W2, b2):
            batch, seq, _ = x.shape
            cos, sin = rope_tables(seq, HD)
            h = rmsnorm(x, ln1_w)
            q = (h @ Wq + bq).reshape(batch, seq, NQ, HD)
            k = (h @ Wk + bk).reshape(batch, seq, NKV, HD)
            v = (h @ Wv + bv).reshape(batch, seq, NKV, HD)
            q = rmsnorm(apply_rope(q, cos, sin), qn_w)
            k = rmsnorm(apply_rope(k, cos, sin), kn_w)
            rep = NQ // NKV
            k = jnp.repeat(k, rep, axis=2)
            v = jnp.repeat(v, rep, axis=2)
            scores = jnp.einsum('bthd,bshd->bhts', q, k) / np.sqrt(HD)
            causal = jnp.tril(jnp.ones((seq, seq), dtype=bool))
            scores = jnp.where(causal[None, None], scores, -jnp.inf)
            attn = jax.nn.softmax(scores, axis=-1)
            out = jnp.einsum('bhts,bshd->bthd', attn, v)
            gate = jax.nn.sigmoid(out @ Wg + bg)
            out = (out * gate).reshape(batch, seq, DIM)
            x = x + out @ Wo + bo
            h2 = rmsnorm(x, ln2_w)
            logits = h2 @ Wr + br
            top1 = jnp.argmax(logits, axis=-1).reshape(-1)
            xt = h2.reshape(-1, DIM)
            u = jnp.einsum('td,edf->tef', xt, W1) + b1
            u1, u2 = (u[..., :HID], u[..., HID:])
            act = u1 * jax.nn.sigmoid(u2)
            y_all = jnp.einsum('teh,ehd->ted', act, W2) + b2
            y = jnp.take_along_axis(y_all, top1[:, None, None], axis=1)[:, 0, :]
            return x + y.reshape(batch, seq, DIM)
        return _forward(x, ln1_w, ln2_w, Wq, bq, Wk, bk, Wv, bv, qn_w, kn_w, Wg, bg, Wo, bo, Wr, br, W1, b1, W2, b2)

    def _L3_xattn_ref(x, context, Wq, Wk, Wv, Wo, bo):
        import jax, jax.numpy as jnp
        import numpy as np
        HEADS = 8
        DIM_HEAD = 64
        QUERY_DIM = 128
        CONTEXT_DIM = 96
        INNER = HEADS * DIM_HEAD
        B, Sq, _ = x.shape
        h, d = (HEADS, DIM_HEAD)
        scale = d ** (-0.5)
        q = (x @ Wq).reshape(B, Sq, h, d).transpose(0, 2, 1, 3)
        k = (context @ Wk).reshape(B, -1, h, d).transpose(0, 2, 1, 3)
        v = (context @ Wv).reshape(B, -1, h, d).transpose(0, 2, 1, 3)
        scores = jnp.einsum('bhid,bhjd->bhij', q, k) * scale
        attn = jax.nn.softmax(scores, axis=-1)
        out = jnp.einsum('bhij,bhjd->bhid', attn, v)
        out = out.transpose(0, 2, 1, 3).reshape(B, Sq, h * d)
        return out @ Wo + bo

    def _L3_ffn_ref(x, wg, W, b):
        import jax, jax.numpy as jnp
        import numpy as np
        H = 128
        E = 8
        B, S = (4, 256)
        Bb, Ss, Hh = x.shape
        Ee = wg.shape[1]
        T = Bb * Ss
        C = T // Ee
        xt = x.reshape(T, Hh)
        logits = xt @ wg
        probs = jax.nn.softmax(logits, axis=-1)
        idx = jnp.argmax(probs, axis=-1)
        mask = jax.nn.one_hot(idx, Ee, dtype=xt.dtype)
        locations = jnp.cumsum(mask, axis=0) - mask
        mask = mask * (locations < C).astype(xt.dtype)
        gate = jnp.sum(probs * mask, axis=-1)
        loc_s = jnp.sum(locations * mask, axis=-1).astype(jnp.int32)
        loc_oh = jax.nn.one_hot(loc_s, C, dtype=xt.dtype)
        dispatch = mask[:, :, None] * loc_oh[:, None, :]
        combine = gate[:, None, None] * dispatch
        exp_in = jnp.einsum('tec,th->ech', dispatch, xt)
        exp_out = jnp.einsum('ech,efh->ecf', exp_in, W) + b[:, None, :]
        out = jnp.einsum('tec,ecf->tf', combine, exp_out)
        return out.reshape(Bb, Ss, Hh)
    x = x + _L0_xattn_ref(_layernorm(x, axis=-1), ctx_768, L0_xattn_wq, L0_xattn_bq, L0_xattn_wk, L0_xattn_bk, L0_xattn_wv, L0_xattn_bv, L0_xattn_wo, L0_xattn_bo)
    x = x + _L0_ffn_ref(_layernorm(x, axis=-1), L0_ffn_gate_w, L0_ffn_gate_b, L0_ffn_w1, L0_ffn_b1, L0_ffn_w2, L0_ffn_b2)
    x = x + _L1_xattn_ref(_layernorm(x, axis=-1), ctx_768, L1_xattn_Wq, L1_xattn_bq, L1_xattn_Wk, L1_xattn_bk, L1_xattn_Wv, L1_xattn_bv)
    x = x + _L1_ffn_ref(_layernorm(x, axis=-1), L1_ffn_router_W, L1_ffn_router_b, L1_ffn_sW1, L1_ffn_sb1, L1_ffn_sW2, L1_ffn_sb2, L1_ffn_eW1, L1_ffn_eb1, L1_ffn_eW2, L1_ffn_eb2)
    x = x + _L2_xattn_ref(_layernorm(x, axis=-1), ctx_768, mask_BxS_bk0, L2_xattn_Wq, L2_xattn_Wkv)
    x = x + _L2_ffn_ref(_layernorm(x, axis=-1), L2_ffn_ln1_w, L2_ffn_ln2_w, L2_ffn_Wq, L2_ffn_bq, L2_ffn_Wk, L2_ffn_bk, L2_ffn_Wv, L2_ffn_bv, L2_ffn_qn_w, L2_ffn_kn_w, L2_ffn_Wg, L2_ffn_bg, L2_ffn_Wo, L2_ffn_bo, L2_ffn_Wr, L2_ffn_br, L2_ffn_W1, L2_ffn_b1, L2_ffn_W2, L2_ffn_b2)
    x = x + _L3_xattn_ref(_layernorm(x, axis=-1), ctx_768, L3_xattn_Wq, L3_xattn_Wk, L3_xattn_Wv, L3_xattn_Wo, L3_xattn_bo)
    x = x + _L3_ffn_ref(_layernorm(x, axis=-1), L3_ffn_wg, L3_ffn_W, L3_ffn_b)
    return x

_drawn_inputs = setup_inputs


def setup_inputs(seed=0):
    import zlib

    import numpy as np

    out = dict(_drawn_inputs(seed))
    spreads = {'L0_ffn_gate_b': (0.0, 0.301),
     'L0_ffn_b1': (0.0, 0.449),
     'L0_ffn_b2': (0.0, 0.1),
     'L1_ffn_router_b': (0.0, 0.334),
     'L1_ffn_sb1': (0.0, 0.297),
     'L1_ffn_sb2': (0.0, 0.1),
     'L1_ffn_eb1': (0.0, 0.598),
     'L1_ffn_eb2': (0.0, 0.1),
     'L2_ffn_ln1_w': (1.0, 0.2),
     'L2_ffn_ln2_w': (1.0, 0.2),
     'L2_ffn_bq': (0.0, 0.286),
     'L2_ffn_bk': (0.0, 0.31),
     'L2_ffn_bv': (0.0, 0.1),
     'L2_ffn_qn_w': (1.0, 0.2),
     'L2_ffn_kn_w': (1.0, 0.2),
     'L2_ffn_bg': (0.0, 0.1),
     'L2_ffn_bo': (0.0, 0.1),
     'L2_ffn_br': (0.0, 0.1),
     'L2_ffn_b1': (0.0, 0.326),
     'L2_ffn_b2': (0.0, 0.1)}
    factors = {'L0_xattn_bk': 8.0,
     'L0_ffn_w1': 3.121,
     'L1_xattn_bq': 3.974,
     'L1_xattn_bk': 8.0,
     'L1_ffn_eW1': 3.594,
     'L1_ffn_eW2': 3.251,
     'L3_xattn_bo': 8.0,
     'L3_ffn_wg': 3.895,
     'L3_ffn_W': 3.746,
     'L3_ffn_b': 8.0}
    for name, (base, spread) in spreads.items():
        noise = np.random.default_rng([zlib.crc32(name.encode()), seed]).standard_normal(out[name].shape)
        drawn = base * np.exp(spread * noise) if base else spread * noise
        out[name] = jnp.asarray(drawn.astype(out[name].dtype))
    for name, factor in factors.items():
        out[name] = (out[name] * factor).astype(out[name].dtype)
    return out
```

```python
from contextlib import ExitStack

import numpy as np

import concourse.bass as bass
from concourse import mybir

F32 = mybir.dt.float32
F32R = mybir.dt.float32r
U8 = mybir.dt.uint8
ALU = mybir.AluOpType
ACT = mybir.ActivationFunctionType
AXX = mybir.AxisListType.X

B, T, D, C = 32, 128, 128, 96
RING = 4
GROUPS = B // RING
EPS = 1e-5
RMS_EPS = 1e-6
BIG = 1e30
H16, DH = 16, 8


class Item:

    def __init__(self, group, slot):
        self.g, self.s = group, slot
        self.n = group * RING + slot


def counted_from(before):
    def at(sem, value):
        return value + before.get(sem.name, 0)
    return at


def due(value):
    return not isinstance(value, int) or value > 0


def following(it, n):
    return min(it.n + n, B) if isinstance(it.n, int) else it.n + n


def ticks(eng, last, peel=2):
    def tick(group, j, edge):
        def item(lag):
            it = Item(group + (j - lag) // RING, (j - lag) % RING)
            return it if not edge or 0 <= it.n < B else None
        return item

    for t in range(peel * RING):
        yield tick(t // RING, t % RING, True)
    with eng.Fori(peel, GROUPS, 1) as group:
        for j in range(RING):
            yield tick(group, j, False)
    for t in range(B, B + last):
        yield tick(t // RING, t % RING, True)


def build(nc, a, out, upto="f3"):
    ctx = ExitStack()
    with ctx:
        def sb(name, shape, dt=F32):
            return ctx.enter_context(nc.sbuf_tensor(name, shape, dt))

        sems = {}

        def sem(name):
            if name not in sems:
                sems[name] = ctx.enter_context(nc.semaphore(name))
            return sems[name]

        reached = {}

        def totals(**counts):
            for name, count in counts.items():
                reached[name] = reached.get(name, 0) + count

        X = sb("X", [T, GROUPS, RING, D])
        Y = sb("Y", [T, GROUPS, RING, D])
        ident = sb("ident", [128, 128])
        ident_r = sb("ident_r", [128, 128], F32R)
        w = {}
        loads = []

        def weight(phase, name, shape, place=None):
            w[name] = sb("w_" + name, shape)[:] if place is None else place
            loads.append((phase, w[name], a[name]))

        jmask = sb("jmask", [D, 4])
        loads.append(("a0", ident[:], a["ident"]))
        loads.append(("a0", jmask[:], a["jmask"]))
        weight("a0", "a0_wq", [D, D])
        weight("a0", "a0_wkv", [C, 2 * D])
        weight("a0", "a0_bqk", [T, 2 * D])
        weight("a0", "a0_bv", [T, D])
        weight("a0", "a0_wo", [D, D])
        weight("a0", "a0_bo", [T, D])

        weight("a1", "a1_wq", [D, D])
        weight("a1", "a1_wk", [C, D])
        weight("a1", "a1_wv", [C, D])
        weight("a1", "a1_bq", [D, 1])
        weight("a1", "a1_bk", [D, 1])
        weight("a1", "a1_bv", [T, D])
        weight("a3", "a3_wq", [D, 512])
        weight("a3", "a3_wk", [C, 512])
        weight("a3", "a3_wv", [C, 512])
        weight("a3", "a3_wo", [128, 4, D])
        weight("a3", "a3_bo", [T, D])
        weight("a2", "a2_wq", [D, D])
        weight("a2", "a2_wkv", [C, 2 * D])
        weight("b2", "b2_wqkv", [D, 192])
        weight("b2", "b2_bqkv", [T, 192])
        weight("b2", "b2_rope", [T, 3, DH // 2])
        weight("b2", "b2_norm", [T, 2, DH])
        weight("b2", "b2_ln", [D, 1])
        weight("b2", "b2_wgate", [D, D])
        weight("a0", "b2_bgate", [D, 1])
        weight("b2", "b2_wo", [D, D])
        weight("b2", "b2_bo", [T, D])
        keep_words = sb("keep_words", [T, B // 4], mybir.dt.int32)
        loads.append(("a0", keep_words[:], a["keep"]))
        causal_in = sb("causal_in", [T, 2, T])
        loads.append(("a0", causal_in[:], a["causal"]))
        weight("f0", "f0_wg", [D, 8])
        weight("f0", "f0_bg", [T, 8])
        weight("f0", "f0_w1", [D, 8, 512])
        weight("f0", "f0_b1", [128, 8, 4])
        weight("f0", "f0_w2", [128, 8, 512])
        weight("f0", "f0_b2", [8, D])
        weight("f1", "f1_wg", [D, 15])
        weight("f1", "f1_bg", [T, 15])
        weight("f1", "f1_w1", [D, 16, 128])
        weight("f1", "f1_b1", [128, 16, 1])
        weight("f1", "f1_w2", [128, 16, 128])
        weight("f1", "f1_b2", [16, D])
        weight("f2", "f2_ln", [D, 1])
        weight("f2", "f2_wg", [D, 8])
        weight("f2", "f2_bg", [T, 8])
        weight("f2", "f2_w1", [D, 8, 512], w["f0_w1"])
        weight("f2", "f2_b1", [128, 8, 4])
        weight("f2", "f2_w2", [128, 8, 256], w["f0_w2"][:, 0:4, :].rearrange("p a (b n) -> p (a b) n", b=2))
        weight("f2", "f2_b2", [8, D])
        weight("f3", "f3_wg", [D, 8])
        weight("f3", "f3_w2", [D, 8, 128], w["f1_w1"][:, 0:8, :])
        weight("f3", "f3_b2", [8, D])
        rank = sb("rank", [T, 16])
        earlier = sb("earlier", [T, T])
        loads.append(("a0", rank[:], a["rank"]))
        loads.append(("a0", earlier[:], a["earlier"]))
        ones = sb("ones", [T, T])
        ones_r = sb("ones_r", [T, T], F32R)
        hT4 = sb("hT4", [D, RING * T])
        sg = sb("sg", [128, 2, RING * T])
        lg, sel, tmp, pr, wt = (sb(n, [T, RING, 16]) for n in ("lg", "sel", "tmp", "pr", "wt"))
        rmax, rsum = sb("rmax", [T, RING]), sb("rsum", [T, RING])
        run = sb("run", [T, RING + 1, 8])
        wT = sb("wT", [16, RING * T])
        ve2 = sb("ve2", [T, RING, 1])
        scratch = sb("scratch", [T, 1])

        ctxT = sb("ctxT", [C, RING, T])
        bn = sb("bn", [T, RING, 6])
        mv = sb("mv", [T, RING, 2])
        ve = sb("ve", [T, RING, 1])
        rstd = sb("rstd", [T, RING, 1])
        neg_half = sb("neg_half", [T, 32])
        eps_t = sb("eps_t", [T, 2])
        zeros = sb("zeros", [T, H16])
        h = sb("h", [T, RING, D])
        hT = sb("hT", [D, RING, T])
        qk = sb("qk", [T, 2, 2, H16, DH])
        parts = sb("parts", [T, RING, 2, H16, 4, DH], F32R)
        vx = sb("vx", [T, RING, 4 * 136])
        ones_x = sb("ones_x", [T, 4, 4, DH])
        qT = sb("qT", [D, RING, T], F32R)
        kx = sb("kx", [D, 2, 4, T], F32R)
        kS = sb("kS", [128, 2, 4, T], F32R)
        qS = sb("qS", [128, 2, 4, 4, T], F32R)
        mx = sb("mx", [T, RING, H16])
        P = sb("P", [T, 2, H16, T])
        rec = sb("rec", [D, T])
        gt = P[:].rearrange("p b h t -> p (b h t)").rearrange("p (n t) -> p n t", t=RING * T)
        oT = sb("oT", [D, RING, T])
        ogT = sb("ogT", [D, RING, T])
        eg = sb("eg", [D, 3, T])
        neg_bgate = sb("neg_bgate", [D, 1])
        causal_q, causal_k = sb("causal_q", [T, 4 * T], F32R), sb("causal_k", [T, 4 * T], F32R)
        qkv = sb("qkv", [T, 192])
        ra, rb = sb("ra", [T, H16 + 4, DH]), sb("rb", [T, H16 + 4, DH])
        rsq, rrs = sb("rsq", [T, H16 + 4]), sb("rrs", [T, H16 + 4])
        bn2, mv2, ms2 = sb("bn2", [T, RING, 6]), sb("mv2", [T, RING, 2]), sb("ms2", [T, RING, 1])
        ve3, rstd2 = sb("ve3", [T, RING, 1]), sb("rstd2", [T, RING, 1])
        keep = sb("keep", [T, GROUPS, RING])

        PS = ctx.enter_context(nc.psum_tensor("PS", [128, 8, 512], F32))
        S_ps, ST_ps = PS[:, 0:2, :], PS[:, 2:4, :]
        TP = [PS[:, 4, :], PS[:, 5, :]]
        FR, OB = PS[:, 6, :], PS[:, 7, :]

        x_dram = a["x"].rearrange("(g s) t d -> t g s d", s=RING)
        out_dram = out.rearrange("(g s) t d -> t g s d", s=RING)
        ctx_dram = a["ctxT"].rearrange("(g s) c t -> c g s t", s=RING)

        consts_ready = sem("consts_ready")
        N_CONSTS = 15
        ones_ready = sem("ones_ready")

        def stat_stages(at):
            s_st, s_rs, s_h = sem("stats"), sem("rstd"), sem("h")
            s_bn, s_ve, s_hps = sem("bn"), sem("ve"), sem("hps")

            def stats(v, it):
                if due(it.n - RING + 1):
                    v.wait_ge(s_h, at(s_h, it.n - RING + 1))
                v.bn_stats(bn[:, it.s, :], X[:, it.g, it.s, :]).then_inc(s_bn, 1)

            def aggregate(v, it):
                if isinstance(it.n, int):
                    v.wait_ge(s_bn, at(s_bn, it.n + 1))
                v.bn_aggr(mv[:, it.s, :], bn[:, it.s, :]).then_inc(s_st, 1)

            def rsqrt(q, it):
                q.wait_ge(s_st, at(s_st, it.n + 1))
                q.tensor_tensor(ve[:, it.s, :], mv[:, it.s, 1:2], eps_t[:, 0:1], ALU.add).then_inc(s_ve, 1)
                q.wait_ge(s_ve, at(s_ve, it.n + 1))
                q.tensor_tensor(rstd[:, it.s, :], ve[:, it.s, :], neg_half[:, 0:1], ALU.pow).then_inc(s_rs, 1)

            def norm(v, it, dst):
                if due(it.n - RING + 1):
                    v.wait_ge(s_hps, at(s_hps, it.n - RING + 1))
                v.wait_ge(s_bn, at(s_bn, following(it, 2)))
                v.wait_ge(s_rs, at(s_rs, it.n + 1))
                v.tensor_scalar(dst, X[:, it.g, it.s, :], mv[:, it.s, 0:1], rstd[:, it.s, :],
                                ALU.subtract, ALU.mult).then_inc(s_h, 1)
            return stats, aggregate, rsqrt, norm, s_h

        def attention16(p, before, kind):
            at = counted_from(dict(reached))
            has_bias, masked, causal = kind == "cross", kind == "masked", kind == "self"
            projected = not masked
            F = 2 if causal else 1
            peel = 3 if causal else 2
            def own(*names):
                return [sem(n) if causal else None for n in names]
            s_ctx = None if causal else [sem(f"ctx{i}") for i in range(RING)]
            s_hps, s_hT = sem("hps"), sem("hT")
            s_qkv, s_qkf, s_v = sem("qkv"), sem("qkf"), sem("v")
            s_hi, s_lo = sem("hi"), sem("lo")
            s_turn, s_kx, s_qT = sem("turn"), sem("kx"), sem("qT")
            s_tk, s_kS, s_tq, s_qSv, s_qSa = (sem(n) for n in ("tk", "kS", "tq", "qSv", "qSa"))
            s_s, s_mx, s_nm = sem("s"), sem("mx"), sem("nm")
            s_st, s_exp = sem("st"), sem("exp")
            s_av, s_rec, s_o = sem("av"), sem("rec"), sem("o")
            s_out, s_xb, s_done = sem("out"), sem("xb"), sem("done")
            stats, aggregate, rsqrt, norm, s_h = stat_stages(at)
            s_y, s_bn2, s_st2, s_ms, s_rs2 = own("h", "bn2", "st2", "ms", "rs2")
            s_rope, s_sum, s_rs3, s_gate, s_eg, s_gt = own("rope", "sum", "rs3", "gate", "eg", "gt")
            s_yb, s_yd, s_gt2, s_ve3 = own("yb", "yd", "gt2", "ve3")
            s_bn, s_rs = sem("bn"), sem("rstd")
            if causal:
                s_h = sem("h2")

            def sync(e):
                if causal:
                    return
                before(e)
                for s in range(RING):
                    e.dma_start(ctxT[:, s, :], ctx_dram[:, 0, s, :]).then_inc(s_ctx[s], 16)
                with e.Fori(1, GROUPS, 1) as g:
                    for s in range(RING):
                        e.wait_ge(s_qkv, at(s_qkv, (g - 1) * RING + s + 1))
                        e.dma_start(ctxT[:, s, :], ctx_dram[:, g, s, :]).then_inc(s_ctx[s], 16)

            def pe_hT(e, it):
                e.wait_ge(s_h, at(s_h, it.n + 1))
                if due(it.n):
                    e.wait_ge(s_kx, at(s_kx, it.n))
                if due(it.n):
                    e.wait_ge(s_qT, at(s_qT, it.n))
                e.transpose(FR[:, 0:T], h[:, it.s, :], ident[:, :]).then_inc(s_hps, 1)

            def pe_qkv(e, it):
                e.wait_ge(s_hT, at(s_hT, it.n + 1))
                if causal:
                    m = e.matmul(FR[:, 0:192], hT[:, it.s, :], w[p + "wqkv"][:, :], start=True, stop=True)
                else:
                    e.wait_ge(s_ctx[it.s], at(s_ctx[it.s], 16 * (it.g + 1)))
                    e.matmul(FR[:, 0:D], hT[:, it.s, :], w[p + "wq"][:, :], start=True, stop=True)
                    m = e.matmul(FR[:, D:3 * D], ctxT[:, it.s, :], w[p + "wkv"][:, :], start=True, stop=True)
                m.then_inc(s_qkv, 1)

            def pe_turn(e, it):
                e.wait_ge(s_v, at(s_v, it.n + 1))
                e.wait_ge(s_qkf, at(s_qkf, (2 if causal else 1) * (it.n + 1)))
                for which in range(2):
                    m = e.transpose(FR[:, which * T:(which + 1) * T],
                                    qk[:, it.s % 2, which, :, :].rearrange("p h d -> p (h d)"), ident[:, :])
                m.then_inc(s_turn, 1)

            def turn_stack(e, it, which, done):
                for g in range(4):
                    m = e.matmul(TP[which][:, g * T:(g + 1) * T],
                                 parts[:, it.s, which, 4 * g:4 * g + 4, :, :].rearrange("p h c d -> p (h c d)"),
                                 ident_r[:, :], start=True, stop=True)
                m.then_inc(done, 1)

            def pe_stack_k(e, it):
                e.wait_ge(s_lo, at(s_lo, 2 * it.n + 2))
                if due(it.n):
                    e.wait_ge(s_kS, at(s_kS, it.n))
                turn_stack(e, it, 1, s_tk)

            def pe_stack_q(e, it):
                e.wait_ge(s_nm, at(s_nm, 2 * it.n + 2))
                if due(it.n):
                    e.wait_ge(s_qSv, at(s_qSv, it.n))
                if due(it.n):
                    e.wait_ge(s_qSa, at(s_qSa, it.n))
                turn_stack(e, it, 0, s_tq)

            def pe_scores(e, it, half):
                if half == 0:
                    e.wait_ge(s_qT, at(s_qT, it.n + 1))
                    e.wait_ge(s_kx, at(s_kx, it.n + 1))
                if due(2 * it.n + half):
                    e.wait_ge(s_mx, at(s_mx, 2 * it.n + half))
                if causal:
                    for i in range(2):
                        e.matmul(S_ps[:, i, :], ident_r[:, :], causal_q[:, :], start=True, stop=False)
                for i in range(2):
                    r = 32 * (2 * half + i)
                    m = e.matmul(S_ps[:, i, :], qT[r:r + 32, it.s, :],
                                 kx[r:r + 32, it.s % 2, :, :].rearrange("p j t -> p (j t)"),
                                 start=not causal, stop=True)
                m.then_inc(s_s, 1)

            def pe_scoresT(e, it, half):
                if half == 0:
                    e.wait_ge(s_kS, at(s_kS, it.n + 1))
                    e.wait_ge(s_qSv, at(s_qSv, it.n + 1))
                    e.wait_ge(s_qSa, at(s_qSa, it.n + 1))
                if due(2 * it.n + half):
                    e.wait_ge(s_exp, at(s_exp, 2 * it.n + half))
                for i in range(2):
                    g = 2 * half + i
                    if causal:
                        e.matmul(ST_ps[:, i, :], ident_r[:, :], causal_k[:, :], start=True, stop=False)
                    m = e.matmul(ST_ps[:, i, :], kS[:, it.s % 2, g, :],
                                 qS[:, it.s % 2, g, :, :].rearrange("p j t -> p (j t)"),
                                 start=not causal, stop=True)
                m.then_inc(s_st, 1)

            def pe_values(e, it):
                e.wait_ge(s_exp, at(s_exp, 2 * it.n + 2))
                e.wait_ge(s_v, at(s_v, it.n + 1))
                if due(it.n):
                    e.wait_ge(s_done, at(s_done, it.n))
                for what in range(2):
                    for j in range(4):
                        for g in range(4):
                            lhs = vx[:, it.s, 128 * j + 32 * g:128 * j + 32 * g + 32] if what == 0 else \
                                ones_x[:, j, :, :].rearrange("p a d -> p (a d)")
                            m = e.matmul(OB[32 * g:32 * g + 32, what * T:(what + 1) * T], lhs,
                                         P[:, it.s % 2, 4 * g + j, :], start=(j == 0), stop=(j == 3))
                m.then_inc(s_av, 1)

            def pe_gate(e, it):
                e.wait_ge(s_o, at(s_o, it.n + 1))
                e.matmul(OB[:, 0:T], w[p + "wgate"][:, :], oT[:, it.s, :], start=True, stop=True).then_inc(s_gate, 1)

            def pe_out(e, it):
                e.wait_ge(s_gt if causal else s_o, at(s_gt if causal else s_o, it.n + 1))
                if causal:
                    m = e.matmul(OB[:, 0:D], ogT[:, it.s, :], w[p + "wo"][:, :], start=True, stop=True)
                elif projected:
                    m = e.matmul(OB[:, 0:D], oT[:, it.s, :], w[p + "wo"][:, :], start=True, stop=True)
                else:
                    m = e.transpose(OB[:, 0:D], oT[:, it.s, :], ident[:, :])
                m.then_inc(s_out, 1)

            def tensor(e):
                before(e)
                e.wait_ge(sem(p + "weights"), 16 * n_loads[p[:2]])
                e.wait_ge(consts_ready, N_CONSTS)
                for item in ticks(e, F + 4, peel):
                    if it := item(F + 4):
                        pe_out(e, it)
                    if it := item(F + 1):
                        pe_turn(e, it)
                    if it := item(F + 2):
                        pe_stack_q(e, it)
                    if it := item(F + 1):
                        pe_stack_k(e, it)
                    if it := item(F):
                        pe_hT(e, it)
                    if it := item(F + 1):
                        pe_scores(e, it, 0)
                    if it := item(F + 3):
                        pe_values(e, it)
                    if it := item(F + 2):
                        pe_scoresT(e, it, 0)
                    if it := item(F):
                        pe_qkv(e, it)
                    if it := item(F + 1):
                        pe_scores(e, it, 1)
                    if it := item(F + 2):
                        pe_scoresT(e, it, 1)
                    if causal and (it := item(F + 3)):
                        pe_gate(e, it)

            def v_qkv(e, it):
                if due(2 * (it.n - 1)):
                    e.wait_ge(s_lo, at(s_lo, 2 * (it.n - 1)))
                if due(it.n - 1):
                    e.wait_ge(s_turn, at(s_turn, it.n - 1))
                e.wait_ge(s_qkv, at(s_qkv, it.n + 1))
                src = FR[:, 0:2 * D]
                dst = qk[:, it.s % 2].rearrange("p a h d -> p (a h d)")
                if has_bias:
                    e.tensor_tensor(dst, src, w[p + "bqk"][:, :], ALU.add).then_inc(s_qkf, 1)
                if masked:
                    e.tensor_scalar(qk[:, it.s % 2, 0].rearrange("p h d -> p (h d)"), FR[:, 0:D],
                                    keep[:, it.g, it.s:it.s + 1], None, ALU.mult)
                    e.tensor_copy(qk[:, it.s % 2, 1].rearrange("p h d -> p (h d)"), FR[:, D:2 * D])\
                     .then_inc(s_qkf, 1)
                if due(it.n - RING + 1):
                    e.wait_ge(s_av, at(s_av, it.n - RING + 1))
                vsrc = FR[:, 2 * D:3 * D].rearrange("p (g j d) -> p j g d", g=4, j=4)
                vdst = vx[:, it.s, :].rearrange("p (j n) -> p j n", j=4)[:, :, 0:128]\
                    .rearrange("p j (g n) -> p j g n", g=4)[:, :, :, 0:DH]
                if has_bias:
                    e.tensor_tensor(vdst, vsrc, w[p + "bv"][:, :].rearrange("p (g j d) -> p j g d", g=4, j=4),
                                    ALU.add).then_inc(s_v, 1)
                if masked:
                    e.tensor_copy(vdst, vsrc).then_inc(s_v, 1)

            def v_self(e, it):
                n_heads = H16 + 4
                n = [0]

                def step(m):
                    n[0] += 1
                    m.then_inc(s_rope, 1)
                    e.wait_ge(s_rope, at(s_rope, 8 * it.n + n[0]))
                if due(it.n - RING + 1):
                    e.wait_ge(s_av, at(s_av, it.n - RING + 1))
                e.wait_ge(s_qkv, at(s_qkv, it.n + 1))
                step(e.tensor_tensor(qkv[:, :], FR[:, 0:192], w[p + "bqkv"][:, :], ALU.add))
                x = qkv[:, 0:160].rearrange("p (h d) -> p h d", d=DH)
                shape = [T, n_heads, DH // 2]

                def table(i):
                    return w[p + "rope"][:, i, :].unsqueeze(1).broadcast_to([T, n_heads, table_width[i]])
                table_width = {0: DH // 2, 1: DH // 2, 2: DH // 2}
                lo_, hi_ = x[:, :, 0:4], x[:, :, 4:8]
                e.tensor_tensor(ra[:, :, 0:4], lo_, table(0), ALU.mult)
                e.tensor_tensor(ra[:, :, 4:8], hi_, table(0), ALU.mult)
                e.tensor_tensor(rb[:, :, 0:4], hi_, table(2), ALU.mult)
                vdst = vx[:, it.s, :].rearrange("p (j n) -> p j n", j=4)[:, :, 0:128]\
                    .rearrange("p j (g n) -> p j g n", g=4)[:, :, :, 0:DH]
                e.tensor_copy(vdst, qkv[:, 160:192].rearrange("p (g d) -> p g d", g=4).unsqueeze(1)
                              .broadcast_to([T, 4, 4, DH])).then_inc(s_v, 1)
                step(e.tensor_tensor(rb[:, :, 4:8], lo_, table(1), ALU.mult))
                step(e.tensor_tensor(ra[:, :, :], ra[:, :, :], rb[:, :, :], ALU.add))
                step(e.tensor_tensor(rb[:, :, :], ra[:, :, :], ra[:, :, :], ALU.mult))
                step(e.tensor_reduce(rsq[:, :], rb[:, :, :], AXX, ALU.add))
                e.tensor_scalar(rsq[:, :], rsq[:, :], 1.0 / DH, RMS_EPS, ALU.mult, ALU.add).then_inc(s_sum, 1)
                e.wait_ge(s_rs3, at(s_rs3, it.n + 1))
                step(e.tensor_tensor(ra[:, :, :], ra[:, :, :],
                                     rrs[:, :].unsqueeze(2).broadcast_to([T, n_heads, DH]), ALU.mult))
                if due(2 * (it.n - 1)):
                    e.wait_ge(s_lo, at(s_lo, 2 * (it.n - 1)))
                if due(it.n - 1):
                    e.wait_ge(s_turn, at(s_turn, it.n - 1))
                e.tensor_tensor(qk[:, it.s % 2, 0], ra[:, 0:H16, :],
                                w[p + "norm"][:, 0, :].unsqueeze(1).broadcast_to([T, H16, DH]), ALU.mult)\
                 .then_inc(s_qkf, 1)
                e.tensor_tensor(qk[:, it.s % 2, 1].rearrange("p (g j) d -> p g j d", g=4),
                                ra[:, H16:n_heads, :].unsqueeze(2).broadcast_to([T, 4, 4, DH]),
                                w[p + "norm"][:, 1, :].unsqueeze(1).unsqueeze(1).broadcast_to([T, 4, 4, DH]),
                                ALU.mult).then_inc(s_qkf, 1)
                e.wait_ge(s_qkf, at(s_qkf, 2 * it.n + 2))
                step(e.tensor_copy(scratch[:, 0:1], neg_half[:, 0:1]))
                step(e.tensor_copy(scratch[:, 0:1], neg_half[:, 0:1]))

            def v_y(e, it):
                e.wait_ge(s_bn, at(s_bn, following(it, 2)))
                e.wait_ge(s_rs, at(s_rs, it.n + 1))
                e.tensor_scalar(Y[:, it.g, it.s, :], X[:, it.g, it.s, :], mv[:, it.s, 0:1], rstd[:, it.s, :],
                                ALU.subtract, ALU.mult).then_inc(s_y, 1)

            def v_y_stats(e, it):
                e.wait_ge(s_y, at(s_y, it.n + 1))
                e.tensor_copy(scratch[:, 0:1], neg_half[:, 0:1])
                e.bn_stats(bn2[:, it.s, :], Y[:, it.g, it.s, :]).then_inc(s_bn2, 1)
                e.wait_ge(s_bn2, at(s_bn2, it.n + 1))
                e.tensor_copy(scratch[:, 0:1], neg_half[:, 0:1])
                e.bn_aggr(mv2[:, it.s, :], bn2[:, it.s, :]).then_inc(s_st2, 1)
                e.wait_ge(s_st2, at(s_st2, it.n + 1))
                e.scalar_tensor_tensor(out=ms2[:, it.s, :], in0=mv2[:, it.s, 0:1], scalar=mv2[:, it.s, 0:1],
                                       in1=mv2[:, it.s, 1:2], op0=ALU.mult, op1=ALU.add).then_inc(s_ms, 1)

            def v_h2(e, it):
                if due(it.n - RING + 1):
                    e.wait_ge(s_hps, at(s_hps, it.n - RING + 1))
                e.wait_ge(s_rs2, at(s_rs2, it.n + 1))
                e.tensor_scalar(h[:, it.s, :], Y[:, it.g, it.s, :], rstd2[:, it.s, :], None, ALU.mult)\
                 .then_inc(s_h, 1)

            def v_gate(e, it):
                e.wait_ge(s_eg, at(s_eg, it.n + 1))
                e.tensor_scalar(eg[:, 1, :], eg[:, 0, :], 1.0, None, ALU.add).then_inc(s_gt2, 1)
                e.wait_ge(s_gt2, at(s_gt2, 2 * it.n + 1))
                e.reciprocal(eg[:, 2, :], eg[:, 1, :]).then_inc(s_gt2, 1)
                e.wait_ge(s_gt2, at(s_gt2, 2 * it.n + 2))
                e.tensor_tensor(ogT[:, it.s, :], oT[:, it.s, :], eg[:, 2, :], ALU.mult).then_inc(s_gt, 1)

            def v_residual_self(e, it):
                e.wait_ge(s_yb, at(s_yb, it.n + 1))
                e.wait_ge(s_out, at(s_out, it.n + 1))
                e.tensor_tensor(Y[:, it.g, it.s, :], Y[:, it.g, it.s, :], OB[:, 0:D], ALU.add).then_inc(s_yd, 1)

            def v_high(e, it):
                if due(it.n - RING + 1):
                    e.wait_ge(s_tq, at(s_tq, it.n - RING + 1))
                e.wait_ge(s_qkf, at(s_qkf, (2 if causal else 1) * (it.n + 1)))
                src = qk[:, it.s % 2].rearrange("p a h d -> p (a h) d").unsqueeze(2).broadcast_to([T, 2 * H16, 3, DH])
                dst = parts[:, it.s, :, :, 0:3, :].rearrange("p a h c d -> p (a h) c d")
                e.tensor_copy(dst, src).then_inc(s_hi, 1)

            def v_kx(e, it):
                e.wait_ge(s_turn, at(s_turn, it.n + 1))
                e.tensor_tensor(kx[:, it.s % 2, :, :], FR[:, T:2 * T].unsqueeze(1).broadcast_to([D, 4, T]),
                                jmask[:, :].unsqueeze(2).broadcast_to([D, 4, T]), ALU.mult).then_inc(s_kx, 1)

            def v_qS(e, it):
                if due(2 * (it.n - 1)):
                    e.wait_ge(s_st, at(s_st, 2 * (it.n - 1)))
                e.wait_ge(s_tq, at(s_tq, it.n + 1))
                e.tensor_copy(qS[0:32, it.s % 2, :, 0, :], TP[0][0:32, :].rearrange("p (g t) -> p g t", g=4))\
                 .then_inc(s_qSv, 1)

            def v_max(e, it, half):
                e.wait_ge(s_s, at(s_s, 2 * it.n + half + 1))
                e.tensor_reduce(mx[:, it.s, 8 * half:8 * half + 8],
                                S_ps[:, :, :].rearrange("p i (j t) -> p (i j) t", t=T), AXX, ALU.max)\
                 .then_inc(s_mx, 1)

            def v_negmax(e, it, half):
                e.wait_ge(s_mx, at(s_mx, 2 * it.n + half + 1))
                dst = parts[:, it.s, 0, 8 * half:8 * half + 8, 3, 0:1]
                e.tensor_scalar(dst, mx[:, it.s, 8 * half:8 * half + 8].unsqueeze(2), -1.0, None, ALU.mult)\
                 .then_inc(s_nm, 1)

            def v_heads(e, it):
                if due(it.n):
                    e.wait_ge(s_o, at(s_o, it.n))
                e.wait_ge(s_av, at(s_av, it.n + 1))
                e.reciprocal(rec[:, :], OB[:, T:2 * T]).then_inc(s_rec, 1)
                if due(it.n - RING + 1):
                    e.wait_ge(s_out, at(s_out, it.n - RING + 1))
                e.wait_ge(s_rec, at(s_rec, it.n + 1))
                e.tensor_tensor(oT[:, it.s, :], OB[:, 0:T], rec[:, :], ALU.mult).then_inc(s_o, 1)

            def v_residual(e, it):
                if projected:
                    e.wait_ge(s_xb, at(s_xb, it.n + 1))
                e.wait_ge(s_out, at(s_out, it.n + 1))
                e.tensor_tensor(X[:, it.g, it.s, :], X[:, it.g, it.s, :], OB[:, 0:D], ALU.add).then_inc(s_done, 1)

            def vector(e):
                before(e)
                e.wait_ge(sem(p + "weights"), 16 * n_loads[p[:2]])
                for item in ticks(e, F + 4, peel):
                    if it := item(F + 4):
                        (v_residual_self if causal else v_residual)(e, it)
                    if it := item(F + 1):
                        v_kx(e, it)
                    if it := item(F + 2):
                        v_qS(e, it)
                    if causal and (it := item(F)):
                        v_h2(e, it)
                    if it := item(0):
                        stats(e, it)
                    if it := item(1):
                        v_y(e, it) if causal else norm(e, it, h[:, it.s, :])
                    if it := item(0):
                        aggregate(e, it)
                    if it := item(F + 1):
                        v_max(e, it, 0)
                        v_negmax(e, it, 0)
                    if it := item(F + 3):
                        v_heads(e, it)
                    if causal and (it := item(1)):
                        v_y_stats(e, it)
                    if it := item(F):
                        (v_self if causal else v_qkv)(e, it)
                        v_high(e, it)
                    if it := item(F + 1):
                        v_max(e, it, 1)
                        v_negmax(e, it, 1)
                    if causal and (it := item(F + 3)):
                        v_gate(e, it)

            def g_low(e, it):
                e.wait_ge(s_hi, at(s_hi, it.n + 1))
                for which, place in ((0, 2), (1, 1)):
                    e.tensor_tensor(parts[:, it.s, which, :, place, :], qk[:, it.s % 2, which, :, :],
                                    parts[:, it.s, which, :, 0, :].bitcast(F32), ALU.subtract).then_inc(s_lo, 1)

            def g_rsqrt2(e, it):
                e.wait_ge(s_ms, at(s_ms, it.n + 1))
                e.tensor_tensor(ve3[:, it.s, :], ms2[:, it.s, :], eps_t[:, 1:2], ALU.add).then_inc(s_ve3, 1)
                e.wait_ge(s_ve3, at(s_ve3, it.n + 1))
                e.tensor_tensor(rstd2[:, it.s, :], ve3[:, it.s, :], neg_half[:, 0:1], ALU.pow).then_inc(s_rs2, 1)

            def g_rsqrt3(e, it):
                e.wait_ge(s_sum, at(s_sum, it.n + 1))
                e.tensor_tensor(rrs[:, :], rsq[:, :], neg_half[:, 0:H16 + 4], ALU.pow).then_inc(s_rs3, 1)

            def g_bias_y(e, it):
                e.wait_ge(s_h, at(s_h, it.n + 1))
                e.tensor_tensor(Y[:, it.g, it.s, :], Y[:, it.g, it.s, :], w[p + "bo"][:, :], ALU.add)\
                 .then_inc(s_yb, 1)

            def g_add_y(e, it):
                e.wait_ge(s_yd, at(s_yd, it.n + 1))
                e.tensor_tensor(X[:, it.g, it.s, :], X[:, it.g, it.s, :], Y[:, it.g, it.s, :], ALU.add)\
                 .then_inc(s_done, 1)

            def g_bias(e, it):
                e.wait_ge(s_h, at(s_h, it.n + 1))
                e.tensor_tensor(X[:, it.g, it.s, :], X[:, it.g, it.s, :], w[p + "bo"][:, :], ALU.add)\
                 .then_inc(s_xb, 1)

            def pool(e):
                before(e)
                e.wait_ge(sem(p + "weights"), 16 * n_loads[p[:2]])
                if causal:
                    for item in ticks(e, 6, peel):
                        if it := item(0):
                            rsqrt(e, it)
                        if it := item(6):
                            g_add_y(e, it)
                        if it := item(1):
                            g_rsqrt2(e, it)
                        if it := item(F):
                            g_rsqrt3(e, it)
                            g_bias_y(e, it)
                            g_low(e, it)
                    return
                for item in ticks(e, 1):
                    if it := item(0):
                        rsqrt(e, it)
                    if projected and (it := item(1)):
                        g_bias(e, it)
                    if it := item(1):
                        g_low(e, it)

            def a_qT(e, it):
                e.wait_ge(s_kx, at(s_kx, it.n + 1))
                e.copy(qT[:, it.s, :], FR[:, 0:T]).then_inc(s_qT, 1)

            def a_kS(e, it):
                e.wait_ge(s_tk, at(s_tk, it.n + 1))
                e.copy(kS[:, it.s % 2].rearrange("p g t -> p (g t)"), TP[1]).then_inc(s_kS, 1)

            def a_qS(e, it):
                e.wait_ge(s_qSv, at(s_qSv, it.n + 1))
                for j in range(1, 4):
                    r = slice(32 * j, 32 * j + 32)
                    m = e.copy(qS[r, it.s % 2, :, j, :], TP[0][r, :].rearrange("p (g t) -> p g t", g=4))
                m.then_inc(s_qSa, 1)

            def a_hT(e, it):
                if due(it.n - RING + 1):
                    e.wait_ge(s_qkv, at(s_qkv, it.n - RING + 1))
                e.wait_ge(s_hps, at(s_hps, it.n + 1))
                if causal:
                    e.activation(hT[:, it.s, :], FR[:, 0:T], ACT.Identity, scale=w[p + "ln"][:, 0:1]).then_inc(s_hT, 1)
                else:
                    e.copy(hT[:, it.s, :], FR[:, 0:T]).then_inc(s_hT, 1)

            def a_gate(e, it):
                if due(it.n):
                    e.wait_ge(s_gt, at(s_gt, it.n))
                e.wait_ge(s_gate, at(s_gate, it.n + 1))
                e.activation(eg[:, 0, :], OB[:, 0:T], ACT.Exp, bias=neg_bgate[:, 0:1], scale=-1.0).then_inc(s_eg, 1)

            def a_exp(e, it, half):
                if due(it.n - 1):
                    e.wait_ge(s_av, at(s_av, it.n - 1))
                e.wait_ge(s_st, at(s_st, 2 * it.n + half + 1))
                e.activation(P[:, it.s % 2, 8 * half:8 * half + 8, :].rearrange("p h t -> p (h t)"),
                             ST_ps[:, :, :].rearrange("p j n -> p (j n)"), ACT.Exp,
                             scale=float(DH) ** -0.5).then_inc(s_exp, 1)

            def scalar(e):
                before(e)
                for item in ticks(e, F + 3, peel):
                    if it := item(F + 1):
                        a_qT(e, it)
                    if it := item(F + 2):
                        a_qS(e, it)
                    if it := item(F + 1):
                        a_kS(e, it)
                    if it := item(F):
                        a_hT(e, it)
                    if it := item(F + 2):
                        a_exp(e, it, 0)
                        a_exp(e, it, 1)
                    if causal and (it := item(F + 3)):
                        a_gate(e, it)

            totals(stats=B, rstd=B, h=B, bn=B, ve=B, hps=B, hT=B, qkv=B, qkf=B * (2 if causal else 1), v=B,
                   hi=B, lo=2 * B, turn=B, kx=B, qT=B, tk=B, kS=B, tq=B, qSv=B, qSa=B, s=2 * B, mx=2 * B,
                   nm=2 * B, st=2 * B, exp=2 * B, av=B, rec=B, o=B, out=B, done=B)
            if projected and not causal:
                totals(xb=B)
            if causal:
                totals(h2=B, bn2=B, st2=B, ms=B, rs2=B, rope=8 * B, sum=B, rs3=B, gate=B, eg=B, gt=B, yb=B,
                       yd=B, gt2=2 * B, ve3=B)
            else:
                totals(**{f"ctx{i}": 16 * GROUPS for i in range(RING)})
            return dict(sync=sync, tensor=tensor, vector=vector, gpsimd=pool, scalar=scalar, done=(s_done, reached["done"]))

        def attention1(p, before):
            at = counted_from(dict(reached))
            s_ctx = [sem(f"ctx{i}") for i in range(RING)]
            s_hps, s_hT, s_qkv, s_qk, s_v = (sem(n) for n in ("hps", "hT", "qkv", "qk", "v"))
            s_s, s_mx, s_nb, s_exp, s_pps, s_pT = (sem(n) for n in ("s", "mx", "nb", "exp", "pps", "pT"))
            s_av, s_rec, s_done = (sem(n) for n in ("av", "rec", "done"))
            stats, aggregate, rsqrt, norm, s_h = stat_stages(at)
            pool_f = P[:].rearrange("p b h t -> p (b h t)")
            q1, k1, v1, p1, pT1 = (pool_f[:, 512 * i:512 * i + 512].rearrange("p (r t) -> p r t", r=RING)
                                   for i in range(5))
            scale = float(D) ** -0.5

            def sync(e):
                before(e)
                for s in range(RING):
                    e.dma_start(ctxT[:, s, :], ctx_dram[:, 0, s, :]).then_inc(s_ctx[s], 16)
                with e.Fori(1, GROUPS, 1) as g:
                    for s in range(RING):
                        e.wait_ge(s_qkv, at(s_qkv, (g - 1) * RING + s + 1))
                        e.dma_start(ctxT[:, s, :], ctx_dram[:, g, s, :]).then_inc(s_ctx[s], 16)

            def tensor(e):
                def pe_hT(it):
                    e.wait_ge(s_h, at(s_h, it.n + 1))
                    if due(it.n):
                        e.wait_ge(s_v, at(s_v, it.n))
                    e.transpose(FR[:, 0:T], h[:, it.s, :], ident[:, :]).then_inc(s_hps, 1)

                def pe_qkv(it):
                    e.wait_ge(s_hT, at(s_hT, it.n + 1))
                    e.wait_ge(s_ctx[it.s], at(s_ctx[it.s], 16 * (it.g + 1)))
                    e.matmul(FR[:, 0:T], w[p + "wq"][:, :], hT[:, it.s, :], start=True, stop=True)
                    e.matmul(FR[:, T:2 * T], w[p + "wk"][:, :], ctxT[:, it.s, :], start=True, stop=True)
                    e.matmul(FR[:, 2 * T:3 * T], ctxT[:, it.s, :], w[p + "wv"][:, :], start=True, stop=True)\
                     .then_inc(s_qkv, 1)

                def pe_scores(it):
                    e.wait_ge(s_qk, at(s_qk, 2 * it.n + 2))
                    if due(it.n):
                        e.wait_ge(s_exp, at(s_exp, it.n))
                    e.matmul(PS[:, 0, 0:T], q1[:, it.s, :], k1[:, it.s, :], start=True, stop=True).then_inc(s_s, 1)

                def pe_pT(it):
                    e.wait_ge(s_exp, at(s_exp, it.n + 1))
                    if due(it.n):
                        e.wait_ge(s_pT, at(s_pT, it.n))
                    e.transpose(PS[:, 4, 0:T], p1[:, it.s, :], ident[:, :]).then_inc(s_pps, 1)

                def pe_values(it):
                    e.wait_ge(s_pT, at(s_pT, it.n + 1))
                    if due(it.n):
                        e.wait_ge(s_done, at(s_done, it.n))
                    e.matmul(OB[:, 0:T], pT1[:, it.s, :], v1[:, it.s, :], start=True, stop=True).then_inc(s_av, 1)
                before(e)
                e.wait_ge(sem(p + "weights"), 16 * n_loads[p[:2]])
                e.wait_ge(consts_ready, N_CONSTS)
                for item in ticks(e, 3):
                    if it := item(3):
                        pe_pT(it)
                    if it := item(1):
                        pe_hT(it)
                    if it := item(2):
                        pe_scores(it)
                    if it := item(3):
                        pe_values(it)
                    if it := item(1):
                        pe_qkv(it)

            def vector(e):
                def v_qkv(it):
                    if due(it.n - RING + 1):
                        e.wait_ge(s_done, at(s_done, it.n - RING + 1))
                    e.wait_ge(s_qkv, at(s_qkv, it.n + 1))
                    e.tensor_scalar(q1[:, it.s, :], FR[:, 0:T], w[p + "bq"][:, 0:1], None, ALU.add).then_inc(s_qk, 1)
                    e.tensor_scalar(k1[:, it.s, :], FR[:, T:2 * T], w[p + "bk"][:, 0:1], None, ALU.add)\
                     .then_inc(s_qk, 1)
                    e.tensor_tensor(v1[:, it.s, :], FR[:, 2 * T:3 * T], w[p + "bv"][:, :], ALU.add).then_inc(s_v, 1)

                def v_max(it):
                    e.wait_ge(s_s, at(s_s, it.n + 1))
                    e.tensor_reduce(mx[:, it.s, 0:1], PS[:, 0, 0:T], AXX, ALU.max).then_inc(s_mx, 1)
                    e.wait_ge(s_mx, at(s_mx, it.n + 1))
                    e.tensor_scalar(mx[:, it.s, 1:2], mx[:, it.s, 0:1], -scale, None, ALU.mult).then_inc(s_nb, 1)

                def v_out(it):
                    e.wait_ge(s_av, at(s_av, it.n + 1))
                    e.reciprocal(mx[:, it.s, 3:4], mx[:, it.s, 2:3]).then_inc(s_rec, 1)
                    e.wait_ge(s_rec, at(s_rec, it.n + 1))
                    e.scalar_tensor_tensor(out=X[:, it.g, it.s, :], in0=OB[:, 0:T], scalar=mx[:, it.s, 3:4],
                                           in1=X[:, it.g, it.s, :], op0=ALU.mult, op1=ALU.add).then_inc(s_done, 1)
                before(e)
                e.wait_ge(sem(p + "weights"), 16 * n_loads[p[:2]])
                for item in ticks(e, 3):
                    if it := item(0):
                        stats(e, it)
                    if it := item(1):
                        norm(e, it, h[:, it.s, :])
                    if it := item(0):
                        aggregate(e, it)
                    if it := item(2):
                        v_max(it)
                    if it := item(3):
                        v_out(it)
                    if it := item(1):
                        v_qkv(it)

            def pool(e):
                before(e)
                for item in ticks(e, 0):
                    if it := item(0):
                        rsqrt(e, it)

            def scalar(e):
                def a_hT(it):
                    if due(it.n - RING + 1):
                        e.wait_ge(s_qkv, at(s_qkv, it.n - RING + 1))
                    e.wait_ge(s_hps, at(s_hps, it.n + 1))
                    e.copy(hT[:, it.s, :], FR[:, 0:T]).then_inc(s_hT, 1)

                def a_exp(it):
                    e.wait_ge(s_nb, at(s_nb, it.n + 1))
                    e.activation(p1[:, it.s, :], PS[:, 0, 0:T], ACT.Exp, scale=scale, bias=mx[:, it.s, 1:2],
                                 accum_out=mx[:, it.s, 2:3]).then_inc(s_exp, 1)

                def a_pT(it):
                    e.wait_ge(s_pps, at(s_pps, it.n + 1))
                    e.copy(pT1[:, it.s, :], PS[:, 4, 0:T]).then_inc(s_pT, 1)
                before(e)
                for item in ticks(e, 3):
                    if it := item(3):
                        a_pT(it)
                    if it := item(1):
                        a_hT(it)
                    if it := item(2):
                        a_exp(it)
            totals(stats=B, rstd=B, h=B, bn=B, ve=B, hps=B, hT=B, qkv=B, qk=2 * B, v=B, s=B, mx=B, nb=B,
                   exp=B, pps=B, pT=B, av=B, rec=B, done=B)
            totals(**{f"ctx{i}": 16 * GROUPS for i in range(RING)})
            return dict(sync=sync, tensor=tensor, vector=vector, gpsimd=pool, scalar=scalar, done=(s_done, reached["done"]))

        def attention8(p, before):
            at = counted_from(dict(reached))
            NH, HD = 8, 64
            s_ctx = [sem(f"ctx{i}") for i in range(RING)]
            s_hps, s_hT, s_q, s_k, s_vps, s_v = (sem(n) for n in ("hps", "hT", "q", "k", "vps", "v"))
            s_qH, s_kH, s_qL, s_kL = (sem(n) for n in ("qH", "kH", "qL", "kL"))
            s_s, s_mx, s_nm, s_md, s_st, s_exp = (sem(n) for n in ("s", "mx", "nm", "md", "st", "exp"))
            s_av, s_rec, s_o, s_ops, s_oT = (sem(n) for n in ("av", "rec", "o", "ops", "oT"))
            s_out, s_xb, s_done, s_pad = (sem(n) for n in ("out", "xb", "done", "pad"))
            stats, aggregate, rsqrt, norm, s_h = stat_stages(at)
            flat = P[:].rearrange("p b h t -> p (b h t)")
            P8 = flat[:, 0:2048].rearrange("p (b h t) -> p b h t", b=2, h=NH)
            VW = 584
            v8 = flat[:, 2048:2048 + 2 * VW].rearrange("p (b n) -> p b n", b=2)
            q8 = qS[:].rearrange("p b g j t -> p (b g j t)").rearrange("p (b a u t) -> p b a u t", b=2, a=2, t=2 * T)
            kH, kL = kx, kS
            md = parts[:].rearrange("p r a h c d -> p (r a h c d)")[:, 0:2048]\
                .rearrange("p (b h t) -> p b h t", b=2, h=NH)
            vflat = vx[:].rearrange("p r n -> p (r n)")
            o8 = vflat[:, 0:1024].rearrange("p (b n) -> p b n", b=2)
            oT8 = vflat[:, 1024:2048].rearrange("p (b n) -> p b n", b=2)

            def sync(e):
                before(e)
                for s in range(RING):
                    e.dma_start(ctxT[:, s, :], ctx_dram[:, 0, s, :]).then_inc(s_ctx[s], 16)
                with e.Fori(1, GROUPS, 1) as g:
                    for s in range(RING):
                        e.wait_ge(s_vps, at(s_vps, (g - 1) * RING + s + 1))
                        e.dma_start(ctxT[:, s, :], ctx_dram[:, g, s, :]).then_inc(s_ctx[s], 16)

            def tensor(e):
                def pe_hT(it):
                    e.wait_ge(s_h, at(s_h, it.n + 1))
                    if due(it.n - 2):
                        e.wait_ge(s_v, at(s_v, it.n - 2))
                    e.transpose(FR[:, 0:T], h[:, it.s, :], ident[:, :]).then_inc(s_hps, 1)

                def pe_qk(it):
                    e.wait_ge(s_hT, at(s_hT, it.n + 1))
                    if due(2 * it.n):
                        e.wait_ge(s_qL, at(s_qL, 2 * it.n))
                    for t in range(4):
                        m = e.matmul(TP[0][:, t * T:(t + 1) * T], w[p + "wq"][:, t * 128:(t + 1) * 128],
                                     hT[:, it.s, :], start=True, stop=True)
                    m.then_inc(s_q, 1)
                    e.wait_ge(s_ctx[it.s], at(s_ctx[it.s], 16 * (it.g + 1)))
                    if due(it.n):
                        e.wait_ge(s_kL, at(s_kL, it.n))
                    for t in range(4):
                        m = e.matmul(TP[1][:, t * T:(t + 1) * T], w[p + "wk"][:, t * 128:(t + 1) * 128],
                                     ctxT[:, it.s, :], start=True, stop=True)
                    m.then_inc(s_k, 1)

                def pe_v(it):
                    e.wait_ge(s_hT, at(s_hT, following(it, 3)))
                    e.matmul(FR[:, :], ctxT[:, it.s, :], w[p + "wv"][:, :], start=True, stop=True).then_inc(s_vps, 1)

                def pe_scores(it):
                    e.wait_ge(s_qH, at(s_qH, 2 * it.n + 2))
                    e.wait_ge(s_kH, at(s_kH, it.n + 1))
                    if due(it.n):
                        e.wait_ge(s_mx, at(s_mx, it.n))
                    for hd in range(NH):
                        t, u = hd // 2, hd % 2
                        m = e.matmul(S_ps[:, hd // 4, (hd % 4) * T:(hd % 4 + 1) * T],
                                     q8[:, it.s % 2, 0, t, u * T:(u + 1) * T], kH[:, it.s % 2, t, :],
                                     start=True, stop=True)
                    m.then_inc(s_s, 1)

                def pe_scoresT(it):
                    e.wait_ge(s_md, at(s_md, it.n + 1))
                    e.wait_ge(s_qL, at(s_qL, 2 * it.n + 2))
                    e.wait_ge(s_kL, at(s_kL, it.n + 1))
                    if due(it.n):
                        e.wait_ge(s_exp, at(s_exp, it.n))
                    for b in range(2):
                        e.matmul(ST_ps[:, b, :], ones_r[:, :],
                                 md[:, it.s % 2, 4 * b:4 * b + 4, :].rearrange("p h t -> p (h t)"),
                                 start=True, stop=False)
                        for t in (2 * b, 2 * b + 1):
                            dst = ST_ps[:, b, (t % 2) * 2 * T:(t % 2 + 1) * 2 * T]
                            for kk, a_ in ((kH, 0), (kL, 0), (kH, 1)):
                                m = e.matmul(dst, kk[:, it.s % 2, t, :], q8[:, it.s % 2, a_, t, :],
                                             start=False, stop=(t == 2 * b + 1 and kk is kH and a_ == 1))
                    m.then_inc(s_st, 1)

                def pe_values(it, half):
                    if half == 0:
                        e.wait_ge(s_exp, at(s_exp, it.n + 1))
                        e.wait_ge(s_v, at(s_v, it.n + 1))
                        if due(it.n):
                            e.wait_ge(s_done, at(s_done, it.n))
                    else:
                        e.wait_ge(s_o, at(s_o, 2 * it.n + 1))
                    for i in range(4):
                        hd = 4 * half + i
                        m = e.matmul(OB[:, i * T:(i + 1) * T], P8[:, it.s % 2, hd, :],
                                     v8[:, it.s % 2, hd * (HD + 1):hd * (HD + 1) + T], start=True, stop=True)
                    m.then_inc(s_av, 1)

                def pe_oT(it):
                    e.wait_ge(s_o, at(s_o, 2 * it.n + 2))
                    for t in range(4):
                        m = e.transpose(OB[:, t * T:(t + 1) * T], o8[:, it.s % 2, t * 128:(t + 1) * 128], ident[:, :])
                    m.then_inc(s_ops, 1)

                def pe_out(it):
                    e.wait_ge(s_oT, at(s_oT, it.n + 1))
                    for t in range(4):
                        m = e.matmul(OB[:, 0:D], oT8[:, it.s % 2, t * T:(t + 1) * T], w[p + "wo"][:, t, :],
                                     start=(t == 0), stop=(t == 3))
                    m.then_inc(s_out, 1)
                before(e)
                e.wait_ge(sem(p + "weights"), 16 * n_loads[p[:2]])
                e.wait_ge(consts_ready, N_CONSTS)
                e.wait_ge(s_pad, at(s_pad, 2))
                for item in ticks(e, 5):
                    if it := item(5):
                        pe_out(it)
                    if it := item(1):
                        pe_hT(it)
                    if it := item(4):
                        pe_values(it, 0)
                    if it := item(2):
                        pe_scores(it)
                    if it := item(3):
                        pe_scoresT(it)
                    if it := item(4):
                        pe_values(it, 1)
                    if it := item(3):
                        pe_v(it)
                    if it := item(1):
                        pe_qk(it)
                    if it := item(4):
                        pe_oT(it)

            def vector(e):
                def v_low(it):
                    e.wait_ge(s_qH, at(s_qH, 2 * it.n + 2))
                    for u in range(2):
                        r = slice(64 * u, 64 * u + 64)
                        e.tensor_tensor(q8[r, it.s % 2, 1, :, u * T:(u + 1) * T],
                                        TP[0][r, :].rearrange("p (t n) -> p t n", t=4),
                                        q8[r, it.s % 2, 0, :, u * T:(u + 1) * T].bitcast(F32),
                                        ALU.subtract).then_inc(s_qL, 1)
                    e.wait_ge(s_kH, at(s_kH, it.n + 1))
                    e.tensor_tensor(kL[:, it.s % 2, :, :].rearrange("p t n -> p (t n)"), TP[1][:, :],
                                    kH[:, it.s % 2, :, :].rearrange("p t n -> p (t n)").bitcast(F32),
                                    ALU.subtract).then_inc(s_kL, 1)

                def v_max(it):
                    e.wait_ge(s_s, at(s_s, it.n + 1))
                    e.tensor_reduce(mx[:, it.s, 0:NH], S_ps[:, :, :].rearrange("p i (j t) -> p (i j) t", t=T),
                                    AXX, ALU.max).then_inc(s_mx, 1)
                    e.wait_ge(s_mx, at(s_mx, it.n + 1))
                    e.tensor_scalar(mx[:, it.s, NH:2 * NH], mx[:, it.s, 0:NH], -1.0, None, ALU.mult).then_inc(s_nm, 1)

                def v_heads(it, half):
                    e.wait_ge(s_av, at(s_av, 2 * it.n + half + 1))
                    ob = OB[:, :].rearrange("p (h n) -> p h n", n=T)
                    e.reciprocal(rec[:, 0:4].unsqueeze(2), ob[:, :, HD:HD + 1]).then_inc(s_rec, 1)
                    if half == 0:
                        if due(it.n - 1):
                            e.wait_ge(s_ops, at(s_ops, it.n - 1))
                    e.wait_ge(s_rec, at(s_rec, 2 * it.n + half + 1))
                    e.tensor_tensor(o8[:, it.s % 2, 256 * half:256 * half + 256].rearrange("p (h n) -> p h n", h=4),
                                    ob[:, :, 0:HD], rec[:, 0:4].unsqueeze(2).broadcast_to([T, 4, HD]),
                                    ALU.mult).then_inc(s_o, 1)

                def v_residual(it):
                    e.wait_ge(s_xb, at(s_xb, it.n + 1))
                    e.wait_ge(s_out, at(s_out, it.n + 1))
                    e.tensor_tensor(X[:, it.g, it.s, :], X[:, it.g, it.s, :], OB[:, 0:D], ALU.add).then_inc(s_done, 1)
                before(e)
                e.wait_ge(sem(p + "weights"), 16 * n_loads[p[:2]])
                for item in ticks(e, 5):
                    if it := item(5):
                        v_residual(it)
                    if it := item(2):
                        v_low(it)
                    if it := item(0):
                        stats(e, it)
                    if it := item(1):
                        norm(e, it, h[:, it.s, :])
                    if it := item(0):
                        aggregate(e, it)
                    if it := item(4):
                        v_heads(it, 0)
                    if it := item(2):
                        v_max(it)
                    if it := item(4):
                        v_heads(it, 1)

            def pool(e):
                def g_bias(it):
                    e.wait_ge(s_h, at(s_h, it.n + 1))
                    e.tensor_tensor(X[:, it.g, it.s, :], X[:, it.g, it.s, :], w[p + "bo"][:, :], ALU.add)\
                     .then_inc(s_xb, 1)

                def g_diagonals(it):
                    if due(it.n - 1):
                        e.wait_ge(s_st, at(s_st, it.n - 1))
                    e.wait_ge(s_nm, at(s_nm, it.n + 1))
                    e.tensor_tensor(md[:, it.s % 2], ident[:, :].unsqueeze(1).broadcast_to([T, NH, T]),
                                    mx[:, it.s, NH:2 * NH].unsqueeze(2).broadcast_to([T, NH, T]),
                                    ALU.mult).then_inc(s_md, 1)
                before(e)
                e.wait_ge(sem(p + "weights"), 16 * n_loads[p[:2]])
                e.memset(qS[:].bitcast(F32), 0.0).then_inc(s_pad, 1)
                e.memset(v8[:, :, :], 1.0).then_inc(s_pad, 1)
                for item in ticks(e, 2):
                    if it := item(0):
                        rsqrt(e, it)
                    if it := item(1):
                        g_bias(it)
                    if it := item(2):
                        g_diagonals(it)

            def scalar(e):
                def a_high(it):
                    if due(it.n - 1):
                        e.wait_ge(s_st, at(s_st, it.n - 1))
                    e.wait_ge(s_q, at(s_q, it.n + 1))
                    for u in range(2):
                        r = slice(64 * u, 64 * u + 64)
                        e.copy(q8[r, it.s % 2, 0, :, u * T:(u + 1) * T],
                               TP[0][r, :].rearrange("p (t n) -> p t n", t=4)).then_inc(s_qH, 1)
                    e.wait_ge(s_k, at(s_k, it.n + 1))
                    e.copy(kH[:, it.s % 2, :, :].rearrange("p t n -> p (t n)"), TP[1][:, :]).then_inc(s_kH, 1)

                def a_hT(it):
                    if due(it.n - RING + 1):
                        e.wait_ge(s_q, at(s_q, it.n - RING + 1))
                    e.wait_ge(s_hps, at(s_hps, it.n + 1))
                    e.copy(hT[:, it.s, :], FR[:, 0:T]).then_inc(s_hT, 1)

                def a_exp(it):
                    if due(2 * (it.n - 1)):
                        e.wait_ge(s_av, at(s_av, 2 * (it.n - 1)))
                    e.wait_ge(s_st, at(s_st, it.n + 1))
                    e.activation(P8[:, it.s % 2, :, :].rearrange("p h t -> p (h t)"),
                                 ST_ps[:, :, :].rearrange("p j n -> p (j n)"), ACT.Exp,
                                 scale=float(HD) ** -0.5).then_inc(s_exp, 1)

                def a_v(it):
                    if due(2 * (it.n - 1)):
                        e.wait_ge(s_av, at(s_av, 2 * (it.n - 1)))
                    e.wait_ge(s_vps, at(s_vps, it.n + 1))
                    e.copy(v8[:, it.s % 2, 0:NH * (HD + 1)].rearrange("p (h n) -> p h n", h=NH)[:, :, 0:HD],
                           FR[:, :].rearrange("p (h n) -> p h n", h=NH)).then_inc(s_v, 1)

                def a_oT(it):
                    if due(it.n - 1):
                        e.wait_ge(s_out, at(s_out, it.n - 1))
                    e.wait_ge(s_ops, at(s_ops, it.n + 1))
                    e.copy(oT8[:, it.s % 2, :], OB[:, :]).then_inc(s_oT, 1)
                before(e)
                e.wait_ge(s_pad, at(s_pad, 2))
                for item in ticks(e, 4):
                    if it := item(2):
                        a_high(it)
                    if it := item(1):
                        a_hT(it)
                    if it := item(3):
                        a_exp(it)
                    if it := item(3):
                        a_v(it)
                    if it := item(4):
                        a_oT(it)
            totals(stats=B, rstd=B, h=B, bn=B, ve=B, hps=B, hT=B, q=B, k=B, vps=B, v=B, qH=2 * B, kH=B,
                   qL=2 * B, kL=B, s=B, mx=B, nm=B, md=B, st=B, exp=B, av=2 * B, rec=2 * B, o=2 * B, ops=B,
                   oT=B, out=B, xb=B, done=B, pad=2)
            totals(**{f"ctx{i}": 16 * GROUPS for i in range(RING)})
            return dict(sync=sync, tensor=tensor, vector=vector, gpsimd=pool, scalar=scalar, done=(s_done, reached["done"]))

        def experts(p, before, E, tiles, kind, top_k, source, shared=False):
            at = counted_from(dict(reached))
            n_exp = E + (1 if shared else 0)
            n_z = {"gelu": tiles, "relu": tiles, "glu": 2 * tiles, "linear": 0}[kind] * n_exp
            per_e = n_z // n_exp
            s_bn, s_st, s_ms = sem("bn"), sem("stats"), sem("ms")
            s_ve, s_rs, s_h = sem("ve"), sem("rstd"), sem("h")
            s_hps, s_hT, s_lg = sem("hps"), sem("hT"), sem("logits")
            s_r, s_e = sem("route"), sem("exp")
            s_wt, s_wps, s_wT = sem("wt"), sem("wps"), sem("wT")
            s_loc, s_locr = sem("loc"), sem("loc_read")
            s_z, s_g, s_sig = sem("z"), sem("g"), sem("sig")
            s_y, s_acc, s_done = sem("y"), sem("acc"), sem("done")
            rms = kind == "glu"
            wg, b2 = w[p + "wg"], w.get(p + "b2")
            w1, b1, w2 = w.get(p + "w1"), w.get(p + "b1"), w[p + "w2"]
            n_steps = n_exp + (1 if b2 is not None else 0)
            ZP = [PS[:, 0, :], PS[:, 1, :]]
            YP = [PS[:, 2, :], PS[:, 3, :]]
            HP, LP, WP = PS[:, 4, :], PS[:, 5, :], PS[:, 6, :]
            chain = {}

            def groups(e, prologue, body):
                before(e)
                e.wait_ge(sem(p + "weights"), 16 * n_loads[p[:2]])
                e.wait_ge(consts_ready, N_CONSTS)
                prologue()
                body(0, True)
                with e.Fori(1, GROUPS - 1, 1) as g:
                    body(g, True)
                body(GROUPS - 1, False)

            def tensor(e):
                def prep(g):
                    for s in range(RING):
                        e.wait_ge(s_h, at(s_h, RING * g + s + 1))
                        if s == 0:
                            if due(g):
                                e.wait_ge(s_hT, at(s_hT, g))
                        m = e.transpose(HP[:, s * T:(s + 1) * T], h[:, s, :], ident[:, :])
                        m.then_inc(s_hps, 1)

                def logits(g):
                    if due(n_route * (g - 1) + 1):
                        e.wait_ge(s_r, at(s_r, n_route * (g - 1) + 1))
                    e.wait_ge(s_hT, at(s_hT, g + 1))
                    for s in range(RING):
                        m = e.matmul(LP[:, s * E:(s + 1) * E], hT4[:, s * T:(s + 1) * T], wg[:, :],
                                     start=True, stop=True)
                    m.then_inc(s_lg, 1)

                def z(g, i):
                    if due(zfree(g, i)):
                        e.wait_ge(s_g, at(s_g, zfree(g, i)))
                    x, t = i // per_e, i % per_e
                    e.matmul(ZP[i % 2][:, :], w1[:, x, t * 128:(t + 1) * 128], hT4[:, :],
                             start=True, stop=True).then_inc(s_z, 1)

                def zfree(g, i):
                    if kind == "glu":
                        return tiles * n_exp * g + i // 2
                    return n_z * g + i - 1

                def y(g, x):
                    k = n_exp * g + x
                    if due(RING * (n_steps * g + x - 1)):
                        e.wait_ge(s_acc, at(s_acc, RING * (n_steps * g + x - 1)))
                    if kind != "linear":
                        e.wait_ge(s_g, at(s_g, tiles * (k + 1)))
                    for s in range(RING):
                        for t in range(tiles):
                            lhs = hT4[:, s * T:(s + 1) * T] if kind == "linear" else \
                                gt[:, (x % 2) * tiles + t, s * T:(s + 1) * T]
                            m = e.matmul(YP[x % 2][:, s * T:(s + 1) * T], lhs, w2[:, x, t * D:(t + 1) * D],
                                         start=(t == 0), stop=(t == tiles - 1))
                    m.then_inc(s_y, 1)

                def bias(g):
                    if due(g):
                        e.wait_ge(s_wT, at(s_wT, g))
                    e.wait_ge(s_wt, at(s_wt, n_wt * (g + 1)))
                    for s in range(RING):
                        m = e.transpose(WP[0:n_exp, s * T:(s + 1) * T], wt[:, s, 0:n_exp], ident[:, :])
                    m.then_inc(s_wps, 1)

                def bias_rows(g):
                    e.wait_ge(s_wT, at(s_wT, g + 1))
                    if due(RING * (n_steps * g + n_exp - 1)):
                        e.wait_ge(s_acc, at(s_acc, RING * (n_steps * g + n_exp - 1)))
                    for s in range(RING):
                        m = e.matmul(YP[n_exp % 2][:, s * T:(s + 1) * T], wT[0:n_exp, s * T:(s + 1) * T],
                                     b2[:, :], start=True, stop=True)
                    m.then_inc(s_y, 1)

                def positions(g):
                    if due(g):
                        e.wait_ge(s_wT, at(s_wT, g))
                    e.wait_ge(s_r, at(s_r, n_route * g + n_before_loc))
                    for s in range(RING):
                        e.matmul(WP[:, s * E:(s + 1) * E], earlier[:, :], sel[:, s, 0:E], start=True, stop=False)
                        m = e.matmul(WP[:, s * E:(s + 1) * E], ones[:, :], run[:, s, :], start=False, stop=True)
                    m.then_inc(s_loc, 1)

                def prologue():
                    prep(0)

                def body(g, more):
                    logits(g)
                    for x in range(n_exp + 1):
                        if x < n_exp:
                            for t in range(per_e):
                                z(g, x * per_e + t)
                        if x == n_exp - (kind != "linear") and more:
                            prep(g + 1)
                        if kind == "linear" and x == 0:
                            positions(g)
                        if x >= 1:
                            y(g, x - 1)
                        if b2 is not None and x == 1:
                            bias(g)
                    if b2 is not None:
                        bias_rows(g)
                groups(e, prologue, body)

            def vector(e):
                def prep(g):
                    for s in range(RING):
                        k = RING * g + s
                        if due(RING * (g - 1) + s + 1):
                            e.wait_ge(s_hps, at(s_hps, RING * (g - 1) + s + 1))
                        e.bn_stats(bn[:, s, :], source[:, g, s, :]).then_inc(s_bn, 1)
                    e.wait_ge(s_bn, at(s_bn, RING * (g + 1)))
                    e.tensor_copy(scratch[:, 0:1], neg_half[:, 0:1])
                    for s in range(RING):
                        m = e.bn_aggr(mv[:, s, :], bn[:, s, :])
                        m.then_inc(s_st, 1)
                    if rms:
                        e.wait_ge(s_st, at(s_st, RING * (g + 1)))
                        e.tensor_tensor(ve[:, :, :], mv[:, :, 0:1], mv[:, :, 0:1], ALU.mult).then_inc(s_ms, 1)
                        e.wait_ge(s_ms, at(s_ms, 2 * g + 1))
                        e.tensor_tensor(mv[:, :, 1:2], mv[:, :, 1:2], ve[:, :, :], ALU.add).then_inc(s_ms, 1)
                    e.wait_ge(s_rs, at(s_rs, g + 1))
                    for s in range(RING):
                        if rms:
                            m = e.tensor_scalar(h[:, s, :], source[:, g, s, :], rstd[:, s, :], None, ALU.mult)
                        else:
                            m = e.tensor_scalar(h[:, s, :], source[:, g, s, :], mv[:, s, 0:1], rstd[:, s, :],
                                                ALU.subtract, ALU.mult)
                        m.then_inc(s_h, 1)

                def bc(t):
                    return t[:, :].unsqueeze(2).broadcast_to([T, RING, E])

                def route(g):
                    n = [0]

                    def step(m):
                        n[0] += 1
                        m.then_inc(s_r, 1)
                        e.wait_ge(s_r, at(s_r, n_route * g + n[0]))
                    e.wait_ge(s_lg, at(s_lg, g + 1))
                    lp = LP[:, 0:RING * E].rearrange("p (s x) -> p s x", s=RING)
                    if p + "bg" in w:
                        step(e.tensor_tensor(lg[:, :, 0:E], lp,
                                             w[p + "bg"][:, :].unsqueeze(1).broadcast_to([T, RING, E]), ALU.add))
                    else:
                        step(e.tensor_copy(lg[:, :, 0:E], lp))
                    L, SEL, TMP = lg[:, :, 0:E], sel[:, :, 0:E], tmp[:, :, 0:E]
                    for k in range(top_k):
                        step(e.tensor_reduce(rmax[:, :], L, AXX, ALU.max))
                        if k == 0 and kind != "glu":
                            step(e.tensor_tensor(pr[:, :, 0:E], L, bc(rmax), ALU.subtract))
                        step(e.tensor_tensor(TMP, L, bc(rmax), ALU.is_equal))
                        step(e.tensor_tensor(TMP, TMP, rank[:, 0:E].unsqueeze(1).broadcast_to([T, RING, E]), ALU.mult))
                        step(e.tensor_reduce(rmax[:, :], TMP, AXX, ALU.max))
                        if k == 0:
                            step(e.tensor_tensor(SEL, TMP, bc(rmax), ALU.is_equal))
                            one = SEL
                        else:
                            step(e.tensor_tensor(TMP, TMP, bc(rmax), ALU.is_equal))
                            step(e.tensor_tensor(SEL, SEL, TMP, ALU.add))
                            one = TMP
                        if k < top_k - 1:
                            step(e.scalar_tensor_tensor(out=L, in0=one, scalar=-BIG, in1=L, op0=ALU.mult, op1=ALU.add))
                    if kind == "linear":
                        for s in range(RING):
                            step(e.tensor_tensor(run[:, s + 1, :], run[:, s, :], sel[:, s, 0:E], ALU.add))
                        assert n[0] == n_before_loc
                        e.wait_ge(s_loc, at(s_loc, g + 1))
                        loc = WP[:, 0:RING * E].rearrange("p (s x) -> p s x", s=RING)
                        e.tensor_scalar(tmp[:, :, 0:E], loc, float(B * T // E), None, ALU.is_lt).then_inc(s_locr, 1)
                        e.wait_ge(s_locr, at(s_locr, g + 1))
                        step(e.tensor_tensor(SEL, SEL, TMP, ALU.mult))
                        step(e.tensor_copy(run[:, 0, :], run[:, RING, :]))
                    if kind != "glu":
                        e.wait_ge(s_e, at(s_e, g + 1))
                        step(e.tensor_reduce(rsum[:, :], pr[:, :, 0:E], AXX, ALU.add))
                        step(e.reciprocal(rsum[:, :], rsum[:, :]))
                        step(e.tensor_tensor(pr[:, :, 0:E], pr[:, :, 0:E], bc(rsum), ALU.mult))
                        e.tensor_tensor(wt[:, :, 0:E], SEL, pr[:, :, 0:E], ALU.mult).then_inc(s_wt, 1)
                    else:
                        e.tensor_copy(wt[:, :, 0:E], SEL).then_inc(s_wt, 1)
                    assert n[0] == n_route, n[0]

                def add(g, x):
                    k = n_steps * g + x
                    e.wait_ge(s_y, at(s_y, k + 1))
                    if x == 0:
                        e.wait_ge(s_wt, at(s_wt, n_wt * (g + 1)))
                    for s in range(RING):
                        if due(RING * (k - 1) + s + 1):
                            e.wait_ge(s_acc, at(s_acc, RING * (k - 1) + s + 1))
                        X_s = X[:, g, s, :]
                        rows = YP[x % 2][:, s * T:(s + 1) * T]
                        if x < E:
                            m = e.scalar_tensor_tensor(out=X_s, in0=rows, scalar=wt[:, s, x:x + 1], in1=X_s,
                                                       op0=ALU.mult, op1=ALU.add)
                        else:
                            m = e.tensor_tensor(X_s, X_s, rows, ALU.add)
                        m.then_inc(s_acc, 1)

                def product(g, i):
                    x, t = i // tiles, i % tiles
                    if due(n_steps * g + x - 1):
                        e.wait_ge(s_y, at(s_y, n_steps * g + x - 1))
                    e.wait_ge(s_sig, at(s_sig, tiles * n_exp * g + i + 1))
                    e.scalar_tensor_tensor(out=gt[:, (x % 2) * tiles + t, :], in0=ZP[0][:, :],
                                           scalar=b1[:, x, t:t + 1], in1=sg[:, i % 2, :],
                                           op0=ALU.add, op1=ALU.mult).then_inc(s_g, 1)

                def prologue():
                    if kind == "linear":
                        e.memset(run[:, 0, :], 0.0).then_inc(s_ms, 1)
                        e.wait_ge(s_ms, at(s_ms, 1))
                    if shared:
                        e.memset(wt[:, :, E:E + 1], 1.0).then_inc(s_ms, 1)
                    prep(0)

                def body(g, more):
                    route(g)
                    for x in range(n_steps + 1):
                        if kind == "glu" and x < n_exp:
                            for t in range(tiles):
                                product(g, x * tiles + t)
                        if x == 1 and more:
                            prep(g + 1)
                        if x >= 1:
                            add(g, x - 1)
                groups(e, prologue, body)

            def pool(e):
                def rs(g):
                    if rms:
                        e.wait_ge(s_ms, at(s_ms, 2 * (g + 1)))
                    else:
                        e.wait_ge(s_st, at(s_st, RING * (g + 1)))
                    e.tensor_tensor(ve2[:, :, :], mv[:, :, 1:2], eps_t[:, (1 if rms else 0):][:, 0:1].unsqueeze(1).broadcast_to([T, RING, 1]),
                                    ALU.add).then_inc(s_ve, 1)
                    e.wait_ge(s_ve, at(s_ve, g + 1))
                    if due(RING * g):
                        e.wait_ge(s_h, at(s_h, RING * g))
                    e.tensor_tensor(rstd[:, :, :], ve2[:, :, :], neg_half[:, 0:RING].unsqueeze(2), ALU.pow)\
                     .then_inc(s_rs, 1)

                def prologue():
                    rs(0)

                def body(g, more):
                    if more:
                        rs(g + 1)
                groups(e, prologue, body)

            def scalar(e):
                def turn(g):
                    if due(g):
                        e.wait_ge(s_lg, at(s_lg, g))
                    if due((n_z or n_steps) * g):
                        e.wait_ge(s_z if n_z else s_y, at(s_z if n_z else s_y, (n_z or n_steps) * g))
                    e.wait_ge(s_hps, at(s_hps, RING * (g + 1)))
                    if rms:
                        m = e.activation(hT4[:, :], HP[:, :], ACT.Identity, scale=w[p + "ln"][:, 0:1])
                    else:
                        m = e.copy(hT4[:, :], HP[:, :])
                    m.then_inc(s_hT, 1)

                def route_exp(g):
                    e.wait_ge(s_r, at(s_r, n_route * g + 3))
                    e.activation(pr[:, :, 0:E], pr[:, :, 0:E], ACT.Exp).then_inc(s_e, 1)

                def hidden(g, i):
                    x, t = i // per_e, i % per_e
                    if kind == "glu":
                        if t % 2 == 0:
                            return
                        j = i // 2
                        if due(tiles * n_exp * g + j - 1):
                            e.wait_ge(s_g, at(s_g, tiles * n_exp * g + j - 1))
                        e.wait_ge(s_z, at(s_z, n_z * g + i + 1))
                        e.activation(sg[:, j % 2, :], ZP[1][:, :], ACT.Sigmoid,
                                     bias=b1[:, x, tiles + t // 2:tiles + t // 2 + 1]).then_inc(s_sig, 1)
                        return
                    if due(n_steps * g + x - 1 if x >= 2 else bound(g, x)):
                        e.wait_ge(s_y, at(s_y, n_steps * g + x - 1 if x >= 2 else bound(g, x)))
                    e.wait_ge(s_z, at(s_z, n_z * g + i + 1))
                    e.activation(gt[:, (x % 2) * tiles + t, :], ZP[i % 2][:, :],
                                 ACT.Gelu if kind == "gelu" else ACT.Relu,
                                 bias=b1[:, x, t:t + 1]).then_inc(s_g, 1)

                def bound(g, x):
                    last = n_exp - 2 + x
                    same = last if last % 2 == x % 2 else last + 1
                    return n_steps * (g - 1) + min(same, n_exp - 1) + 1

                def turn_weights(g):
                    if due(n_steps * g):
                        e.wait_ge(s_y, at(s_y, n_steps * g))
                    e.wait_ge(s_wps, at(s_wps, g + 1))
                    e.copy(wT[0:n_exp, :], WP[0:n_exp, :]).then_inc(s_wT, 1)

                def body(g, more):
                    if kind != "glu":
                        route_exp(g)
                    if b2 is not None and n_z == 0:
                        turn_weights(g)
                    for i in range(n_z):
                        hidden(g, i)
                        if b2 is not None and i == min(2 * per_e, n_z) - 1:
                            turn_weights(g)
                    if more:
                        turn(g + 1)
                groups(e, lambda: turn(0), body)

            n_wt = 1
            n_route = 1
            for k in range(top_k):
                n_route += 1 + (1 if k == 0 and kind != "glu" else 0) + 3
                n_route += 1 if k == 0 else 2
                n_route += 1 if k < top_k - 1 else 0
            n_before_loc = n_route + RING
            if kind == "linear":
                n_route += RING + 2
            if kind != "glu":
                n_route += 3

            hidden_steps = n_z // 2 if kind == "glu" else n_z
            totals(bn=B, stats=B, h=B, hps=B, ve=GROUPS, rstd=GROUPS, hT=GROUPS, logits=GROUPS,
                   route=n_route * GROUPS, wt=GROUPS, z=n_z * GROUPS, g=hidden_steps * GROUPS,
                   y=n_steps * GROUPS, acc=RING * n_steps * GROUPS)
            if kind == "glu":
                totals(ms=2 * GROUPS, sig=hidden_steps * GROUPS)
            else:
                totals(exp=GROUPS)
            totals(ms=int(kind == "linear") + int(shared))
            if kind == "linear":
                totals(loc=GROUPS, loc_read=GROUPS)
            if b2 is not None:
                totals(wps=GROUPS, wT=GROUPS)
            return dict(sync=lambda e: None, tensor=tensor, vector=vector, gpsimd=pool, scalar=scalar,
                        done=(s_acc, reached["acc"]))

        n_loads = {}
        for ph, _, _ in loads:
            n_loads[ph] = n_loads.get(ph, 0) + 1
        x_loaded = sem("x_loaded")

        def first(e):
            e.wait_ge(x_loaded, 16)
            e.wait_ge(sem("a0_weights"), 16 * n_loads["a0"])

        phases = []

        def follow(make, *args, **kw):
            if phases:
                s_before, count = phases[-1]["done"]
                phases.append(make(args[0], lambda e: e.wait_ge(s_before, count), *args[1:], **kw))
            else:
                phases.append(make(args[0], first, *args[1:], **kw))

        plan = [("a0", lambda: follow(attention16, "a0_", "cross")),
                ("f0", lambda: follow(experts, "f0_", 8, 4, "gelu", 1, X)),
                ("a1", lambda: follow(attention1, "a1_")),
                ("f1", lambda: follow(experts, "f1_", 15, 1, "relu", 3, X, shared=True)),
                ("a2", lambda: follow(attention16, "a2_", "masked")),
                ("b2", lambda: follow(attention16, "b2_", "self")),
                ("f2", lambda: follow(experts, "f2_", 8, 2, "glu", 1, Y)),
                ("a3", lambda: follow(attention8, "a3_")),
                ("f3", lambda: follow(experts, "f3_", 8, 1, "linear", 1, X))]
        ran = []
        only = upto.split(":")[1] if ":" in upto else None
        for name, make in plan:
            if only is None or name in only.split("+"):
                make()
                ran.append(name)
            if name == upto:
                break
        stored = sem("stored")
        block = ctx.enter_context(nc.Block())

        @block.sync
        def _(e):
            late = {n: b for n, b in (("f2", "f0"), ("f3", "f1")) if b in ran}

            def load(name):
                for ph, tile, arr in loads:
                    if ph == name:
                        e.dma_start(tile, arr).then_inc(sem(ph + "_weights"), 16)
            load("a0")
            e.dma_start(X[:], x_dram).then_inc(x_loaded, 16)
            for name in ran:
                if name != "a0" and name not in late:
                    load(name)
            for name, p in zip(ran, phases):
                p["sync"](e)
                for later, earlier_phase in late.items():
                    if earlier_phase == name and later in ran:
                        e.wait_ge(*p["done"])
                        load(later)
            e.wait_ge(*phases[-1]["done"])
            e.dma_start(out_dram, X[:]).then_inc(stored, 16)
            e.wait_ge(stored, 16)

        @block.tensor
        def _(e):
            for p in phases:
                p["tensor"](e)

        @block.vector
        def _(e):
            e.memset(neg_half[:], -0.5).then_inc(consts_ready, 1)
            e.memset(vx[:], 0.0).then_inc(consts_ready, 1)
            e.memset(ones_x[:], 0.0).then_inc(consts_ready, 1)
            e.memset(ones[:], 1.0).then_inc(consts_ready, 1)
            e.memset(qS[:].bitcast(F32), 0.0).then_inc(consts_ready, 1)
            e.wait_ge(consts_ready, 4)
            for j in range(4):
                e.memset(ones_x[:, j, j, :], 1.0).then_inc(consts_ready, 1)
            e.wait_ge(sem("a0_weights"), 16 * n_loads["a0"])
            e.tensor_copy(ident_r[:], ident[:]).then_inc(consts_ready, 1)
            e.tensor_copy(ones_r[:], ones[:]).then_inc(consts_ready, 1)
            e.tensor_copy(keep[:].rearrange("p g s -> p (g s)"), keep_words[:].bitcast(U8)).then_inc(consts_ready, 1)
            for i, dst in enumerate((causal_q, causal_k)):
                e.tensor_copy(dst[:].rearrange("p (j t) -> p j t", j=4),
                              causal_in[:, i, :].unsqueeze(1).broadcast_to([T, 4, T])).then_inc(consts_ready, 1)
            e.tensor_scalar(neg_bgate[:], w["b2_bgate"][:], -1.0, None, ALU.mult).then_inc(consts_ready, 1)
            for p in phases:
                p["vector"](e)

        @block.gpsimd
        def _(e):
            e.memset(eps_t[:, 0:1], EPS).then_inc(ones_ready, 1)
            e.memset(eps_t[:, 1:2], RMS_EPS).then_inc(ones_ready, 1)
            e.memset(zeros[:], 0.0).then_inc(ones_ready, 1)
            e.memset(parts[:].bitcast(F32), 0.0).then_inc(ones_ready, 1)
            e.wait_ge(ones_ready, 4)
            e.memset(parts[:, :, 1, :, 3, 0:1].rearrange("p r h o -> p r (h o)").bitcast(F32), 1.0)\
             .then_inc(ones_ready, 1)
            e.wait_ge(ones_ready, 5)
            e.wait_ge(consts_ready, N_CONSTS)
            for p in phases:
                p["gpsimd"](e)

        @block.scalar
        def _(e):
            for p in phases:
                p["scalar"](e)


def layout(i):
    def rows(v, n=128):
        return np.broadcast_to(v, (n,) + v.shape).reshape(n, -1)
    a = {}
    a["x"] = i["x"]
    a["ctxT"] = i["ctx_768"].transpose(0, 2, 1)
    a["ident"] = np.eye(128, dtype=np.float32)
    a["jmask"] = np.tile(np.repeat(np.eye(4, dtype=np.float32), DH, 0), (4, 1))
    a["a0_wq"] = i["L0_xattn_wq"].T
    a["a0_wkv"] = np.concatenate([i["L0_xattn_wk"].T, i["L0_xattn_wv"].T], 1)
    a["a0_bqk"] = rows(np.concatenate([i["L0_xattn_bq"], i["L0_xattn_bk"]]))
    a["a0_bv"] = rows(i["L0_xattn_bv"])
    a["a0_wo"] = i["L0_xattn_wo"].T
    a["a0_bo"] = rows(i["L0_xattn_bo"])
    a["a1_wq"], a["a1_wk"], a["a1_wv"] = i["L1_xattn_Wq"], i["L1_xattn_Wk"], i["L1_xattn_Wv"]
    a["a1_bq"], a["a1_bk"] = i["L1_xattn_bq"].reshape(D, 1), i["L1_xattn_bk"].reshape(D, 1)
    a["a1_bv"] = rows(i["L1_xattn_bv"])
    a["a3_wq"], a["a3_wk"], a["a3_wv"] = i["L3_xattn_Wq"], i["L3_xattn_Wk"], i["L3_xattn_Wv"]
    a["a3_wo"] = i["L3_xattn_Wo"].reshape(4, 128, D).transpose(1, 0, 2)
    a["a3_bo"] = rows(i["L3_xattn_bo"])
    a["keep"] = np.ascontiguousarray(i["mask_BxS_bk0"].T).view(np.int32)
    q, k = np.arange(T)[:, None], np.arange(T)[None, :]
    a["causal"] = np.stack([np.where(k > q, -BIG, 0), np.where(q > k, -BIG, 0)], 1).astype(np.float32)
    a["a2_wq"], a["a2_wkv"] = i["L2_xattn_Wq"].T, i["L2_xattn_Wkv"].T
    a["b2_wqkv"] = np.concatenate([i["L2_ffn_Wq"], i["L2_ffn_Wk"], i["L2_ffn_Wv"]], 1)
    a["b2_bqkv"] = rows(np.concatenate([i["L2_ffn_bq"], i["L2_ffn_bk"], i["L2_ffn_bv"]]))
    freq = 1.0 / 10000.0 ** (np.arange(0, DH, 2, dtype=np.float32) / DH)
    angle = np.arange(T, dtype=np.float32)[:, None] * freq.astype(np.float32)[None, :]
    a["b2_rope"] = np.stack([np.cos(angle), np.sin(angle), -np.sin(angle)], 1).astype(np.float32)
    a["b2_norm"] = rows(np.concatenate([i["L2_ffn_qn_w"], i["L2_ffn_kn_w"]])).reshape(T, 2, DH)
    a["b2_ln"] = i["L2_ffn_ln1_w"].reshape(D, 1)
    gate = np.zeros((H16, DH, H16, DH), np.float32)
    for head in range(H16):
        gate[head, :, head, :] = i["L2_ffn_Wg"]
    a["b2_wgate"] = gate.reshape(D, D)
    a["b2_bgate"] = np.tile(i["L2_ffn_bg"], H16).reshape(D, 1)
    a["b2_wo"], a["b2_bo"] = i["L2_ffn_Wo"], rows(i["L2_ffn_bo"])
    a["rank"] = rows(16.0 - np.arange(16, dtype=np.float32))
    a["earlier"] = np.triu(np.ones((T, T), np.float32), 1)

    def hidden_bias(v):
        return v.reshape(v.shape[0], -1, 128).transpose(2, 0, 1)

    def down(v):
        return v.reshape(v.shape[0], -1, 128, D).transpose(2, 0, 1, 3).reshape(128, v.shape[0], -1)
    a["f0_wg"], a["f0_bg"] = i["L0_ffn_gate_w"], rows(i["L0_ffn_gate_b"])
    a["f0_w1"], a["f0_b1"] = i["L0_ffn_w1"].transpose(1, 0, 2), hidden_bias(i["L0_ffn_b1"])
    a["f0_w2"], a["f0_b2"] = down(i["L0_ffn_w2"]), i["L0_ffn_b2"]
    a["f1_wg"], a["f1_bg"] = i["L1_ffn_router_W"], rows(i["L1_ffn_router_b"])

    def with_shared(e, s):
        return np.concatenate([i["L1_ffn_" + e], i["L1_ffn_" + s][None]], 0)
    a["f1_w1"] = with_shared("eW1", "sW1").transpose(1, 0, 2)
    a["f1_b1"] = hidden_bias(with_shared("eb1", "sb1"))
    a["f1_w2"], a["f1_b2"] = down(with_shared("eW2", "sW2")), with_shared("eb2", "sb2")
    a["f2_ln"] = i["L2_ffn_ln2_w"].reshape(D, 1)
    a["f2_wg"], a["f2_bg"] = i["L2_ffn_Wr"], rows(i["L2_ffn_br"])
    order = [0, 2, 1, 3]
    a["f2_w1"] = i["L2_ffn_W1"].reshape(8, D, 4, 128)[:, :, order].reshape(8, D, 512).transpose(1, 0, 2)
    a["f2_b1"] = hidden_bias(i["L2_ffn_b1"])
    a["f2_w2"], a["f2_b2"] = down(i["L2_ffn_W2"]), i["L2_ffn_b2"]
    a["f3_wg"] = i["L3_ffn_wg"]
    a["f3_w2"], a["f3_b2"] = i["L3_ffn_W"].transpose(2, 0, 1), i["L3_ffn_b"]
    return a


def kernel(**inputs):
    import concourse.bacc as bacc
    from concourse.bass_utils import run_bass_kernel_spmd as run

    nc = bacc.Bacc("TRN2", target_bir_lowering=False, num_devices=1)
    laid = layout({k: np.asarray(v) for k, v in inputs.items()})
    arrays, aps = {}, {}
    for name, v in laid.items():
        v = np.ascontiguousarray(v)
        arrays["in_" + name] = v
        aps[name] = nc.dram_tensor("in_" + name, v.shape, mybir.dt.from_np(v.dtype), kind="ExternalInput").ap()
    out = nc.dram_tensor("out", (B, T, D), F32, kind="ExternalOutput").ap()
    build(nc, aps, out)
    r = run(nc, [arrays], core_ids=[0])
    return r.results[0]["out"]
```

```python
from contextlib import ExitStack

import numpy as np

import concourse.bass as bass
from concourse import mybir

F32 = mybir.dt.float32
F32R = mybir.dt.float32r
U8 = mybir.dt.uint8
ALU = mybir.AluOpType
ACT = mybir.ActivationFunctionType
AXX = mybir.AxisListType.X

B, T, D, C = 32, 128, 128, 96
RING = 4
GROUPS = B // RING
EPS = 1e-5
RMS_EPS = 1e-6
BIG = 1e30
H16, DH = 16, 8


class Item:

    def __init__(self, group, slot):
        self.g, self.s = group, slot
        self.n = group * RING + slot


def counted_from(before):
    def at(sem, value):
        return value + before.get(sem.name, 0)
    return at


def due(value):
    return not isinstance(value, int) or value > 0


def following(it, n):
    return min(it.n + n, B) if isinstance(it.n, int) else it.n + n


def ticks(eng, last, peel=2):
    def tick(group, j, edge):
        def item(lag):
            it = Item(group + (j - lag) // RING, (j - lag) % RING)
            return it if not edge or 0 <= it.n < B else None
        return item

    for t in range(peel * RING):
        yield tick(t // RING, t % RING, True)
    with eng.Fori(peel, GROUPS, 1) as group:
        for j in range(RING):
            yield tick(group, j, False)
    for t in range(B, B + last):
        yield tick(t // RING, t % RING, True)


def build(nc, a, out, upto="f3"):
    ctx = ExitStack()
    with ctx:
        def sb(name, shape, dt=F32):
            return ctx.enter_context(nc.sbuf_tensor(name, shape, dt))

        sems = {}

        def sem(name):
            if name not in sems:
                sems[name] = ctx.enter_context(nc.semaphore(name))
            return sems[name]

        reached = {}

        def totals(**counts):
            for name, count in counts.items():
                reached[name] = reached.get(name, 0) + count

        X = sb("X", [T, GROUPS, RING, D])
        Y = sb("Y", [T, GROUPS, RING, D])
        ident = sb("ident", [128, 128])
        ident_r = sb("ident_r", [128, 128], F32R)
        w = {}
        loads = []

        def weight(phase, name, shape, place=None):
            w[name] = sb("w_" + name, shape)[:] if place is None else place
            loads.append((phase, w[name], a[name]))

        jmask = sb("jmask", [D, 4])
        loads.append(("a0", ident[:], a["ident"]))
        loads.append(("a0", jmask[:], a["jmask"]))
        weight("a0", "a0_wq", [D, D])
        weight("a0", "a0_wkv", [C, 2 * D])
        weight("a0", "a0_bqk", [T, 2 * D])
        weight("a0", "a0_bv", [T, D])
        weight("a0", "a0_wo", [D, D])
        weight("a0", "a0_bo", [T, D])

        weight("a1", "a1_wq", [D, D])
        weight("a1", "a1_wk", [C, D])
        weight("a1", "a1_wv", [C, D])
        weight("a1", "a1_bq", [D, 1])
        weight("a1", "a1_bk", [D, 1])
        weight("a1", "a1_bv", [T, D])
        weight("a3", "a3_wq", [D, 512])
        weight("a3", "a3_wk", [C, 512])
        weight("a3", "a3_wv", [C, 512])
        weight("a3", "a3_wo", [128, 4, D])
        weight("a3", "a3_bo", [T, D])
        weight("a2", "a2_wq", [D, D])
        weight("a2", "a2_wkv", [C, 2 * D])
        weight("b2", "b2_wqkv", [D, 192])
        weight("b2", "b2_bqkv", [T, 192])
        weight("b2", "b2_rope", [T, 3, DH // 2])
        weight("b2", "b2_norm", [T, 2, DH])
        weight("b2", "b2_ln", [D, 1])
        weight("b2", "b2_wgate", [D, D])
        weight("a0", "b2_bgate", [D, 1])
        weight("b2", "b2_wo", [D, D])
        weight("b2", "b2_bo", [T, D])
        keep_words = sb("keep_words", [T, B // 4], mybir.dt.int32)
        loads.append(("a0", keep_words[:], a["keep"]))
        causal_in = sb("causal_in", [T, 2, T])
        loads.append(("a0", causal_in[:], a["causal"]))
        weight("f0", "f0_wg", [D, 8])
        weight("f0", "f0_bg", [T, 8])
        weight("f0", "f0_w1", [D, 8, 512])
        weight("f0", "f0_b1", [128, 8, 4])
        weight("f0", "f0_w2", [128, 8, 512])
        weight("f0", "f0_b2", [8, D])
        weight("f1", "f1_wg", [D, 15])
        weight("f1", "f1_bg", [T, 15])
        weight("f1", "f1_w1", [D, 16, 128])
        weight("f1", "f1_b1", [128, 16, 1])
        weight("f1", "f1_w2", [128, 16, 128])
        weight("f1", "f1_b2", [16, D])
        weight("f2", "f2_ln", [D, 1])
        weight("f2", "f2_wg", [D, 8])
        weight("f2", "f2_bg", [T, 8])
        weight("f2", "f2_w1", [D, 8, 512], w["f0_w1"])
        weight("f2", "f2_b1", [128, 8, 4])
        weight("f2", "f2_w2", [128, 8, 256], w["f0_w2"][:, 0:4, :].rearrange("p a (b n) -> p (a b) n", b=2))
        weight("f2", "f2_b2", [8, D])
        weight("f3", "f3_wg", [D, 8])
        weight("f3", "f3_w2", [D, 8, 128], w["f1_w1"][:, 0:8, :])
        weight("f3", "f3_b2", [8, D])
        rank = sb("rank", [T, 16])
        earlier = sb("earlier", [T, T])
        loads.append(("a0", rank[:], a["rank"]))
        loads.append(("a0", earlier[:], a["earlier"]))
        ones = sb("ones", [T, T])
        ones_r = sb("ones_r", [T, T], F32R)
        hT4 = sb("hT4", [D, 2, RING * T])
        sg = sb("sg", [128, 2, RING * T])
        lg, sel, tmp, pr = (sb(n, [T, RING, 16]) for n in ("lg", "sel", "tmp", "pr"))
        wt = sb("wt", [T, 2, RING, 16])
        rmax, rsum = sb("rmax", [T, RING]), sb("rsum", [T, RING])
        run = sb("run", [T, RING + 1, 8])
        wT = sb("wT", [16, RING * T])
        ve2 = sb("ve2", [T, RING, 1])
        scratch = sb("scratch", [T, 1])

        ctxT = sb("ctxT", [C, RING, T])
        bn = sb("bn", [T, RING, 6])
        mv = sb("mv", [T, RING, 2])
        ve = sb("ve", [T, RING, 1])
        rstd = sb("rstd", [T, RING, 1])
        neg_half = sb("neg_half", [T, 32])
        eps_t = sb("eps_t", [T, 2])
        zeros = sb("zeros", [T, H16])
        h = sb("h", [T, RING, D])
        hT = sb("hT", [D, RING, T])
        qk = sb("qk", [T, 2, 2, H16, DH])
        parts = sb("parts", [T, RING, 2, H16, 4, DH], F32R)
        vx = sb("vx", [T, RING, 4 * 136])
        ones_x = sb("ones_x", [T, 4, 4, DH])
        qT = sb("qT", [D, RING, T], F32R)
        kx = sb("kx", [D, 2, 4, T], F32R)
        kS = sb("kS", [128, 2, 4, T], F32R)
        qS = sb("qS", [128, 2, 4, 4, T], F32R)
        mx = sb("mx", [T, RING, H16])
        P = sb("P", [T, 2, H16, T])
        rec = sb("rec", [D, T])
        gt = P[:].rearrange("p b h t -> p (b h t)").rearrange("p (n t) -> p n t", t=RING * T)
        oT = sb("oT", [D, RING, T])
        ogT = sb("ogT", [D, RING, T])
        eg = sb("eg", [D, 3, T])
        neg_bgate = sb("neg_bgate", [D, 1])
        causal_q, causal_k = sb("causal_q", [T, 4 * T], F32R), sb("causal_k", [T, 4 * T], F32R)
        qkv = sb("qkv", [T, 192])
        ra, rb = sb("ra", [T, H16 + 4, DH]), sb("rb", [T, H16 + 4, DH])
        rsq, rrs = sb("rsq", [T, H16 + 4]), sb("rrs", [T, H16 + 4])
        bn2, mv2, ms2 = sb("bn2", [T, RING, 6]), sb("mv2", [T, RING, 2]), sb("ms2", [T, RING, 1])
        ve3, rstd2 = sb("ve3", [T, RING, 1]), sb("rstd2", [T, RING, 1])
        keep = sb("keep", [T, GROUPS, RING])

        PS = ctx.enter_context(nc.psum_tensor("PS", [128, 8, 512], F32))
        S_ps, ST_ps = PS[:, 0:2, :], PS[:, 2:4, :]
        TP = [PS[:, 4, :], PS[:, 5, :]]
        FR, OB = PS[:, 6, :], PS[:, 7, :]

        x_dram = a["x"].rearrange("(g s) t d -> t g s d", s=RING)
        out_dram = out.rearrange("(g s) t d -> t g s d", s=RING)
        ctx_dram = a["ctxT"].rearrange("(g s) c t -> c g s t", s=RING)

        consts_ready = sem("consts_ready")
        N_CONSTS = 14
        ones_ready = sem("ones_ready")

        def stat_stages(at):
            s_st, s_rs, s_h = sem("stats"), sem("rstd"), sem("h")
            s_bn, s_ve, s_hps = sem("bn"), sem("ve"), sem("hps")

            def stats(v, it):
                if due(it.n - RING + 1):
                    v.wait_ge(s_h, at(s_h, it.n - RING + 1))
                v.bn_stats(bn[:, it.s, :], X[:, it.g, it.s, :]).then_inc(s_bn, 1)

            def aggregate(v, it):
                if isinstance(it.n, int):
                    v.wait_ge(s_bn, at(s_bn, it.n + 1))
                v.bn_aggr(mv[:, it.s, :], bn[:, it.s, :]).then_inc(s_st, 1)

            def rsqrt(q, it):
                q.wait_ge(s_st, at(s_st, it.n + 1))
                q.tensor_tensor(ve[:, it.s, :], mv[:, it.s, 1:2], eps_t[:, 0:1], ALU.add).then_inc(s_ve, 1)
                q.wait_ge(s_ve, at(s_ve, it.n + 1))
                q.tensor_tensor(rstd[:, it.s, :], ve[:, it.s, :], neg_half[:, 0:1], ALU.pow).then_inc(s_rs, 1)

            def norm(v, it, dst):
                if due(it.n - RING + 1):
                    v.wait_ge(s_hps, at(s_hps, it.n - RING + 1))
                v.wait_ge(s_bn, at(s_bn, following(it, 2)))
                v.wait_ge(s_rs, at(s_rs, it.n + 1))
                v.tensor_scalar(dst, X[:, it.g, it.s, :], mv[:, it.s, 0:1], rstd[:, it.s, :],
                                ALU.subtract, ALU.mult).then_inc(s_h, 1)
            return stats, aggregate, rsqrt, norm, s_h

        def attention16(p, before, kind):
            at = counted_from(dict(reached))
            has_bias, masked, causal = kind == "cross", kind == "masked", kind == "self"
            projected = not masked
            n_heads = H16 + 4
            F = 2 if causal else 1
            L = 4 if causal else 2
            peel = 3 if causal else 2
            def own(*names):
                return [sem(n) if causal else None for n in names]
            s_ctx = None if causal else [sem(f"ctx{i}") for i in range(RING)]
            s_hps, s_hT = sem("hps"), sem("hT")
            s_qkv, s_qkf, s_v = sem("qkv"), sem("qkf"), sem("v")
            s_hi, s_lo = sem("hi"), sem("lo")
            s_pad = sem("pad")
            s_turn, s_kx, s_qT = sem("turn"), sem("kx"), sem("qT")
            s_tk, s_kS, s_tq, s_qSv, s_qSa = (sem(n) for n in ("tk", "kS", "tq", "qSv", "qSa"))
            s_s, s_mx, s_nm = sem("s"), sem("mx"), sem("nm")
            s_st, s_exp = sem("st"), sem("exp")
            s_av, s_rec, s_o = sem("av"), sem("rec"), sem("o")
            s_out, s_xb, s_done = sem("out"), sem("xb"), sem("done")
            stats, aggregate, rsqrt, norm, s_h = stat_stages(at)
            s_added = sem("yd") if causal else s_done
            s_fr = sem("fr_read") if causal else s_v
            s_y, s_bn2, s_st2, s_ms, s_rs2 = own("h", "bn2", "st2", "ms", "rs2")
            s_rope, s_sum, s_rs3, s_gate, s_eg, s_gt = own("rope", "sum", "rs3", "gate", "eg", "gt")
            s_yb, s_yd, s_gt2, s_ve3 = own("yb", "yd", "gt2", "ve3")
            s_bn, s_rs = sem("bn"), sem("rstd")
            if causal:
                s_h = sem("h2")

            def sync(e):
                if causal:
                    return
                before(e)
                for s in range(RING):
                    e.dma_start(ctxT[:, s, :], ctx_dram[:, 0, s, :]).then_inc(s_ctx[s], 16)
                with e.Fori(1, GROUPS, 1) as g:
                    for s in range(RING):
                        e.wait_ge(s_qkv, at(s_qkv, (g - 1) * RING + s + 1))
                        e.dma_start(ctxT[:, s, :], ctx_dram[:, g, s, :]).then_inc(s_ctx[s], 16)

            def pe_hT(e, it):
                e.wait_ge(s_h, at(s_h, it.n + 1))
                before_it = it.n - (L - F) + 1
                if due(before_it):
                    e.wait_ge(s_kx, at(s_kx, before_it))
                    e.wait_ge(s_qT, at(s_qT, before_it))
                e.transpose(FR[:, 0:T], h[:, it.s, :], ident[:, :]).then_inc(s_hps, 1)

            def pe_qkv(e, it):
                e.wait_ge(s_hT, at(s_hT, it.n + 1))
                if causal:
                    m = e.matmul(FR[:, 0:192], hT[:, it.s, :], w[p + "wqkv"][:, :], start=True, stop=True)
                else:
                    e.wait_ge(s_ctx[it.s], at(s_ctx[it.s], 16 * (it.g + 1)))
                    e.matmul(FR[:, 0:D], hT[:, it.s, :], w[p + "wq"][:, :], start=True, stop=True)
                    m = e.matmul(FR[:, D:3 * D], ctxT[:, it.s, :], w[p + "wkv"][:, :], start=True, stop=True)
                m.then_inc(s_qkv, 1)

            def pe_turn(e, it):
                e.wait_ge(s_fr, at(s_fr, following(it, L - F)))
                e.wait_ge(s_qkf, at(s_qkf, (2 if causal else 1) * (it.n + 1)))
                for which in range(2):
                    m = e.transpose(FR[:, which * T:(which + 1) * T],
                                    qk[:, it.s % 2, which, :, :].rearrange("p h d -> p (h d)"), ident[:, :])
                m.then_inc(s_turn, 1)

            def turn_stack(e, it, which, done):
                for g in range(4):
                    m = e.matmul(TP[which][:, g * T:(g + 1) * T],
                                 parts[:, it.s, which, 4 * g:4 * g + 4, :, :].rearrange("p h c d -> p (h c d)"),
                                 ident_r[:, :], start=True, stop=True)
                m.then_inc(done, 1)

            def pe_stack_k(e, it):
                e.wait_ge(s_lo, at(s_lo, 2 * it.n + 2))
                if due(it.n):
                    e.wait_ge(s_kS, at(s_kS, it.n))
                turn_stack(e, it, 1, s_tk)

            def pe_stack_q(e, it):
                e.wait_ge(s_nm, at(s_nm, 2 * it.n + 2))
                if due(it.n):
                    e.wait_ge(s_qSv, at(s_qSv, it.n))
                if due(it.n):
                    e.wait_ge(s_qSa, at(s_qSa, it.n))
                turn_stack(e, it, 0, s_tq)

            def pe_scores(e, it, half):
                if half == 0:
                    e.wait_ge(s_qT, at(s_qT, it.n + 1))
                    e.wait_ge(s_kx, at(s_kx, it.n + 1))
                if due(2 * it.n + half):
                    e.wait_ge(s_mx, at(s_mx, 2 * it.n + half))
                if causal:
                    for i in range(2):
                        e.matmul(S_ps[:, i, :], ident_r[:, :], causal_q[:, :], start=True, stop=False)
                for i in range(2):
                    r = 32 * (2 * half + i)
                    m = e.matmul(S_ps[:, i, :], qT[r:r + 32, it.s, :],
                                 kx[r:r + 32, it.s % 2, :, :].rearrange("p j t -> p (j t)"),
                                 start=not causal, stop=True)
                m.then_inc(s_s, 1)

            def pe_scoresT(e, it, half):
                if half == 0:
                    e.wait_ge(s_kS, at(s_kS, it.n + 1))
                    e.wait_ge(s_qSv, at(s_qSv, it.n + 1))
                    e.wait_ge(s_qSa, at(s_qSa, it.n + 1))
                if due(2 * it.n + half):
                    e.wait_ge(s_exp, at(s_exp, 2 * it.n + half))
                for i in range(2):
                    g = 2 * half + i
                    if causal:
                        e.matmul(ST_ps[:, i, :], ident_r[:, :], causal_k[:, :], start=True, stop=False)
                    m = e.matmul(ST_ps[:, i, :], kS[:, it.s % 2, g, :],
                                 qS[:, it.s % 2, g, :, :].rearrange("p j t -> p (j t)"),
                                 start=not causal, stop=True)
                m.then_inc(s_st, 1)

            def pe_values(e, it, what):
                if what == 0:
                    e.wait_ge(s_exp, at(s_exp, 2 * it.n + 2))
                    e.wait_ge(s_v, at(s_v, it.n + 1))
                    if due(it.n):
                        e.wait_ge(s_added, at(s_added, it.n))
                for j in range(4):
                    for g in range(4):
                        lhs = vx[:, it.s, 128 * j + 32 * g:128 * j + 32 * g + 32] if what == 0 else \
                            ones_x[:, j, :, :].rearrange("p a d -> p (a d)")
                        m = e.matmul(OB[32 * g:32 * g + 32, what * T:(what + 1) * T], lhs,
                                     P[:, it.s % 2, 4 * g + j, :], start=(j == 0), stop=(j == 3))
                if what == 1:
                    m.then_inc(s_av, 1)

            def pe_gate(e, it):
                e.wait_ge(s_o, at(s_o, it.n + 1))
                e.matmul(OB[:, 0:T], w[p + "wgate"][:, :], oT[:, it.s, :], start=True, stop=True).then_inc(s_gate, 1)

            def pe_out(e, it):
                e.wait_ge(s_gt if causal else s_o, at(s_gt if causal else s_o, it.n + 1))
                if causal:
                    m = e.matmul(OB[:, 0:D], ogT[:, it.s, :], w[p + "wo"][:, :], start=True, stop=True)
                elif projected:
                    m = e.matmul(OB[:, 0:D], oT[:, it.s, :], w[p + "wo"][:, :], start=True, stop=True)
                else:
                    m = e.transpose(OB[:, 0:D], oT[:, it.s, :], ident[:, :])
                m.then_inc(s_out, 1)

            def tensor(e):
                before(e)
                e.wait_ge(s_pad, at(s_pad, 3))
                e.wait_ge(sem(p + "weights"), 16 * n_loads[p[:2]])
                e.wait_ge(consts_ready, N_CONSTS)
                for item in ticks(e, L + 3, peel):
                    if it := item(L + 3):
                        pe_out(e, it)
                    if it := item(L + 1):
                        pe_stack_q(e, it)
                    if it := item(L):
                        pe_turn(e, it)
                        pe_stack_k(e, it)
                    if it := item(L + 2):
                        pe_values(e, it, 0)
                    if it := item(L):
                        pe_scores(e, it, 0)
                    if it := item(L + 1):
                        pe_scoresT(e, it, 0)
                    if it := item(F):
                        pe_hT(e, it)
                    if it := item(L + 2):
                        pe_values(e, it, 1)
                    if it := item(F):
                        pe_qkv(e, it)
                    if it := item(L):
                        pe_scores(e, it, 1)
                    if it := item(L + 1):
                        pe_scoresT(e, it, 1)
                    if causal and (it := item(L + 2)):
                        pe_gate(e, it)

            def v_qkv(e, it):
                if due(2 * (it.n - 1)):
                    e.wait_ge(s_lo, at(s_lo, 2 * (it.n - 1)))
                if due(it.n - 1):
                    e.wait_ge(s_turn, at(s_turn, it.n - 1))
                e.wait_ge(s_qkv, at(s_qkv, it.n + 1))
                src = FR[:, 0:2 * D]
                dst = qk[:, it.s % 2].rearrange("p a h d -> p (a h d)")
                if has_bias:
                    e.tensor_tensor(dst, src, w[p + "bqk"][:, :], ALU.add).then_inc(s_qkf, 1)
                if masked:
                    e.tensor_scalar(qk[:, it.s % 2, 0].rearrange("p h d -> p (h d)"), FR[:, 0:D],
                                    keep[:, it.g, it.s:it.s + 1], None, ALU.mult)
                    e.tensor_copy(qk[:, it.s % 2, 1].rearrange("p h d -> p (h d)"), FR[:, D:2 * D])\
                     .then_inc(s_qkf, 1)
                if due(it.n - RING + 1):
                    e.wait_ge(s_av, at(s_av, it.n - RING + 1))
                vsrc = FR[:, 2 * D:3 * D].rearrange("p (g j d) -> p j g d", g=4, j=4)
                vdst = vx[:, it.s, :].rearrange("p (j n) -> p j n", j=4)[:, :, 0:128]\
                    .rearrange("p j (g n) -> p j g n", g=4)[:, :, :, 0:DH]
                if has_bias:
                    e.tensor_tensor(vdst, vsrc, w[p + "bv"][:, :].rearrange("p (g j d) -> p j g d", g=4, j=4),
                                    ALU.add).then_inc(s_v, 1)
                if masked:
                    e.tensor_copy(vdst, vsrc).then_inc(s_v, 1)

            def v_rotate(e, it):
                n = [0]

                def step(m):
                    n[0] += 1
                    m.then_inc(s_rope, 1)
                    e.wait_ge(s_rope, at(s_rope, 5 * it.n + n[0]))
                e.wait_ge(s_qkv, at(s_qkv, it.n + 1))
                if due(it.n):
                    e.wait_ge(s_qkf, at(s_qkf, 2 * it.n))
                    e.wait_ge(s_v, at(s_v, it.n))
                e.tensor_tensor(qkv[:, :], FR[:, 0:192], w[p + "bqkv"][:, :], ALU.add).then_inc(s_fr, 1)
                e.wait_ge(s_fr, at(s_fr, it.n + 1))
                x = qkv[:, 0:160].rearrange("p (h d) -> p h d", d=DH)
                cos, sin, neg_sin = (w[p + "rope"][:, i, :].unsqueeze(1).broadcast_to([T, n_heads, DH // 2])
                                     for i in range(3))
                low, high = x[:, :, 0:4], x[:, :, 4:8]
                e.tensor_tensor(ra[:, :, 0:4], low, cos, ALU.mult)
                e.tensor_tensor(ra[:, :, 4:8], high, cos, ALU.mult)
                e.tensor_tensor(rb[:, :, 0:4], high, neg_sin, ALU.mult)
                step(e.tensor_tensor(rb[:, :, 4:8], low, sin, ALU.mult))
                step(e.tensor_tensor(ra[:, :, :], ra[:, :, :], rb[:, :, :], ALU.add))
                step(e.tensor_tensor(rb[:, :, :], ra[:, :, :], ra[:, :, :], ALU.mult))
                step(e.tensor_reduce(rsq[:, :], rb[:, :, :], AXX, ALU.add))
                e.tensor_scalar(rsq[:, :], rsq[:, :], 1.0 / DH, RMS_EPS, ALU.mult, ALU.add).then_inc(s_sum, 1)

            def v_qk_norm(e, it):
                if due(it.n - RING + 1):
                    e.wait_ge(s_av, at(s_av, it.n - RING + 1))
                vdst = vx[:, it.s, :].rearrange("p (j n) -> p j n", j=4)[:, :, 0:128]\
                    .rearrange("p j (g n) -> p j g n", g=4)[:, :, :, 0:DH]
                e.tensor_copy(vdst, qkv[:, 160:192].rearrange("p (g d) -> p g d", g=4).unsqueeze(1)
                              .broadcast_to([T, 4, 4, DH])).then_inc(s_v, 1)
                e.wait_ge(s_rs3, at(s_rs3, it.n + 1))
                e.tensor_tensor(ra[:, :, :], ra[:, :, :], rrs[:, :].unsqueeze(2).broadcast_to([T, n_heads, DH]),
                                ALU.mult).then_inc(s_rope, 1)
                e.wait_ge(s_rope, at(s_rope, 5 * it.n + 5))
                if due(2 * (it.n - 1)):
                    e.wait_ge(s_lo, at(s_lo, 2 * (it.n - 1)))
                if due(it.n - 1):
                    e.wait_ge(s_turn, at(s_turn, it.n - 1))
                e.tensor_tensor(qk[:, it.s % 2, 0], ra[:, 0:H16, :],
                                w[p + "norm"][:, 0, :].unsqueeze(1).broadcast_to([T, H16, DH]), ALU.mult)\
                 .then_inc(s_qkf, 1)
                e.tensor_tensor(qk[:, it.s % 2, 1].rearrange("p (g j) d -> p g j d", g=4),
                                ra[:, H16:n_heads, :].unsqueeze(2).broadcast_to([T, 4, 4, DH]),
                                w[p + "norm"][:, 1, :].unsqueeze(1).unsqueeze(1).broadcast_to([T, 4, 4, DH]),
                                ALU.mult).then_inc(s_qkf, 1)

            def v_y(e, it):
                e.wait_ge(s_bn, at(s_bn, following(it, 2)))
                e.wait_ge(s_rs, at(s_rs, it.n + 1))
                e.tensor_scalar(Y[:, it.g, it.s, :], X[:, it.g, it.s, :], mv[:, it.s, 0:1], rstd[:, it.s, :],
                                ALU.subtract, ALU.mult).then_inc(s_y, 1)

            def v_y_stats(e, it):
                e.wait_ge(s_y, at(s_y, it.n + 1))
                e.tensor_copy(scratch[:, 0:1], neg_half[:, 0:1])
                e.bn_stats(bn2[:, it.s, :], Y[:, it.g, it.s, :]).then_inc(s_bn2, 1)
                e.wait_ge(s_bn2, at(s_bn2, it.n + 1))
                e.tensor_copy(scratch[:, 0:1], neg_half[:, 0:1])
                e.bn_aggr(mv2[:, it.s, :], bn2[:, it.s, :]).then_inc(s_st2, 1)
                e.wait_ge(s_st2, at(s_st2, it.n + 1))
                e.scalar_tensor_tensor(out=ms2[:, it.s, :], in0=mv2[:, it.s, 0:1], scalar=mv2[:, it.s, 0:1],
                                       in1=mv2[:, it.s, 1:2], op0=ALU.mult, op1=ALU.add).then_inc(s_ms, 1)

            def v_h2(e, it):
                if due(it.n - RING + 1):
                    e.wait_ge(s_hps, at(s_hps, it.n - RING + 1))
                e.wait_ge(s_rs2, at(s_rs2, it.n + 1))
                e.tensor_scalar(h[:, it.s, :], Y[:, it.g, it.s, :], rstd2[:, it.s, :], None, ALU.mult)\
                 .then_inc(s_h, 1)

            def v_gate(e, it):
                e.wait_ge(s_eg, at(s_eg, it.n + 1))
                e.tensor_scalar(eg[:, 1, :], eg[:, 0, :], 1.0, None, ALU.add).then_inc(s_gt2, 1)
                e.wait_ge(s_gt2, at(s_gt2, 2 * it.n + 1))
                e.reciprocal(eg[:, 2, :], eg[:, 1, :]).then_inc(s_gt2, 1)
                e.wait_ge(s_gt2, at(s_gt2, 2 * it.n + 2))
                e.tensor_tensor(ogT[:, it.s, :], oT[:, it.s, :], eg[:, 2, :], ALU.mult).then_inc(s_gt, 1)

            def v_residual_self(e, it):
                e.wait_ge(s_yb, at(s_yb, it.n + 1))
                e.wait_ge(s_out, at(s_out, it.n + 1))
                e.tensor_tensor(Y[:, it.g, it.s, :], Y[:, it.g, it.s, :], OB[:, 0:D], ALU.add).then_inc(s_yd, 1)

            def v_high(e, it):
                if due(it.n - RING + 1):
                    e.wait_ge(s_tq, at(s_tq, it.n - RING + 1))
                e.wait_ge(s_qkf, at(s_qkf, (2 if causal else 1) * (it.n + 1)))
                src = qk[:, it.s % 2].rearrange("p a h d -> p (a h) d").unsqueeze(2).broadcast_to([T, 2 * H16, 3, DH])
                dst = parts[:, it.s, :, :, 0:3, :].rearrange("p a h c d -> p (a h) c d")
                e.tensor_copy(dst, src).then_inc(s_hi, 1)

            def v_kx(e, it):
                e.wait_ge(s_turn, at(s_turn, it.n + 1))
                e.tensor_tensor(kx[:, it.s % 2, :, :], FR[:, T:2 * T].unsqueeze(1).broadcast_to([D, 4, T]),
                                jmask[:, :].unsqueeze(2).broadcast_to([D, 4, T]), ALU.mult).then_inc(s_kx, 1)

            def v_qS(e, it):
                if due(2 * (it.n - 1)):
                    e.wait_ge(s_st, at(s_st, 2 * (it.n - 1)))
                e.wait_ge(s_tq, at(s_tq, it.n + 1))
                e.tensor_copy(qS[0:32, it.s % 2, :, 0, :], TP[0][0:32, :].rearrange("p (g t) -> p g t", g=4))\
                 .then_inc(s_qSv, 1)

            def v_max(e, it, half):
                e.wait_ge(s_s, at(s_s, 2 * it.n + half + 1))
                e.tensor_reduce(mx[:, it.s, 8 * half:8 * half + 8],
                                S_ps[:, :, :].rearrange("p i (j t) -> p (i j) t", t=T), AXX, ALU.max)\
                 .then_inc(s_mx, 1)

            def v_negmax(e, it, half):
                e.wait_ge(s_mx, at(s_mx, 2 * it.n + half + 1))
                dst = parts[:, it.s, 0, 8 * half:8 * half + 8, 3, 0:1]
                e.tensor_scalar(dst, mx[:, it.s, 8 * half:8 * half + 8].unsqueeze(2), -1.0, None, ALU.mult)\
                 .then_inc(s_nm, 1)

            def v_heads(e, it):
                if due(it.n):
                    e.wait_ge(s_o, at(s_o, it.n))
                e.wait_ge(s_av, at(s_av, it.n + 1))
                e.reciprocal(rec[:, :], OB[:, T:2 * T]).then_inc(s_rec, 1)
                if due(it.n - RING + 1):
                    e.wait_ge(s_out, at(s_out, it.n - RING + 1))
                e.wait_ge(s_rec, at(s_rec, it.n + 1))
                e.tensor_tensor(oT[:, it.s, :], OB[:, 0:T], rec[:, :], ALU.mult).then_inc(s_o, 1)

            def v_residual(e, it):
                if projected:
                    e.wait_ge(s_xb, at(s_xb, it.n + 1))
                e.wait_ge(s_out, at(s_out, it.n + 1))
                e.tensor_tensor(X[:, it.g, it.s, :], X[:, it.g, it.s, :], OB[:, 0:D], ALU.add).then_inc(s_done, 1)

            def vector(e):
                before(e)
                e.wait_ge(s_pad, at(s_pad, 3))
                e.wait_ge(sem(p + "weights"), 16 * n_loads[p[:2]])
                for item in ticks(e, L + 3, peel):
                    if it := item(L + 3):
                        (v_residual_self if causal else v_residual)(e, it)
                    if it := item(L + 1):
                        v_qS(e, it)
                    if it := item(L):
                        v_kx(e, it)
                    if causal and (it := item(F)):
                        v_h2(e, it)
                    if it := item(0):
                        stats(e, it)
                    if it := item(1):
                        v_y(e, it) if causal else norm(e, it, h[:, it.s, :])
                    if it := item(0):
                        aggregate(e, it)
                    if causal and (it := item(1)):
                        v_y_stats(e, it)
                    if it := item(L):
                        v_max(e, it, 0)
                        v_negmax(e, it, 0)
                    if causal and (it := item(F + 1)):
                        v_qk_norm(e, it)
                    if it := item(L + 2):
                        v_heads(e, it)
                    if causal and (it := item(F + 1)):
                        v_high(e, it)
                    if causal and (it := item(F)):
                        v_rotate(e, it)
                    if causal and (it := item(L + 2)):
                        v_gate(e, it)
                    if not causal and (it := item(F)):
                        v_qkv(e, it)
                    if it := item(L):
                        v_max(e, it, 1)
                    if not causal and (it := item(F)):
                        v_high(e, it)
                    if it := item(L):
                        v_negmax(e, it, 1)

            def g_low(e, it):
                e.wait_ge(s_hi, at(s_hi, it.n + 1))
                for which, place in ((0, 2), (1, 1)):
                    e.tensor_tensor(parts[:, it.s, which, :, place, :], qk[:, it.s % 2, which, :, :],
                                    parts[:, it.s, which, :, 0, :].bitcast(F32), ALU.subtract).then_inc(s_lo, 1)

            def g_rsqrt2(e, it):
                e.wait_ge(s_ms, at(s_ms, it.n + 1))
                e.tensor_tensor(ve3[:, it.s, :], ms2[:, it.s, :], eps_t[:, 1:2], ALU.add).then_inc(s_ve3, 1)
                e.wait_ge(s_ve3, at(s_ve3, it.n + 1))
                e.tensor_tensor(rstd2[:, it.s, :], ve3[:, it.s, :], neg_half[:, 0:1], ALU.pow).then_inc(s_rs2, 1)

            def g_rsqrt3(e, it):
                e.wait_ge(s_sum, at(s_sum, it.n + 1))
                e.tensor_tensor(rrs[:, :], rsq[:, :], neg_half[:, 0:H16 + 4], ALU.pow).then_inc(s_rs3, 1)

            def g_rsqrt3(e, it):
                e.wait_ge(s_sum, at(s_sum, it.n + 1))
                e.tensor_tensor(rrs[:, :], rsq[:, :], neg_half[:, 0:n_heads], ALU.pow).then_inc(s_rs3, 1)

            def g_bias_y(e, it):
                e.wait_ge(s_h, at(s_h, it.n + 1))
                e.tensor_tensor(Y[:, it.g, it.s, :], Y[:, it.g, it.s, :], w[p + "bo"][:, :], ALU.add)\
                 .then_inc(s_yb, 1)

            def g_add_y(e, it):
                e.wait_ge(s_yd, at(s_yd, it.n + 1))
                e.tensor_tensor(X[:, it.g, it.s, :], X[:, it.g, it.s, :], Y[:, it.g, it.s, :], ALU.add)\
                 .then_inc(s_done, 1)

            def g_bias(e, it):
                e.wait_ge(s_h, at(s_h, it.n + 1))
                e.tensor_tensor(X[:, it.g, it.s, :], X[:, it.g, it.s, :], w[p + "bo"][:, :], ALU.add)\
                 .then_inc(s_xb, 1)

            def pool(e):
                before(e)
                e.memset(parts[:].bitcast(F32), 0.0).then_inc(s_pad, 1)
                e.memset(qS[:].bitcast(F32), 0.0).then_inc(s_pad, 1)
                e.wait_ge(s_pad, at(s_pad, 1))
                e.memset(parts[:, :, 1, :, 3, 0:1].rearrange("p r h o -> p r (h o)").bitcast(F32), 1.0)\
                 .then_inc(s_pad, 1)
                e.wait_ge(s_pad, at(s_pad, 3))
                e.wait_ge(sem(p + "weights"), 16 * n_loads[p[:2]])
                if causal:
                    for item in ticks(e, L + 3, peel):
                        if it := item(0):
                            rsqrt(e, it)
                        if it := item(1):
                            g_rsqrt2(e, it)
                        if it := item(L + 3):
                            g_add_y(e, it)
                        if it := item(F + 1):
                            g_low(e, it)
                        if it := item(F):
                            g_bias_y(e, it)
                            g_rsqrt3(e, it)
                    return
                for item in ticks(e, 1):
                    if projected and (it := item(1)):
                        g_bias(e, it)
                    if it := item(0):
                        rsqrt(e, it)
                    if it := item(1):
                        g_low(e, it)

            def a_qT(e, it):
                e.wait_ge(s_kx, at(s_kx, it.n + 1))
                e.copy(qT[:, it.s, :], FR[:, 0:T]).then_inc(s_qT, 1)

            def a_kS(e, it):
                e.wait_ge(s_tk, at(s_tk, it.n + 1))
                e.copy(kS[:, it.s % 2].rearrange("p g t -> p (g t)"), TP[1]).then_inc(s_kS, 1)

            def a_qS(e, it):
                e.wait_ge(s_qSv, at(s_qSv, it.n + 1))
                for j in range(1, 4):
                    r = slice(32 * j, 32 * j + 32)
                    m = e.copy(qS[r, it.s % 2, :, j, :], TP[0][r, :].rearrange("p (g t) -> p g t", g=4))
                m.then_inc(s_qSa, 1)

            def a_hT(e, it):
                if due(it.n - RING + 1):
                    e.wait_ge(s_qkv, at(s_qkv, it.n - RING + 1))
                e.wait_ge(s_hps, at(s_hps, it.n + 1))
                if causal:
                    e.activation(hT[:, it.s, :], FR[:, 0:T], ACT.Identity, scale=w[p + "ln"][:, 0:1]).then_inc(s_hT, 1)
                else:
                    e.copy(hT[:, it.s, :], FR[:, 0:T]).then_inc(s_hT, 1)

            def a_gate(e, it):
                if due(it.n):
                    e.wait_ge(s_gt, at(s_gt, it.n))
                e.wait_ge(s_gate, at(s_gate, it.n + 1))
                e.activation(eg[:, 0, :], OB[:, 0:T], ACT.Exp, bias=neg_bgate[:, 0:1], scale=-1.0).then_inc(s_eg, 1)

            def a_exp(e, it, half):
                if due(it.n - 1):
                    e.wait_ge(s_av, at(s_av, it.n - 1))
                e.wait_ge(s_st, at(s_st, 2 * it.n + half + 1))
                e.activation(P[:, it.s % 2, 8 * half:8 * half + 8, :].rearrange("p h t -> p (h t)"),
                             ST_ps[:, :, :].rearrange("p j n -> p (j n)"), ACT.Exp,
                             scale=float(DH) ** -0.5).then_inc(s_exp, 1)

            def scalar(e):
                before(e)
                e.wait_ge(s_pad, at(s_pad, 3))
                for item in ticks(e, L + 2, peel):
                    if it := item(L):
                        a_qT(e, it)
                        a_kS(e, it)
                    if it := item(L + 1):
                        a_qS(e, it)
                        a_exp(e, it, 0)
                    if it := item(F):
                        a_hT(e, it)
                    if causal and (it := item(L + 2)):
                        a_gate(e, it)
                    if it := item(L + 1):
                        a_exp(e, it, 1)
            totals(stats=B, rstd=B, h=B, bn=B, ve=B, hps=B, hT=B, qkv=B, qkf=B * (2 if causal else 1), v=B,
                   hi=B, lo=2 * B, turn=B, kx=B, qT=B, tk=B, kS=B, tq=B, qSv=B, qSa=B, s=2 * B, mx=2 * B,
                   nm=2 * B, st=2 * B, exp=2 * B, av=B, rec=B, o=B, out=B, done=B, pad=3)
            if projected and not causal:
                totals(xb=B)
            if causal:
                totals(h2=B, bn2=B, st2=B, ms=B, rs2=B, rope=5 * B, fr_read=B, sum=B, rs3=B, gate=B, eg=B, gt=B, yb=B,
                       yd=B, gt2=2 * B, ve3=B)
            else:
                totals(**{f"ctx{i}": 16 * GROUPS for i in range(RING)})
            return dict(sync=sync, tensor=tensor, vector=vector, gpsimd=pool, scalar=scalar, done=(s_done, reached["done"]))

        def attention1(p, before):
            at = counted_from(dict(reached))
            s_ctx = [sem(f"ctx{i}") for i in range(RING)]
            s_hps, s_hT, s_qkv, s_qk, s_v = (sem(n) for n in ("hps", "hT", "qkv", "qk", "v"))
            s_s, s_mx, s_nb, s_exp, s_pps, s_pT = (sem(n) for n in ("s", "mx", "nb", "exp", "pps", "pT"))
            s_av, s_rec, s_done = (sem(n) for n in ("av", "rec", "done"))
            stats, aggregate, rsqrt, norm, s_h = stat_stages(at)
            pool_f = P[:].rearrange("p b h t -> p (b h t)")
            q1, k1, v1, p1, pT1 = (pool_f[:, 512 * i:512 * i + 512].rearrange("p (r t) -> p r t", r=RING)
                                   for i in range(5))
            scale = float(D) ** -0.5

            def sync(e):
                before(e)
                for s in range(RING):
                    e.dma_start(ctxT[:, s, :], ctx_dram[:, 0, s, :]).then_inc(s_ctx[s], 16)
                with e.Fori(1, GROUPS, 1) as g:
                    for s in range(RING):
                        e.wait_ge(s_qkv, at(s_qkv, (g - 1) * RING + s + 1))
                        e.dma_start(ctxT[:, s, :], ctx_dram[:, g, s, :]).then_inc(s_ctx[s], 16)

            def tensor(e):
                def pe_hT(it):
                    e.wait_ge(s_h, at(s_h, it.n + 1))
                    if due(it.n):
                        e.wait_ge(s_v, at(s_v, it.n))
                    e.transpose(FR[:, 0:T], h[:, it.s, :], ident[:, :]).then_inc(s_hps, 1)

                def pe_qkv(it):
                    e.wait_ge(s_hT, at(s_hT, it.n + 1))
                    e.wait_ge(s_ctx[it.s], at(s_ctx[it.s], 16 * (it.g + 1)))
                    e.matmul(FR[:, 0:T], w[p + "wq"][:, :], hT[:, it.s, :], start=True, stop=True)
                    e.matmul(FR[:, T:2 * T], w[p + "wk"][:, :], ctxT[:, it.s, :], start=True, stop=True)
                    e.matmul(FR[:, 2 * T:3 * T], ctxT[:, it.s, :], w[p + "wv"][:, :], start=True, stop=True)\
                     .then_inc(s_qkv, 1)

                def pe_scores(it):
                    e.wait_ge(s_qk, at(s_qk, 2 * it.n + 2))
                    if due(it.n):
                        e.wait_ge(s_exp, at(s_exp, it.n))
                    e.matmul(PS[:, 0, 0:T], q1[:, it.s, :], k1[:, it.s, :], start=True, stop=True).then_inc(s_s, 1)

                def pe_pT(it):
                    e.wait_ge(s_exp, at(s_exp, it.n + 1))
                    if due(it.n):
                        e.wait_ge(s_pT, at(s_pT, it.n))
                    e.transpose(PS[:, 4, 0:T], p1[:, it.s, :], ident[:, :]).then_inc(s_pps, 1)

                def pe_values(it):
                    e.wait_ge(s_pT, at(s_pT, it.n + 1))
                    if due(it.n):
                        e.wait_ge(s_done, at(s_done, it.n))
                    e.matmul(OB[:, 0:T], pT1[:, it.s, :], v1[:, it.s, :], start=True, stop=True).then_inc(s_av, 1)
                before(e)
                e.wait_ge(sem(p + "weights"), 16 * n_loads[p[:2]])
                e.wait_ge(consts_ready, N_CONSTS)
                for item in ticks(e, 3):
                    if it := item(3):
                        pe_pT(it)
                    if it := item(1):
                        pe_hT(it)
                    if it := item(2):
                        pe_scores(it)
                    if it := item(3):
                        pe_values(it)
                    if it := item(1):
                        pe_qkv(it)

            def vector(e):
                def v_qkv(it):
                    if due(it.n - RING + 1):
                        e.wait_ge(s_done, at(s_done, it.n - RING + 1))
                    e.wait_ge(s_qkv, at(s_qkv, it.n + 1))
                    e.tensor_scalar(q1[:, it.s, :], FR[:, 0:T], w[p + "bq"][:, 0:1], None, ALU.add).then_inc(s_qk, 1)
                    e.tensor_scalar(k1[:, it.s, :], FR[:, T:2 * T], w[p + "bk"][:, 0:1], None, ALU.add)\
                     .then_inc(s_qk, 1)
                    e.tensor_tensor(v1[:, it.s, :], FR[:, 2 * T:3 * T], w[p + "bv"][:, :], ALU.add).then_inc(s_v, 1)

                def v_max(it):
                    e.wait_ge(s_s, at(s_s, it.n + 1))
                    e.tensor_reduce(mx[:, it.s, 0:1], PS[:, 0, 0:T], AXX, ALU.max).then_inc(s_mx, 1)
                    e.wait_ge(s_mx, at(s_mx, it.n + 1))
                    e.tensor_scalar(mx[:, it.s, 1:2], mx[:, it.s, 0:1], -scale, None, ALU.mult).then_inc(s_nb, 1)

                def v_out(it):
                    e.wait_ge(s_av, at(s_av, it.n + 1))
                    e.reciprocal(mx[:, it.s, 3:4], mx[:, it.s, 2:3]).then_inc(s_rec, 1)
                    e.wait_ge(s_rec, at(s_rec, it.n + 1))
                    e.scalar_tensor_tensor(out=X[:, it.g, it.s, :], in0=OB[:, 0:T], scalar=mx[:, it.s, 3:4],
                                           in1=X[:, it.g, it.s, :], op0=ALU.mult, op1=ALU.add).then_inc(s_done, 1)
                before(e)
                e.wait_ge(sem(p + "weights"), 16 * n_loads[p[:2]])
                for item in ticks(e, 3):
                    if it := item(0):
                        stats(e, it)
                    if it := item(1):
                        norm(e, it, h[:, it.s, :])
                    if it := item(0):
                        aggregate(e, it)
                    if it := item(2):
                        v_max(it)
                    if it := item(3):
                        v_out(it)
                    if it := item(1):
                        v_qkv(it)

            def pool(e):
                before(e)
                for item in ticks(e, 0):
                    if it := item(0):
                        rsqrt(e, it)

            def scalar(e):
                def a_hT(it):
                    if due(it.n - RING + 1):
                        e.wait_ge(s_qkv, at(s_qkv, it.n - RING + 1))
                    e.wait_ge(s_hps, at(s_hps, it.n + 1))
                    e.copy(hT[:, it.s, :], FR[:, 0:T]).then_inc(s_hT, 1)

                def a_exp(it):
                    e.wait_ge(s_nb, at(s_nb, it.n + 1))
                    e.activation(p1[:, it.s, :], PS[:, 0, 0:T], ACT.Exp, scale=scale, bias=mx[:, it.s, 1:2],
                                 accum_out=mx[:, it.s, 2:3]).then_inc(s_exp, 1)

                def a_pT(it):
                    e.wait_ge(s_pps, at(s_pps, it.n + 1))
                    e.copy(pT1[:, it.s, :], PS[:, 4, 0:T]).then_inc(s_pT, 1)
                before(e)
                for item in ticks(e, 3):
                    if it := item(3):
                        a_pT(it)
                    if it := item(1):
                        a_hT(it)
                    if it := item(2):
                        a_exp(it)
            totals(stats=B, rstd=B, h=B, bn=B, ve=B, hps=B, hT=B, qkv=B, qk=2 * B, v=B, s=B, mx=B, nb=B,
                   exp=B, pps=B, pT=B, av=B, rec=B, done=B)
            totals(**{f"ctx{i}": 16 * GROUPS for i in range(RING)})
            return dict(sync=sync, tensor=tensor, vector=vector, gpsimd=pool, scalar=scalar, done=(s_done, reached["done"]))

        def attention8(p, before):
            at = counted_from(dict(reached))
            NH, HD = 8, 64
            s_ctx = [sem(f"ctx{i}") for i in range(RING)]
            s_hps, s_hT, s_q, s_k, s_vps, s_v = (sem(n) for n in ("hps", "hT", "q", "k", "vps", "v"))
            s_qH, s_kH, s_qL, s_kL = (sem(n) for n in ("qH", "kH", "qL", "kL"))
            s_s, s_mx, s_nm, s_md, s_st, s_exp = (sem(n) for n in ("s", "mx", "nm", "md", "st", "exp"))
            s_av, s_rec, s_o, s_ops, s_oT = (sem(n) for n in ("av", "rec", "o", "ops", "oT"))
            s_out, s_xb, s_done, s_pad = (sem(n) for n in ("out", "xb", "done", "pad"))
            stats, aggregate, rsqrt, norm, s_h = stat_stages(at)
            flat = P[:].rearrange("p b h t -> p (b h t)")
            P8 = flat[:, 0:2048].rearrange("p (b h t) -> p b h t", b=2, h=NH)
            VW = 584
            v8 = flat[:, 2048:2048 + 2 * VW].rearrange("p (b n) -> p b n", b=2)
            q8 = qS[:].rearrange("p b g j t -> p (b g j t)").rearrange("p (b a u t) -> p b a u t", b=2, a=2, t=2 * T)
            kH, kL = kx, kS
            md = parts[:].rearrange("p r a h c d -> p (r a h c d)")[:, 0:2048]\
                .rearrange("p (b h t) -> p b h t", b=2, h=NH)
            vflat = vx[:].rearrange("p r n -> p (r n)")
            o8 = vflat[:, 0:1024].rearrange("p (b n) -> p b n", b=2)
            oT8 = vflat[:, 1024:2048].rearrange("p (b n) -> p b n", b=2)

            def sync(e):
                before(e)
                for s in range(RING):
                    e.dma_start(ctxT[:, s, :], ctx_dram[:, 0, s, :]).then_inc(s_ctx[s], 16)
                with e.Fori(1, GROUPS, 1) as g:
                    for s in range(RING):
                        e.wait_ge(s_vps, at(s_vps, (g - 1) * RING + s + 1))
                        e.dma_start(ctxT[:, s, :], ctx_dram[:, g, s, :]).then_inc(s_ctx[s], 16)

            def tensor(e):
                def pe_hT(it):
                    e.wait_ge(s_h, at(s_h, it.n + 1))
                    if due(it.n - 2):
                        e.wait_ge(s_v, at(s_v, it.n - 2))
                    e.transpose(FR[:, 0:T], h[:, it.s, :], ident[:, :]).then_inc(s_hps, 1)

                def pe_qk(it):
                    e.wait_ge(s_hT, at(s_hT, it.n + 1))
                    if due(2 * it.n):
                        e.wait_ge(s_qL, at(s_qL, 2 * it.n))
                    for t in range(4):
                        m = e.matmul(TP[0][:, t * T:(t + 1) * T], w[p + "wq"][:, t * 128:(t + 1) * 128],
                                     hT[:, it.s, :], start=True, stop=True)
                    m.then_inc(s_q, 1)
                    e.wait_ge(s_ctx[it.s], at(s_ctx[it.s], 16 * (it.g + 1)))
                    if due(it.n):
                        e.wait_ge(s_kL, at(s_kL, it.n))
                    for t in range(4):
                        m = e.matmul(TP[1][:, t * T:(t + 1) * T], w[p + "wk"][:, t * 128:(t + 1) * 128],
                                     ctxT[:, it.s, :], start=True, stop=True)
                    m.then_inc(s_k, 1)

                def pe_v(it):
                    e.wait_ge(s_hT, at(s_hT, following(it, 3)))
                    e.matmul(FR[:, :], ctxT[:, it.s, :], w[p + "wv"][:, :], start=True, stop=True).then_inc(s_vps, 1)

                def pe_scores(it):
                    e.wait_ge(s_qH, at(s_qH, 2 * it.n + 2))
                    e.wait_ge(s_kH, at(s_kH, it.n + 1))
                    if due(it.n):
                        e.wait_ge(s_mx, at(s_mx, it.n))
                    for hd in range(NH):
                        t, u = hd // 2, hd % 2
                        m = e.matmul(S_ps[:, hd // 4, (hd % 4) * T:(hd % 4 + 1) * T],
                                     q8[:, it.s % 2, 0, t, u * T:(u + 1) * T], kH[:, it.s % 2, t, :],
                                     start=True, stop=True)
                    m.then_inc(s_s, 1)

                def pe_scoresT(it):
                    e.wait_ge(s_md, at(s_md, it.n + 1))
                    e.wait_ge(s_qL, at(s_qL, 2 * it.n + 2))
                    e.wait_ge(s_kL, at(s_kL, it.n + 1))
                    if due(it.n):
                        e.wait_ge(s_exp, at(s_exp, it.n))
                    for b in range(2):
                        e.matmul(ST_ps[:, b, :], ones_r[:, :],
                                 md[:, it.s % 2, 4 * b:4 * b + 4, :].rearrange("p h t -> p (h t)"),
                                 start=True, stop=False)
                        for t in (2 * b, 2 * b + 1):
                            dst = ST_ps[:, b, (t % 2) * 2 * T:(t % 2 + 1) * 2 * T]
                            for kk, a_ in ((kH, 0), (kL, 0), (kH, 1)):
                                m = e.matmul(dst, kk[:, it.s % 2, t, :], q8[:, it.s % 2, a_, t, :],
                                             start=False, stop=(t == 2 * b + 1 and kk is kH and a_ == 1))
                    m.then_inc(s_st, 1)

                def pe_values(it, half):
                    if half == 0:
                        e.wait_ge(s_exp, at(s_exp, it.n + 1))
                        e.wait_ge(s_v, at(s_v, it.n + 1))
                        if due(it.n):
                            e.wait_ge(s_done, at(s_done, it.n))
                    else:
                        e.wait_ge(s_o, at(s_o, 2 * it.n + 1))
                    for i in range(4):
                        hd = 4 * half + i
                        m = e.matmul(OB[:, i * T:(i + 1) * T], P8[:, it.s % 2, hd, :],
                                     v8[:, it.s % 2, hd * (HD + 1):hd * (HD + 1) + T], start=True, stop=True)
                    m.then_inc(s_av, 1)

                def pe_oT(it):
                    e.wait_ge(s_o, at(s_o, 2 * it.n + 2))
                    for t in range(4):
                        m = e.transpose(OB[:, t * T:(t + 1) * T], o8[:, it.s % 2, t * 128:(t + 1) * 128], ident[:, :])
                    m.then_inc(s_ops, 1)

                def pe_out(it):
                    e.wait_ge(s_oT, at(s_oT, it.n + 1))
                    for t in range(4):
                        m = e.matmul(OB[:, 0:D], oT8[:, it.s % 2, t * T:(t + 1) * T], w[p + "wo"][:, t, :],
                                     start=(t == 0), stop=(t == 3))
                    m.then_inc(s_out, 1)
                before(e)
                e.wait_ge(sem(p + "weights"), 16 * n_loads[p[:2]])
                e.wait_ge(consts_ready, N_CONSTS)
                e.wait_ge(s_pad, at(s_pad, 2))
                for item in ticks(e, 5):
                    if it := item(5):
                        pe_out(it)
                    if it := item(3):
                        pe_scoresT(it)
                    if it := item(4):
                        pe_values(it, 0)
                    if it := item(2):
                        pe_scores(it)
                    if it := item(1):
                        pe_hT(it)
                    if it := item(4):
                        pe_values(it, 1)
                    if it := item(3):
                        pe_v(it)
                    if it := item(4):
                        pe_oT(it)
                    if it := item(1):
                        pe_qk(it)

            def vector(e):
                def v_low(it):
                    e.wait_ge(s_qH, at(s_qH, 2 * it.n + 2))
                    for u in range(2):
                        r = slice(64 * u, 64 * u + 64)
                        e.tensor_tensor(q8[r, it.s % 2, 1, :, u * T:(u + 1) * T],
                                        TP[0][r, :].rearrange("p (t n) -> p t n", t=4),
                                        q8[r, it.s % 2, 0, :, u * T:(u + 1) * T].bitcast(F32),
                                        ALU.subtract).then_inc(s_qL, 1)
                    e.wait_ge(s_kH, at(s_kH, it.n + 1))
                    e.tensor_tensor(kL[:, it.s % 2, :, :].rearrange("p t n -> p (t n)"), TP[1][:, :],
                                    kH[:, it.s % 2, :, :].rearrange("p t n -> p (t n)").bitcast(F32),
                                    ALU.subtract).then_inc(s_kL, 1)

                def v_max(it):
                    e.wait_ge(s_s, at(s_s, it.n + 1))
                    e.tensor_reduce(mx[:, it.s, 0:NH], S_ps[:, :, :].rearrange("p i (j t) -> p (i j) t", t=T),
                                    AXX, ALU.max).then_inc(s_mx, 1)
                    e.wait_ge(s_mx, at(s_mx, it.n + 1))
                    e.tensor_scalar(mx[:, it.s, NH:2 * NH], mx[:, it.s, 0:NH], -1.0, None, ALU.mult).then_inc(s_nm, 1)

                def v_heads(it, half):
                    e.wait_ge(s_av, at(s_av, 2 * it.n + half + 1))
                    ob = OB[:, :].rearrange("p (h n) -> p h n", n=T)
                    e.reciprocal(rec[:, 0:4].unsqueeze(2), ob[:, :, HD:HD + 1]).then_inc(s_rec, 1)
                    if half == 0:
                        if due(it.n - 1):
                            e.wait_ge(s_ops, at(s_ops, it.n - 1))
                    e.wait_ge(s_rec, at(s_rec, 2 * it.n + half + 1))
                    e.tensor_tensor(o8[:, it.s % 2, 256 * half:256 * half + 256].rearrange("p (h n) -> p h n", h=4),
                                    ob[:, :, 0:HD], rec[:, 0:4].unsqueeze(2).broadcast_to([T, 4, HD]),
                                    ALU.mult).then_inc(s_o, 1)

                def v_residual(it):
                    e.wait_ge(s_xb, at(s_xb, it.n + 1))
                    e.wait_ge(s_out, at(s_out, it.n + 1))
                    e.tensor_tensor(X[:, it.g, it.s, :], X[:, it.g, it.s, :], OB[:, 0:D], ALU.add).then_inc(s_done, 1)
                before(e)
                e.wait_ge(sem(p + "weights"), 16 * n_loads[p[:2]])
                for item in ticks(e, 5):
                    if it := item(5):
                        v_residual(it)
                    if it := item(0):
                        stats(e, it)
                    if it := item(2):
                        v_low(it)
                    if it := item(1):
                        norm(e, it, h[:, it.s, :])
                    if it := item(4):
                        v_heads(it, 0)
                    if it := item(2):
                        v_max(it)
                    if it := item(4):
                        v_heads(it, 1)
                    if it := item(0):
                        aggregate(e, it)

            def pool(e):
                def g_bias(it):
                    e.wait_ge(s_h, at(s_h, it.n + 1))
                    e.tensor_tensor(X[:, it.g, it.s, :], X[:, it.g, it.s, :], w[p + "bo"][:, :], ALU.add)\
                     .then_inc(s_xb, 1)

                def g_diagonals(it):
                    if due(it.n - 1):
                        e.wait_ge(s_st, at(s_st, it.n - 1))
                    e.wait_ge(s_nm, at(s_nm, it.n + 1))
                    e.tensor_tensor(md[:, it.s % 2], ident[:, :].unsqueeze(1).broadcast_to([T, NH, T]),
                                    mx[:, it.s, NH:2 * NH].unsqueeze(2).broadcast_to([T, NH, T]),
                                    ALU.mult).then_inc(s_md, 1)
                before(e)
                e.wait_ge(sem(p + "weights"), 16 * n_loads[p[:2]])
                e.memset(qS[:].bitcast(F32), 0.0).then_inc(s_pad, 1)
                e.memset(v8[:, :, :], 1.0).then_inc(s_pad, 1)
                for item in ticks(e, 2):
                    if it := item(1):
                        g_bias(it)
                    if it := item(2):
                        g_diagonals(it)
                    if it := item(0):
                        rsqrt(e, it)

            def scalar(e):
                def a_high(it):
                    if due(it.n - 1):
                        e.wait_ge(s_st, at(s_st, it.n - 1))
                    e.wait_ge(s_q, at(s_q, it.n + 1))
                    for u in range(2):
                        r = slice(64 * u, 64 * u + 64)
                        e.copy(q8[r, it.s % 2, 0, :, u * T:(u + 1) * T],
                               TP[0][r, :].rearrange("p (t n) -> p t n", t=4)).then_inc(s_qH, 1)
                    e.wait_ge(s_k, at(s_k, it.n + 1))
                    e.copy(kH[:, it.s % 2, :, :].rearrange("p t n -> p (t n)"), TP[1][:, :]).then_inc(s_kH, 1)

                def a_hT(it):
                    if due(it.n - RING + 1):
                        e.wait_ge(s_q, at(s_q, it.n - RING + 1))
                    e.wait_ge(s_hps, at(s_hps, it.n + 1))
                    e.copy(hT[:, it.s, :], FR[:, 0:T]).then_inc(s_hT, 1)

                def a_exp(it):
                    if due(2 * (it.n - 1)):
                        e.wait_ge(s_av, at(s_av, 2 * (it.n - 1)))
                    e.wait_ge(s_st, at(s_st, it.n + 1))
                    e.activation(P8[:, it.s % 2, :, :].rearrange("p h t -> p (h t)"),
                                 ST_ps[:, :, :].rearrange("p j n -> p (j n)"), ACT.Exp,
                                 scale=float(HD) ** -0.5).then_inc(s_exp, 1)

                def a_v(it):
                    if due(2 * (it.n - 1)):
                        e.wait_ge(s_av, at(s_av, 2 * (it.n - 1)))
                    e.wait_ge(s_vps, at(s_vps, it.n + 1))
                    e.copy(v8[:, it.s % 2, 0:NH * (HD + 1)].rearrange("p (h n) -> p h n", h=NH)[:, :, 0:HD],
                           FR[:, :].rearrange("p (h n) -> p h n", h=NH)).then_inc(s_v, 1)

                def a_oT(it):
                    if due(it.n - 1):
                        e.wait_ge(s_out, at(s_out, it.n - 1))
                    e.wait_ge(s_ops, at(s_ops, it.n + 1))
                    e.copy(oT8[:, it.s % 2, :], OB[:, :]).then_inc(s_oT, 1)
                before(e)
                e.wait_ge(s_pad, at(s_pad, 2))
                for item in ticks(e, 4):
                    if it := item(2):
                        a_high(it)
                    if it := item(3):
                        a_exp(it)
                    if it := item(1):
                        a_hT(it)
                    if it := item(4):
                        a_oT(it)
                    if it := item(3):
                        a_v(it)
            totals(stats=B, rstd=B, h=B, bn=B, ve=B, hps=B, hT=B, q=B, k=B, vps=B, v=B, qH=2 * B, kH=B,
                   qL=2 * B, kL=B, s=B, mx=B, nm=B, md=B, st=B, exp=B, av=2 * B, rec=2 * B, o=2 * B, ops=B,
                   oT=B, out=B, xb=B, done=B, pad=2)
            totals(**{f"ctx{i}": 16 * GROUPS for i in range(RING)})
            return dict(sync=sync, tensor=tensor, vector=vector, gpsimd=pool, scalar=scalar, done=(s_done, reached["done"]))

        def experts(p, before, E, tiles, kind, top_k, source, shared=False):
            at = counted_from(dict(reached))
            n_exp = E + (1 if shared else 0)
            n_z = {"gelu": tiles, "relu": tiles, "glu": 2 * tiles, "linear": 0}[kind] * n_exp
            per_e = n_z // n_exp
            s_bn, s_st, s_ms = sem("bn"), sem("stats"), sem("ms")
            s_ve, s_rs, s_h = sem("ve"), sem("rstd"), sem("h")
            s_hps, s_hT, s_lg = sem("hps"), sem("hT"), sem("logits")
            s_r, s_e = sem("route"), sem("exp")
            s_wt, s_wps, s_wT = sem("wt"), sem("wps"), sem("wT")
            s_loc, s_locr = sem("loc"), sem("loc_read")
            s_z, s_g, s_sig = sem("z"), sem("g"), sem("sig")
            s_y, s_acc, s_done = sem("y"), sem("acc"), sem("done")
            rms = kind == "glu"
            wg, b2 = w[p + "wg"], w.get(p + "b2")
            w1, b1, w2 = w.get(p + "w1"), w.get(p + "b1"), w[p + "w2"]
            STATS, NORM, TURN, LOGITS, ROUTE = 1, 2, 3, 5, 6
            n_steps = n_exp + (1 if b2 is not None else 0)
            ZP = [PS[:, bank, :] for bank in (0, 1, 6, 7)]
            YP = [PS[:, 2, :], PS[:, 3, :]]
            HP, LP = PS[:, 4, :], PS[:, 5, :]
            WP = HP if n_z else PS[:, 6, :]
            if n_z:
                s_wh, s_wl, s_hH, s_hL = (sem(n) for n in ("w_high", "w_low", "rows_high", "rows_low"))
                n_cuts = n_z // 4
                w_in = w1.rearrange("p x n -> p (x n)").rearrange("p (c n) -> p c n", n=512)
                w_high = parts[:].rearrange("p r a h c d -> p (r a h c d)").rearrange("p (c n) -> p c n", n=512)
                w_low = qS[:].rearrange("p b g j t -> p (b g j t)").rearrange("p (c n) -> p c n", n=512)
                hH, hL = (buf[:].rearrange("p b j t -> p b (j t)") for buf in (kx, kS))

            def groups(e, prologue, body):
                before(e)
                e.wait_ge(sem(p + "weights"), 16 * n_loads[p[:2]])
                e.wait_ge(consts_ready, N_CONSTS)
                prologue()
                body(0, 0, True)
                with e.Fori(0, GROUPS // 2 - 1, 1) as pair:
                    body(2 * pair + 1, 1, True)
                    body(2 * pair + 2, 0, True)
                body(GROUPS - 1, (GROUPS - 1) % 2, False)

            def tensor(e):
                def prep(g, b):
                    for s in range(RING):
                        e.wait_ge(s_h, at(s_h, RING * g + s + 1))
                        if s == 0:
                            if due(g):
                                e.wait_ge(s_hT, at(s_hT, g))
                            if b2 is not None and n_z and due(g):
                                e.wait_ge(s_wT, at(s_wT, g))
                        m = e.transpose(HP[:, s * T:(s + 1) * T], h[:, s, :], ident[:, :])
                        m.then_inc(s_hps, 1)

                def logits(g, b):
                    if due(n_route * (g - 1) + 1):
                        e.wait_ge(s_r, at(s_r, n_route * (g - 1) + 1))
                    e.wait_ge(s_hT, at(s_hT, g + 1))
                    for s in range(RING):
                        m = e.matmul(LP[:, s * E:(s + 1) * E], hT4[:, b, s * T:(s + 1) * T], wg[:, :],
                                     start=True, stop=True)
                    m.then_inc(s_lg, 1)

                def z(g, b, i):
                    if due(zfree(g, i)):
                        e.wait_ge(s_g, at(s_g, zfree(g, i)))
                    if i == 0:
                        e.wait_ge(s_hL, at(s_hL, g + 1))
                    if isinstance(g, int) and g == 0 and i % 4 == 0:
                        e.wait_ge(s_wl, at(s_wl, i // 4 + 1))
                    c, n = i // 4, slice(i % 4 * 128, i % 4 * 128 + 128)
                    e.matmul(ZP[i % 4][:, :], w_high[:, c, n], hH[:, b], start=True, stop=False)
                    e.matmul(ZP[i % 4][:, :], w_low[:, c, n], hH[:, b], start=False, stop=False)
                    e.matmul(ZP[i % 4][:, :], w_high[:, c, n], hL[:, b], start=False, stop=True)\
                     .then_inc(s_z, 1)

                def zfree(g, i):
                    if kind == "glu":
                        return tiles * n_exp * g + i // 2 - 1
                    return n_z * g + i - 3

                def y(g, b, x):
                    k = n_exp * g + x
                    if due(RING * (n_steps * g + x - 1)):
                        e.wait_ge(s_acc, at(s_acc, RING * (n_steps * g + x - 1)))
                    if kind != "linear":
                        e.wait_ge(s_g, at(s_g, tiles * (k + 1)))
                    for s in range(RING):
                        for t in range(tiles):
                            lhs = hT4[:, b, s * T:(s + 1) * T] if kind == "linear" else \
                                gt[:, (x % 2) * tiles + t, s * T:(s + 1) * T]
                            m = e.matmul(YP[(n_steps * b + x) % 2][:, s * T:(s + 1) * T], lhs, w2[:, x, t * D:(t + 1) * D],
                                         start=(t == 0), stop=(t == tiles - 1))
                    m.then_inc(s_y, 1)

                def bias(g, b):
                    if due(g):
                        e.wait_ge(s_wT, at(s_wT, g))
                    e.wait_ge(s_wt, at(s_wt, n_wt * (g + 1)))
                    for s in range(RING):
                        m = e.transpose(WP[0:n_exp, s * T:(s + 1) * T], wt[:, b, s, 0:n_exp], ident[:, :])
                    m.then_inc(s_wps, 1)

                def bias_rows(g, b):
                    e.wait_ge(s_wT, at(s_wT, g + 1))
                    if due(RING * (n_steps * g + n_exp - 1)):
                        e.wait_ge(s_acc, at(s_acc, RING * (n_steps * g + n_exp - 1)))
                    for s in range(RING):
                        m = e.matmul(YP[(n_steps * b + n_exp) % 2][:, s * T:(s + 1) * T], wT[0:n_exp, s * T:(s + 1) * T],
                                     b2[:, :], start=True, stop=True)
                    m.then_inc(s_y, 1)

                def positions(g):
                    if due(g):
                        e.wait_ge(s_wT, at(s_wT, g))
                    e.wait_ge(s_r, at(s_r, n_route * g + n_before_loc))
                    for s in range(RING):
                        e.matmul(WP[:, s * E:(s + 1) * E], earlier[:, :], sel[:, s, 0:E], start=True, stop=False)
                        m = e.matmul(WP[:, s * E:(s + 1) * E], ones[:, :], run[:, s, :], start=False, stop=True)
                    m.then_inc(s_loc, 1)

                def prologue():
                    prep(0, 0)
                    logits(0, 0)
                    if kind == "linear":
                        positions(0)

                def body(g, b, more):
                    for x in range(n_exp + 1):
                        if x < n_exp:
                            for t in range(per_e):
                                z(g, b, x * per_e + t)
                        if x == TURN and more:
                            prep(g + 1, 1 - b)
                        if x == LOGITS and more:
                            logits(g + 1, 1 - b)
                        if kind == "linear" and x == ROUTE + 1 and more:
                            positions(g + 1)
                        if x >= 1:
                            y(g, b, x - 1)
                        if b2 is not None and x == 1:
                            bias(g, b)
                    if b2 is not None:
                        bias_rows(g, b)
                groups(e, prologue, body)

            def vector(e):
                def statistics(g):
                    for s in range(RING):
                        if due(RING * (g - 1) + s + 1):
                            e.wait_ge(s_hps, at(s_hps, RING * (g - 1) + s + 1))
                        e.bn_stats(bn[:, s, :], source[:, g, s, :]).then_inc(s_bn, 1)
                    e.wait_ge(s_bn, at(s_bn, RING * (g + 1)))
                    e.tensor_copy(scratch[:, 0:1], neg_half[:, 0:1])
                    for s in range(RING):
                        m = e.bn_aggr(mv[:, s, :], bn[:, s, :])
                        m.then_inc(s_st, 1)
                    if rms:
                        e.wait_ge(s_st, at(s_st, RING * (g + 1)))
                        e.tensor_tensor(ve[:, :, :], mv[:, :, 0:1], mv[:, :, 0:1], ALU.mult).then_inc(s_ms, 1)
                        e.wait_ge(s_ms, at(s_ms, 2 * g + 1))
                        e.tensor_tensor(mv[:, :, 1:2], mv[:, :, 1:2], ve[:, :, :], ALU.add).then_inc(s_ms, 1)

                def norm(g):
                    e.wait_ge(s_rs, at(s_rs, g + 1))
                    for s in range(RING):
                        if rms:
                            m = e.tensor_scalar(h[:, s, :], source[:, g, s, :], rstd[:, s, :], None, ALU.mult)
                        else:
                            m = e.tensor_scalar(h[:, s, :], source[:, g, s, :], mv[:, s, 0:1], rstd[:, s, :],
                                                ALU.subtract, ALU.mult)
                        m.then_inc(s_h, 1)

                def bc(t):
                    return t[:, :].unsqueeze(2).broadcast_to([T, RING, E])

                def route(g, b):
                    n = [0]

                    def step(m):
                        n[0] += 1
                        m.then_inc(s_r, 1)
                        e.wait_ge(s_r, at(s_r, n_route * g + n[0]))
                    e.wait_ge(s_lg, at(s_lg, g + 1))
                    lp = LP[:, 0:RING * E].rearrange("p (s x) -> p s x", s=RING)
                    if p + "bg" in w:
                        step(e.tensor_tensor(lg[:, :, 0:E], lp,
                                             w[p + "bg"][:, :].unsqueeze(1).broadcast_to([T, RING, E]), ALU.add))
                    else:
                        step(e.tensor_copy(lg[:, :, 0:E], lp))
                    L, SEL, TMP = lg[:, :, 0:E], sel[:, :, 0:E], tmp[:, :, 0:E]
                    for k in range(top_k):
                        step(e.tensor_reduce(rmax[:, :], L, AXX, ALU.max))
                        if k == 0 and kind != "glu":
                            step(e.tensor_tensor(pr[:, :, 0:E], L, bc(rmax), ALU.subtract))
                        step(e.tensor_tensor(TMP, L, bc(rmax), ALU.is_equal))
                        step(e.tensor_tensor(TMP, TMP, rank[:, 0:E].unsqueeze(1).broadcast_to([T, RING, E]), ALU.mult))
                        step(e.tensor_reduce(rmax[:, :], TMP, AXX, ALU.max))
                        if top_k > 1:
                            yield
                        if k == 0:
                            step(e.tensor_tensor(SEL, TMP, bc(rmax), ALU.is_equal))
                            one = SEL
                        else:
                            step(e.tensor_tensor(TMP, TMP, bc(rmax), ALU.is_equal))
                            step(e.tensor_tensor(SEL, SEL, TMP, ALU.add))
                            one = TMP
                        if k < top_k - 1:
                            step(e.scalar_tensor_tensor(out=L, in0=one, scalar=-BIG, in1=L, op0=ALU.mult, op1=ALU.add))
                            yield
                    if kind == "linear":
                        for s in range(RING):
                            step(e.tensor_tensor(run[:, s + 1, :], run[:, s, :], sel[:, s, 0:E], ALU.add))
                        assert n[0] == n_before_loc
                        yield
                        e.wait_ge(s_loc, at(s_loc, g + 1))
                        loc = WP[:, 0:RING * E].rearrange("p (s x) -> p s x", s=RING)
                        e.tensor_scalar(tmp[:, :, 0:E], loc, float(B * T // E), None, ALU.is_lt).then_inc(s_locr, 1)
                        e.wait_ge(s_locr, at(s_locr, g + 1))
                        step(e.tensor_tensor(SEL, SEL, TMP, ALU.mult))
                        step(e.tensor_copy(run[:, 0, :], run[:, RING, :]))
                    if kind != "glu":
                        e.wait_ge(s_e, at(s_e, g + 1))
                        step(e.tensor_reduce(rsum[:, :], pr[:, :, 0:E], AXX, ALU.add))
                        step(e.reciprocal(rsum[:, :], rsum[:, :]))
                        step(e.tensor_tensor(pr[:, :, 0:E], pr[:, :, 0:E], bc(rsum), ALU.mult))
                        e.tensor_tensor(wt[:, b, :, 0:E], SEL, pr[:, :, 0:E], ALU.mult).then_inc(s_wt, 1)
                    else:
                        e.tensor_copy(wt[:, b, :, 0:E], SEL).then_inc(s_wt, 1)
                    assert n[0] == n_route, n[0]

                def add(g, b, x):
                    k = n_steps * g + x
                    e.wait_ge(s_y, at(s_y, k + 1))
                    if x == 0:
                        e.wait_ge(s_wt, at(s_wt, n_wt * (g + 1)))
                    for s in range(RING):
                        if due(RING * (k - 1) + s + 1):
                            e.wait_ge(s_acc, at(s_acc, RING * (k - 1) + s + 1))
                        X_s = X[:, g, s, :]
                        rows = YP[(n_steps * b + x) % 2][:, s * T:(s + 1) * T]
                        if x < E:
                            m = e.scalar_tensor_tensor(out=X_s, in0=rows, scalar=wt[:, b, s, x:x + 1], in1=X_s,
                                                       op0=ALU.mult, op1=ALU.add)
                        else:
                            m = e.tensor_tensor(X_s, X_s, rows, ALU.add)
                        m.then_inc(s_acc, 1)

                def product(g, i):
                    x, t = i // tiles, i % tiles
                    if due(n_steps * g + x - 1):
                        e.wait_ge(s_y, at(s_y, n_steps * g + x - 1))
                    e.wait_ge(s_sig, at(s_sig, tiles * n_exp * g + i + 1))
                    e.scalar_tensor_tensor(out=gt[:, (x % 2) * tiles + t, :], in0=ZP[2 * (i % 2)][:, :],
                                           scalar=b1[:, x, t:t + 1], in1=sg[:, i % 2, :],
                                           op0=ALU.add, op1=ALU.mult).then_inc(s_g, 1)

                def prologue():
                    if kind == "linear":
                        e.memset(run[:, 0, :], 0.0).then_inc(s_ms, 1)
                        e.wait_ge(s_ms, at(s_ms, 1))
                    if shared:
                        e.memset(wt[:, :, :, E:E + 1], 1.0).then_inc(s_ms, 1)
                    statistics(0)
                    norm(0)
                    if n_z:
                        for c in range(n_cuts):
                            e.wait_ge(s_wh, at(s_wh, c + 1))
                            e.tensor_tensor(w_low[:, c, :], w_in[:, c, :], w_high[:, c, :].bitcast(F32),
                                            ALU.subtract).then_inc(s_wl, 1)
                    for _ in route(0, 0):
                        pass

                def body(g, b, more):
                    pieces = route(g + 1, 1 - b)
                    for x in range(n_steps + 1):
                        if kind == "glu" and x < n_exp:
                            for t in range(tiles):
                                product(g, x * tiles + t)
                        if x == STATS and more:
                            statistics(g + 1)
                        if x == NORM and more:
                            norm(g + 1)
                        if x >= ROUTE and more:
                            next(pieces, None)
                        if x >= 1:
                            add(g, b, x - 1)
                groups(e, prologue, body)

            def pool(e):
                def rs(g):
                    if rms:
                        e.wait_ge(s_ms, at(s_ms, 2 * (g + 1)))
                    else:
                        e.wait_ge(s_st, at(s_st, RING * (g + 1)))
                    e.tensor_tensor(ve2[:, :, :], mv[:, :, 1:2], eps_t[:, (1 if rms else 0):][:, 0:1].unsqueeze(1).broadcast_to([T, RING, 1]),
                                    ALU.add).then_inc(s_ve, 1)
                    e.wait_ge(s_ve, at(s_ve, g + 1))
                    if due(RING * g):
                        e.wait_ge(s_h, at(s_h, RING * g))
                    e.tensor_tensor(rstd[:, :, :], ve2[:, :, :], neg_half[:, 0:RING].unsqueeze(2), ALU.pow)\
                     .then_inc(s_rs, 1)

                def low_rows(g, b):
                    e.wait_ge(s_hH, at(s_hH, g + 1))
                    e.tensor_tensor(hL[:, b], hT4[:, b], hH[:, b].bitcast(F32), ALU.subtract).then_inc(s_hL, 1)

                def prologue():
                    rs(0)
                    if n_z:
                        low_rows(0, 0)

                def body(g, b, more):
                    if more:
                        rs(g + 1)
                        if n_z:
                            low_rows(g + 1, 1 - b)
                groups(e, prologue, body)

            def scalar(e):
                def turn(g, b):
                    if due(g - 1):
                        e.wait_ge(s_lg, at(s_lg, g - 1))
                        if n_z:
                            e.wait_ge(s_hL, at(s_hL, g - 1))
                            e.wait_ge(s_z, at(s_z, n_z * (g - 1)))
                        else:
                            e.wait_ge(s_y, at(s_y, n_steps * (g - 1)))
                    e.wait_ge(s_hps, at(s_hps, RING * (g + 1)))
                    if rms:
                        m = e.activation(hT4[:, b], HP[:, :], ACT.Identity, scale=w[p + "ln"][:, 0:1])
                    else:
                        m = e.copy(hT4[:, b], HP[:, :])
                    m.then_inc(s_hT, 1)
                    if n_z:
                        e.wait_ge(s_hT, at(s_hT, g + 1))
                        e.copy(hH[:, b], hT4[:, b]).then_inc(s_hH, 1)

                def round_weights():
                    for c in range(n_cuts):
                        e.copy(w_high[:, c, :], w_in[:, c, :]).then_inc(s_wh, 1)

                def prologue():
                    if n_z:
                        round_weights()
                    turn(0, 0)
                    if kind != "glu":
                        route_exp(0)

                def route_exp(g):
                    e.wait_ge(s_r, at(s_r, n_route * g + 3))
                    e.activation(pr[:, :, 0:E], pr[:, :, 0:E], ACT.Exp).then_inc(s_e, 1)

                def hidden(g, i):
                    x, t = i // per_e, i % per_e
                    if kind == "glu":
                        if t % 2 == 0:
                            return
                        j = i // 2
                        if due(tiles * n_exp * g + j - 1):
                            e.wait_ge(s_g, at(s_g, tiles * n_exp * g + j - 1))
                        e.wait_ge(s_z, at(s_z, n_z * g + i + 1))
                        e.activation(sg[:, j % 2, :], ZP[i % 4][:, :], ACT.Sigmoid,
                                     bias=b1[:, x, tiles + t // 2:tiles + t // 2 + 1]).then_inc(s_sig, 1)
                        return
                    if due(n_steps * g + x - 1 if x >= 2 else bound(g, x)):
                        e.wait_ge(s_y, at(s_y, n_steps * g + x - 1 if x >= 2 else bound(g, x)))
                    e.wait_ge(s_z, at(s_z, n_z * g + i + 1))
                    e.activation(gt[:, (x % 2) * tiles + t, :], ZP[i % 4][:, :],
                                 ACT.Gelu if kind == "gelu" else ACT.Relu,
                                 bias=b1[:, x, t:t + 1]).then_inc(s_g, 1)

                def bound(g, x):
                    last = n_exp - 2 + x
                    same = last if last % 2 == x % 2 else last + 1
                    return n_steps * (g - 1) + min(same, n_exp - 1) + 1

                def turn_weights(g):
                    if due(n_steps * g):
                        e.wait_ge(s_y, at(s_y, n_steps * g))
                    e.wait_ge(s_wps, at(s_wps, g + 1))
                    e.copy(wT[0:n_exp, :], WP[0:n_exp, :]).then_inc(s_wT, 1)

                def body(g, b, more):
                    for x in range(n_exp):
                        for t in range(per_e):
                            hidden(g, x * per_e + t)
                        if b2 is not None and x == 1:
                            turn_weights(g)
                        if x == TURN and more:
                            turn(g + 1, 1 - b)
                        if x == ROUTE and more and kind != "glu":
                            route_exp(g + 1)
                groups(e, prologue, body)

            n_wt = 1
            n_route = 1
            for k in range(top_k):
                n_route += 1 + (1 if k == 0 and kind != "glu" else 0) + 3
                n_route += 1 if k == 0 else 2
                n_route += 1 if k < top_k - 1 else 0
            n_before_loc = n_route + RING
            if kind == "linear":
                n_route += RING + 2
            if kind != "glu":
                n_route += 3

            hidden_steps = n_z // 2 if kind == "glu" else n_z
            totals(bn=B, stats=B, h=B, hps=B, ve=GROUPS, rstd=GROUPS, hT=GROUPS, logits=GROUPS,
                   route=n_route * GROUPS, wt=GROUPS, z=n_z * GROUPS, g=hidden_steps * GROUPS,
                   y=n_steps * GROUPS, acc=RING * n_steps * GROUPS)
            if kind == "glu":
                totals(ms=2 * GROUPS, sig=hidden_steps * GROUPS)
            else:
                totals(exp=GROUPS)
            totals(ms=int(kind == "linear") + int(shared))
            if n_z:
                totals(w_low=n_cuts, w_high=n_cuts, rows_high=GROUPS, rows_low=GROUPS)
            if kind == "linear":
                totals(loc=GROUPS, loc_read=GROUPS)
            if b2 is not None:
                totals(wps=GROUPS, wT=GROUPS)
            return dict(sync=lambda e: None, tensor=tensor, vector=vector, gpsimd=pool, scalar=scalar,
                        done=(s_acc, reached["acc"]))

        n_loads = {}
        for ph, _, _ in loads:
            n_loads[ph] = n_loads.get(ph, 0) + 1
        x_loaded = sem("x_loaded")

        def first(e):
            e.wait_ge(x_loaded, 16)
            e.wait_ge(sem("a0_weights"), 16 * n_loads["a0"])

        phases = []

        def follow(make, *args, **kw):
            if phases:
                s_before, count = phases[-1]["done"]
                phases.append(make(args[0], lambda e: e.wait_ge(s_before, count), *args[1:], **kw))
            else:
                phases.append(make(args[0], first, *args[1:], **kw))

        plan = [("a0", lambda: follow(attention16, "a0_", "cross")),
                ("f0", lambda: follow(experts, "f0_", 8, 4, "gelu", 1, X)),
                ("a1", lambda: follow(attention1, "a1_")),
                ("f1", lambda: follow(experts, "f1_", 15, 1, "relu", 3, X, shared=True)),
                ("a2", lambda: follow(attention16, "a2_", "masked")),
                ("b2", lambda: follow(attention16, "b2_", "self")),
                ("f2", lambda: follow(experts, "f2_", 8, 2, "glu", 1, Y)),
                ("a3", lambda: follow(attention8, "a3_")),
                ("f3", lambda: follow(experts, "f3_", 8, 1, "linear", 1, X))]
        ran = []
        only = upto.split(":")[1] if ":" in upto else None
        for name, make in plan:
            if only is None or name in only.split("+"):
                make()
                ran.append(name)
            if name == upto:
                break
        stored = sem("stored")
        block = ctx.enter_context(nc.Block())

        @block.sync
        def _(e):
            late = {n: b for n, b in (("f2", "f0"), ("f3", "f1")) if b in ran}

            def load(name):
                for ph, tile, arr in loads:
                    if ph == name:
                        e.dma_start(tile, arr).then_inc(sem(ph + "_weights"), 16)
            load("a0")
            e.dma_start(X[:], x_dram).then_inc(x_loaded, 16)
            for name in ran:
                if name != "a0" and name not in late:
                    load(name)
            for name, p in zip(ran, phases):
                p["sync"](e)
                for later, earlier_phase in late.items():
                    if earlier_phase == name and later in ran:
                        e.wait_ge(*p["done"])
                        load(later)
            e.wait_ge(*phases[-1]["done"])
            e.dma_start(out_dram, X[:]).then_inc(stored, 16)
            e.wait_ge(stored, 16)

        @block.tensor
        def _(e):
            for p in phases:
                p["tensor"](e)

        @block.vector
        def _(e):
            e.memset(neg_half[:], -0.5).then_inc(consts_ready, 1)
            e.memset(vx[:], 0.0).then_inc(consts_ready, 1)
            e.memset(ones_x[:], 0.0).then_inc(consts_ready, 1)
            e.memset(ones[:], 1.0).then_inc(consts_ready, 1)
            e.wait_ge(consts_ready, 4)
            for j in range(4):
                e.memset(ones_x[:, j, j, :], 1.0).then_inc(consts_ready, 1)
            e.wait_ge(sem("a0_weights"), 16 * n_loads["a0"])
            e.tensor_copy(ident_r[:], ident[:]).then_inc(consts_ready, 1)
            e.tensor_copy(ones_r[:], ones[:]).then_inc(consts_ready, 1)
            e.tensor_copy(keep[:].rearrange("p g s -> p (g s)"), keep_words[:].bitcast(U8)).then_inc(consts_ready, 1)
            for i, dst in enumerate((causal_q, causal_k)):
                e.tensor_copy(dst[:].rearrange("p (j t) -> p j t", j=4),
                              causal_in[:, i, :].unsqueeze(1).broadcast_to([T, 4, T])).then_inc(consts_ready, 1)
            e.tensor_scalar(neg_bgate[:], w["b2_bgate"][:], -1.0, None, ALU.mult).then_inc(consts_ready, 1)
            for p in phases:
                p["vector"](e)

        @block.gpsimd
        def _(e):
            e.memset(eps_t[:, 0:1], EPS).then_inc(ones_ready, 1)
            e.memset(eps_t[:, 1:2], RMS_EPS).then_inc(ones_ready, 1)
            e.memset(zeros[:], 0.0).then_inc(ones_ready, 1)
            e.wait_ge(ones_ready, 3)
            e.wait_ge(consts_ready, N_CONSTS)
            for p in phases:
                p["gpsimd"](e)

        @block.scalar
        def _(e):
            for p in phases:
                p["scalar"](e)


def layout(i):
    def rows(v, n=128):
        return np.broadcast_to(v, (n,) + v.shape).reshape(n, -1)
    a = {}
    a["x"] = i["x"]
    a["ctxT"] = i["ctx_768"].transpose(0, 2, 1)
    a["ident"] = np.eye(128, dtype=np.float32)
    a["jmask"] = np.tile(np.repeat(np.eye(4, dtype=np.float32), DH, 0), (4, 1))
    a["a0_wq"] = i["L0_xattn_wq"].T
    a["a0_wkv"] = np.concatenate([i["L0_xattn_wk"].T, i["L0_xattn_wv"].T], 1)
    a["a0_bqk"] = rows(np.concatenate([i["L0_xattn_bq"], i["L0_xattn_bk"]]))
    a["a0_bv"] = rows(i["L0_xattn_bv"])
    a["a0_wo"] = i["L0_xattn_wo"].T
    a["a0_bo"] = rows(i["L0_xattn_bo"])
    a["a1_wq"], a["a1_wk"], a["a1_wv"] = i["L1_xattn_Wq"], i["L1_xattn_Wk"], i["L1_xattn_Wv"]
    a["a1_bq"], a["a1_bk"] = i["L1_xattn_bq"].reshape(D, 1), i["L1_xattn_bk"].reshape(D, 1)
    a["a1_bv"] = rows(i["L1_xattn_bv"])
    a["a3_wq"], a["a3_wk"], a["a3_wv"] = i["L3_xattn_Wq"], i["L3_xattn_Wk"], i["L3_xattn_Wv"]
    a["a3_wo"] = i["L3_xattn_Wo"].reshape(4, 128, D).transpose(1, 0, 2)
    a["a3_bo"] = rows(i["L3_xattn_bo"])
    a["keep"] = np.ascontiguousarray(i["mask_BxS_bk0"].T).view(np.int32)
    q, k = np.arange(T)[:, None], np.arange(T)[None, :]
    a["causal"] = np.stack([np.where(k > q, -BIG, 0), np.where(q > k, -BIG, 0)], 1).astype(np.float32)
    a["a2_wq"], a["a2_wkv"] = i["L2_xattn_Wq"].T, i["L2_xattn_Wkv"].T
    a["b2_wqkv"] = np.concatenate([i["L2_ffn_Wq"], i["L2_ffn_Wk"], i["L2_ffn_Wv"]], 1)
    a["b2_bqkv"] = rows(np.concatenate([i["L2_ffn_bq"], i["L2_ffn_bk"], i["L2_ffn_bv"]]))
    freq = 1.0 / 10000.0 ** (np.arange(0, DH, 2, dtype=np.float32) / DH)
    angle = np.arange(T, dtype=np.float32)[:, None] * freq.astype(np.float32)[None, :]
    a["b2_rope"] = np.stack([np.cos(angle), np.sin(angle), -np.sin(angle)], 1).astype(np.float32)
    a["b2_norm"] = rows(np.concatenate([i["L2_ffn_qn_w"], i["L2_ffn_kn_w"]])).reshape(T, 2, DH)
    a["b2_ln"] = i["L2_ffn_ln1_w"].reshape(D, 1)
    gate = np.zeros((H16, DH, H16, DH), np.float32)
    for head in range(H16):
        gate[head, :, head, :] = i["L2_ffn_Wg"]
    a["b2_wgate"] = gate.reshape(D, D)
    a["b2_bgate"] = np.tile(i["L2_ffn_bg"], H16).reshape(D, 1)
    a["b2_wo"], a["b2_bo"] = i["L2_ffn_Wo"], rows(i["L2_ffn_bo"])
    a["rank"] = rows(16.0 - np.arange(16, dtype=np.float32))
    a["earlier"] = np.triu(np.ones((T, T), np.float32), 1)

    def hidden_bias(v):
        return v.reshape(v.shape[0], -1, 128).transpose(2, 0, 1)

    def down(v):
        return v.reshape(v.shape[0], -1, 128, D).transpose(2, 0, 1, 3).reshape(128, v.shape[0], -1)
    a["f0_wg"], a["f0_bg"] = i["L0_ffn_gate_w"], rows(i["L0_ffn_gate_b"])
    a["f0_w1"], a["f0_b1"] = i["L0_ffn_w1"].transpose(1, 0, 2), hidden_bias(i["L0_ffn_b1"])
    a["f0_w2"], a["f0_b2"] = down(i["L0_ffn_w2"]), i["L0_ffn_b2"]
    a["f1_wg"], a["f1_bg"] = i["L1_ffn_router_W"], rows(i["L1_ffn_router_b"])

    def with_shared(e, s):
        return np.concatenate([i["L1_ffn_" + e], i["L1_ffn_" + s][None]], 0)
    a["f1_w1"] = with_shared("eW1", "sW1").transpose(1, 0, 2)
    a["f1_b1"] = hidden_bias(with_shared("eb1", "sb1"))
    a["f1_w2"], a["f1_b2"] = down(with_shared("eW2", "sW2")), with_shared("eb2", "sb2")
    a["f2_ln"] = i["L2_ffn_ln2_w"].reshape(D, 1)
    a["f2_wg"], a["f2_bg"] = i["L2_ffn_Wr"], rows(i["L2_ffn_br"])
    order = [0, 2, 1, 3]
    a["f2_w1"] = i["L2_ffn_W1"].reshape(8, D, 4, 128)[:, :, order].reshape(8, D, 512).transpose(1, 0, 2)
    a["f2_b1"] = hidden_bias(i["L2_ffn_b1"])
    a["f2_w2"], a["f2_b2"] = down(i["L2_ffn_W2"]), i["L2_ffn_b2"]
    a["f3_wg"] = i["L3_ffn_wg"]
    a["f3_w2"], a["f3_b2"] = i["L3_ffn_W"].transpose(2, 0, 1), i["L3_ffn_b"]
    return a


def kernel(**inputs):
    import concourse.bacc as bacc
    from concourse.bass_utils import run_bass_kernel_spmd as run

    nc = bacc.Bacc("TRN2", target_bir_lowering=False, num_devices=1)
    laid = layout({k: np.asarray(v) for k, v in inputs.items()})
    arrays, aps = {}, {}
    for name, v in laid.items():
        v = np.ascontiguousarray(v)
        arrays["in_" + name] = v
        aps[name] = nc.dram_tensor("in_" + name, v.shape, mybir.dt.from_np(v.dtype), kind="ExternalInput").ap()
    out = nc.dram_tensor("out", (B, T, D), F32, kind="ExternalOutput").ap()
    build(nc, aps, out)
    r = run(nc, [arrays], core_ids=[0])
    return r.results[0]["out"]
```

```python
from contextlib import ExitStack

import numpy as np

from concourse import mybir

F32 = mybir.dt.float32
F32R = mybir.dt.float32r
U8 = mybir.dt.uint8
ALU = mybir.AluOpType
ACT = mybir.ActivationFunctionType
AXX = mybir.AxisListType.X

B, T, D, C = 32, 128, 128, 96
RING = 4
GROUPS = B // RING
EPS = 1e-5
RMS_EPS = 1e-6
BIG = 1e30
H16, DH = 16, 8


class Item:

    def __init__(self, group, slot):
        self.g, self.s = group, slot
        self.n = group * RING + slot


def counted_from(before):
    def at(sem, value):
        return value + before.get(sem.name, 0)
    return at


def due(value):
    return not isinstance(value, int) or value > 0


def following(it, n):
    return min(it.n + n, B) if isinstance(it.n, int) else it.n + n


def ticks(eng, last, peel=2):
    def tick(group, j, edge):
        def item(lag):
            it = Item(group + (j - lag) // RING, (j - lag) % RING)
            return it if not edge or 0 <= it.n < B else None
        return item

    for t in range(peel * RING):
        yield tick(t // RING, t % RING, True)
    with eng.Fori(peel, GROUPS, 1) as group:
        for j in range(RING):
            yield tick(group, j, False)
    for t in range(B, B + last):
        yield tick(t // RING, t % RING, True)


def build(nc, a, out):
    ctx = ExitStack()
    with ctx:
        def sb(name, shape, dt=F32):
            return ctx.enter_context(nc.sbuf_tensor(name, shape, dt))

        sems = {}

        def sem(name):
            if name not in sems:
                sems[name] = ctx.enter_context(nc.semaphore(name))
            return sems[name]

        reached = {}

        def totals(**counts):
            for name, count in counts.items():
                reached[name] = reached.get(name, 0) + count

        X = sb("X", [T, GROUPS, RING, D])
        Y = sb("Y", [T, GROUPS, RING, D])
        ident = sb("ident", [128, 128])
        ident_r = sb("ident_r", [128, 128], F32R)
        w = {}
        loads = []

        def weight(phase, name, shape, place=None):
            w[name] = sb("w_" + name, shape)[:] if place is None else place
            loads.append((phase, w[name], a[name]))

        jmask = sb("jmask", [D, 4])
        loads.append(("a0", ident[:], a["ident"]))
        loads.append(("a0", jmask[:], a["jmask"]))
        weight("a0", "a0_wq", [D, D])
        weight("a0", "a0_wkv", [C, 2 * D])
        weight("a0", "a0_bqk", [T, 2 * D])
        weight("a0", "a0_bv", [T, D])
        weight("a0", "a0_wo", [D, D])
        weight("a0", "a0_bo", [T, D])

        weight("a1", "a1_wq", [D, D])
        weight("a1", "a1_wk", [C, D])
        weight("a1", "a1_wv", [C, D])
        weight("a1", "a1_bq", [D, 1])
        weight("a1", "a1_bk", [D, 1])
        weight("a1", "a1_bv", [T, D])
        weight("a3", "a3_wq", [D, 512])
        weight("a3", "a3_wk", [C, 512])
        weight("a3", "a3_wv", [C, 512])
        weight("a3", "a3_wo", [128, 4, D])
        weight("a3", "a3_bo", [T, D])
        weight("a2", "a2_wq", [D, D])
        weight("a2", "a2_wkv", [C, 2 * D])
        weight("b2", "b2_wqkv", [D, 192])
        weight("b2", "b2_bqkv", [T, 192])
        weight("b2", "b2_rope", [T, 3, DH // 2])
        weight("b2", "b2_norm", [T, 2, DH])
        weight("b2", "b2_ln", [D, 1])
        weight("b2", "b2_wgate", [D, D])
        weight("a0", "b2_bgate", [D, 1])
        weight("b2", "b2_wo", [D, D])
        weight("b2", "b2_bo", [T, D])
        keep_words = sb("keep_words", [T, B // 4], mybir.dt.int32)
        loads.append(("a0", keep_words[:], a["keep"]))
        causal_in = sb("causal_in", [T, 2, T])
        loads.append(("a0", causal_in[:], a["causal"]))
        weight("f0", "f0_wg", [D, 8])
        weight("f0", "f0_bg", [T, 8])
        weight("f0", "f0_w1", [D, 8, 512])
        weight("f0", "f0_b1", [128, 8, 4])
        weight("f0", "f0_w2", [128, 8, 512])
        weight("f0", "f0_b2", [8, D])
        weight("f1", "f1_wg", [D, 15])
        weight("f1", "f1_bg", [T, 15])
        weight("f1", "f1_w1", [D, 16, 128])
        weight("f1", "f1_b1", [128, 16, 1])
        weight("f1", "f1_w2", [128, 16, 128])
        weight("f1", "f1_b2", [16, D])
        weight("f2", "f2_ln", [D, 1])
        weight("f2", "f2_wg", [D, 8])
        weight("f2", "f2_bg", [T, 8])
        weight("f2", "f2_w1", [D, 8, 512], w["f0_w1"])
        weight("f2", "f2_b1", [128, 8, 4])
        weight("f2", "f2_w2", [128, 8, 256], w["f0_w2"][:, 0:4, :].rearrange("p a (b n) -> p (a b) n", b=2))
        weight("f2", "f2_b2", [8, D])
        weight("f3", "f3_wg", [D, 8])
        weight("f3", "f3_w2", [D, 8, 128], w["f1_w1"][:, 0:8, :])
        weight("f3", "f3_b2", [8, D])
        rank = sb("rank", [T, 16])
        earlier = sb("earlier", [T, T])
        loads.append(("a0", rank[:], a["rank"]))
        loads.append(("a0", earlier[:], a["earlier"]))
        ones = sb("ones", [T, T])
        minus_ones = sb("minus_ones", [T, T], F32R)
        hT4 = sb("hT4", [D, 2, RING * T])
        sg = sb("sg", [128, 2, RING * T])
        lg, sel, tmp, pr = (sb(n, [T, RING, 16]) for n in ("lg", "sel", "tmp", "pr"))
        wt = sb("wt", [T, 2, RING, 16])
        rmax, rsum = sb("rmax", [T, RING]), sb("rsum", [T, RING])
        run = sb("run", [T, RING + 1, 8])
        wT = sb("wT", [16, RING * T])
        ve2 = sb("ve2", [T, RING, 1])
        scratch = sb("scratch", [T, 1])

        ctxT = sb("ctxT", [C, RING, T])
        bn = sb("bn", [T, RING, 6])
        mv = sb("mv", [T, RING, 2])
        ve = sb("ve", [T, RING, 1])
        rstd = sb("rstd", [T, RING, 1])
        neg_half = sb("neg_half", [T, 32])
        eps_t = sb("eps_t", [T, 2])
        h = sb("h", [T, RING, D])
        hT = sb("hT", [D, RING, T])
        qk = sb("qk", [T, 2, 2, H16, DH])
        parts = sb("parts", [T, RING, 2, H16, 4, DH], F32R)
        vx = sb("vx", [T, RING, 4 * 136])
        ones_x = sb("ones_x", [T, 4, 4, DH])
        qT = sb("qT", [D, RING, T], F32R)
        kx = sb("kx", [D, 2, 4, T], F32R)
        kS = sb("kS", [128, 2, 4, T], F32R)
        qS = sb("qS", [128, 2, 4, 4, T], F32R)
        mx = sb("mx", [T, RING, H16])
        P = sb("P", [T, 2, H16, T])
        rec = sb("rec", [D, T])
        gt = P[:].rearrange("p b h t -> p (b h t)").rearrange("p (n t) -> p n t", t=RING * T)
        oT = sb("oT", [D, RING, T])
        ogT = sb("ogT", [D, RING, T])
        eg = sb("eg", [D, 3, T])
        neg_bgate = sb("neg_bgate", [D, 1])
        causal_q, causal_k = sb("causal_q", [T, 4 * T], F32R), sb("causal_k", [T, 4 * T], F32R)
        qkv = sb("qkv", [T, 192])
        ra, rb = sb("ra", [T, H16 + 4, DH]), sb("rb", [T, H16 + 4, DH])
        rsq, rrs = sb("rsq", [T, H16 + 4]), sb("rrs", [T, H16 + 4])
        ms2 = sb("ms2", [T, RING, 1])
        ve3, rstd2 = sb("ve3", [T, RING, 1]), sb("rstd2", [T, RING, 1])
        keep = sb("keep", [T, GROUPS, RING])

        PS = ctx.enter_context(nc.psum_tensor("PS", [128, 8, 512], F32))
        S_ps, ST_ps = PS[:, 0:2, :], PS[:, 2:4, :]
        TP = [PS[:, 4, :], PS[:, 5, :]]
        FR, OB = PS[:, 6, :], PS[:, 7, :]

        x_dram = a["x"].rearrange("(g s) t d -> t g s d", s=RING)
        out_dram = out.rearrange("(g s) t d -> t g s d", s=RING)
        ctx_dram = a["ctxT"].rearrange("(g s) c t -> c g s t", s=RING)

        consts_ready = sem("consts_ready")
        N_CONSTS = 14
        eps_ready = sem("eps_ready")

        stored = sem("stored")
        x_begin, x_rest = sem("x_begin"), sem("x_rest")
        X_BEGIN = 2

        def stat_stages(at):
            s_st, s_rs, s_h = sem("stats"), sem("rstd"), sem("h")
            s_bn, s_ve, s_hps = sem("bn"), sem("ve"), sem("hps")

            def stats(v, it):
                if due(it.n - RING + 1):
                    v.wait_ge(s_h, at(s_h, it.n - RING + 1))
                if isinstance(it.n, int) and it.n == X_BEGIN * RING:
                    v.wait_ge(x_rest, 16)
                v.bn_stats(bn[:, it.s, :], X[:, it.g, it.s, :]).then_inc(s_bn, 1)

            def aggregate(v, it):
                if isinstance(it.n, int):
                    v.wait_ge(s_bn, at(s_bn, it.n + 1))
                v.bn_aggr(mv[:, it.s, :], bn[:, it.s, :]).then_inc(s_st, 1)

            def rsqrt(q, it):
                q.wait_ge(s_st, at(s_st, it.n + 1))
                q.tensor_tensor(ve[:, it.s, :], mv[:, it.s, 1:2], eps_t[:, 0:1], ALU.add).then_inc(s_ve, 1)
                q.wait_ge(s_ve, at(s_ve, it.n + 1))
                q.tensor_tensor(rstd[:, it.s, :], ve[:, it.s, :], neg_half[:, 0:1], ALU.pow).then_inc(s_rs, 1)

            def norm(v, it, dst):
                if due(it.n - RING + 1):
                    v.wait_ge(s_hps, at(s_hps, it.n - RING + 1))
                v.wait_ge(s_bn, at(s_bn, following(it, 2)))
                v.wait_ge(s_rs, at(s_rs, it.n + 1))
                v.tensor_scalar(dst, X[:, it.g, it.s, :], mv[:, it.s, 0:1], rstd[:, it.s, :],
                                ALU.subtract, ALU.mult).then_inc(s_h, 1)
            return stats, aggregate, rsqrt, norm, s_h

        def attention16(p, before, kind):
            at = counted_from(dict(reached))
            has_bias, masked, causal = kind == "cross", kind == "masked", kind == "self"
            projected = not masked
            n_heads = H16 + 4
            F = 2 if causal else 1
            L = 4 if causal else 2
            G = L + 4
            O = L + 5 if causal else L + 4
            peel = 3

            def own(*names):
                return [sem(n) if causal else None for n in names]
            s_ctx = None if causal else [sem(f"ctx{i}") for i in range(RING)]
            s_hps, s_hT = sem("hps"), sem("hT")
            s_qkv, s_qkf, s_v = sem("qkv"), sem("qkf"), sem("v")
            s_hi, s_lo = sem("hi"), sem("lo")
            s_pad = sem("pad")
            n_pad = 3 if kind == "cross" else 2 if masked else 0
            s_turn, s_kx, s_qT = sem("turn"), sem("kx"), sem("qT")
            s_tk, s_kS, s_tq, s_qS = (sem(n) for n in ("tk", "kS", "tq", "qS"))
            s_s, s_mx = sem("s"), sem("mx")
            s_st, s_exp = sem("st"), sem("exp")
            s_av, s_rec, s_o = sem("av"), sem("rec"), sem("o")
            s_out, s_xb, s_done = sem("out"), sem("xb"), sem("done")
            stats, aggregate, rsqrt, norm, s_h = stat_stages(at)
            s_added = sem("yd") if causal else s_done
            s_fr = sem("fr_read") if causal else s_v
            s_y, s_ms = own("h", "ms")
            s_rope, s_sum, s_rs3, s_gate, s_eg, s_gt = own("rope", "sum", "rs3", "gate", "eg", "gt")
            s_yb, s_yd, s_gt2 = own("yb", "yd", "gt2")
            s_bn, s_rs = sem("bn"), sem("rstd")
            if causal:
                s_h = sem("h2")

            def ahead(e):
                if not causal:
                    for s in range(RING):
                        e.dma_start(ctxT[:, s, :], ctx_dram[:, 0, s, :]).then_inc(s_ctx[s], 16)

            def sync(e):
                if causal:
                    return
                with e.Fori(1, GROUPS, 1) as g:
                    for s in range(RING):
                        e.wait_ge(s_qkv, at(s_qkv, (g - 1) * RING + s + 1))
                        e.dma_start(ctxT[:, s, :], ctx_dram[:, g, s, :]).then_inc(s_ctx[s], 16)

            def pe_hT(e, it):
                e.wait_ge(s_h, at(s_h, it.n + 1))
                before_it = it.n - (L - F) + 1
                if due(before_it):
                    e.wait_ge(s_kx, at(s_kx, before_it))
                    e.wait_ge(s_qT, at(s_qT, before_it))
                e.transpose(FR[:, 0:T], h[:, it.s, :], ident[:, :]).then_inc(s_hps, 1)

            def pe_qkv(e, it):
                e.wait_ge(s_hT, at(s_hT, it.n + 1))
                if causal:
                    m = e.matmul(FR[:, 0:192], hT[:, it.s, :], w[p + "wqkv"][:, :], start=True, stop=True)
                else:
                    e.wait_ge(s_ctx[it.s], at(s_ctx[it.s], 16 * (it.g + 1)))
                    e.matmul(FR[:, 0:D], hT[:, it.s, :], w[p + "wq"][:, :], start=True, stop=True)
                    m = e.matmul(FR[:, D:3 * D], ctxT[:, it.s, :], w[p + "wkv"][:, :], start=True, stop=True)
                m.then_inc(s_qkv, 1)

            def pe_turn(e, it):
                e.wait_ge(s_fr, at(s_fr, following(it, L - F)))
                e.wait_ge(s_qkf, at(s_qkf, (2 if causal else 1) * (it.n + 1)))
                for which in range(2):
                    m = e.transpose(FR[:, which * T:(which + 1) * T],
                                    qk[:, it.s % 2, which, :, :].rearrange("p h d -> p (h d)"), ident[:, :])
                m.then_inc(s_turn, 1)

            def turn_stack(e, it, which, done):
                for g in range(4):
                    m = e.matmul(TP[which][:, g * T:(g + 1) * T],
                                 parts[:, it.s, which, 4 * g:4 * g + 4, :, :].rearrange("p h c d -> p (h c d)"),
                                 ident_r[:, :], start=True, stop=True)
                m.then_inc(done, 1)

            def pe_stack_k(e, it):
                e.wait_ge(s_lo, at(s_lo, 2 * it.n + 2))
                if due(it.n - (O - L - 1)):
                    e.wait_ge(s_added, at(s_added, it.n - (O - L - 1)))
                if causal and due(it.n - (G - L - 1)):
                    e.wait_ge(s_eg, at(s_eg, it.n - (G - L - 1)))
                if due(it.n):
                    e.wait_ge(s_kS, at(s_kS, it.n))
                turn_stack(e, it, 1, s_tk)

            def pe_stack_q(e, it):
                e.wait_ge(s_lo, at(s_lo, 2 * it.n + 2))
                e.wait_ge(s_mx, at(s_mx, 2 * it.n + 2))
                if due(it.n):
                    e.wait_ge(s_qS, at(s_qS, it.n))
                turn_stack(e, it, 0, s_tq)

            def pe_scores(e, it, half):
                if half == 0:
                    e.wait_ge(s_qT, at(s_qT, it.n + 1))
                    e.wait_ge(s_kx, at(s_kx, it.n + 1))
                if due(2 * it.n + half):
                    e.wait_ge(s_mx, at(s_mx, 2 * it.n + half))
                if causal:
                    for i in range(2):
                        e.matmul(S_ps[:, i, :], ident_r[:, :], causal_q[:, :], start=True, stop=False)
                for i in range(2):
                    r = 32 * (2 * half + i)
                    m = e.matmul(S_ps[:, i, :], qT[r:r + 32, it.s, :],
                                 kx[r:r + 32, it.s % 2, :, :].rearrange("p j t -> p (j t)"),
                                 start=not causal, stop=True)
                m.then_inc(s_s, 1)

            def pe_scoresT(e, it, half):
                if half == 0:
                    e.wait_ge(s_kS, at(s_kS, it.n + 1))
                    e.wait_ge(s_qS, at(s_qS, it.n + 1))
                if due(2 * it.n + half):
                    e.wait_ge(s_exp, at(s_exp, 2 * it.n + half))
                for i in range(2):
                    g = 2 * half + i
                    if causal:
                        e.matmul(ST_ps[:, i, :], ident_r[:, :], causal_k[:, :], start=True, stop=False)
                    m = e.matmul(ST_ps[:, i, :], kS[:, it.s % 2, g, :],
                                 qS[:, it.s % 2, g, :, :].rearrange("p j t -> p (j t)"),
                                 start=not causal, stop=True)
                m.then_inc(s_st, 1)

            def pe_values(e, it, what):
                if what == 0:
                    e.wait_ge(s_exp, at(s_exp, 2 * it.n + 2))
                    e.wait_ge(s_v, at(s_v, it.n + 1))
                    if due(it.n):
                        e.wait_ge(s_o, at(s_o, it.n))
                for j in range(4):
                    for g in range(4):
                        lhs = vx[:, it.s, 128 * j + 32 * g:128 * j + 32 * g + 32] if what == 0 else \
                            ones_x[:, j, :, :].rearrange("p a d -> p (a d)")
                        m = e.matmul(OB[32 * g:32 * g + 32, what * T:(what + 1) * T], lhs,
                                     P[:, it.s % 2, 4 * g + j, :], start=(j == 0), stop=(j == 3))
                if what == 1:
                    m.then_inc(s_av, 1)

            def pe_gate(e, it):
                e.wait_ge(s_o, at(s_o, it.n + 1))
                e.wait_ge(s_kS, at(s_kS, following(it, G - L)))
                if due(it.n - (O - G)):
                    e.wait_ge(s_added, at(s_added, it.n - (O - G)))
                e.matmul(TP[1][:, 0:T], w[p + "wgate"][:, :], oT[:, it.s, :], start=True, stop=True).then_inc(s_gate, 1)

            def pe_out(e, it):
                s_in = s_gt if causal else s_o
                e.wait_ge(s_in, at(s_in, it.n + 1))
                e.wait_ge(s_kS, at(s_kS, following(it, O - L)))
                if due(it.n):
                    e.wait_ge(s_added, at(s_added, it.n))
                if causal:
                    e.wait_ge(s_eg, at(s_eg, following(it, O - G + 1)))
                    m = e.matmul(TP[1][:, 0:D], ogT[:, it.s, :], w[p + "wo"][:, :], start=True, stop=True)
                elif projected:
                    m = e.matmul(TP[1][:, 0:D], oT[:, it.s, :], w[p + "wo"][:, :], start=True, stop=True)
                else:
                    m = e.transpose(TP[1][:, 0:D], oT[:, it.s, :], ident[:, :])
                m.then_inc(s_out, 1)

            def tensor(e):
                before(e)
                e.wait_ge(s_pad, at(s_pad, n_pad))
                e.wait_ge(sem(p + "weights"), 16 * n_loads[p[:2]])
                e.wait_ge(consts_ready, N_CONSTS)
                if causal:
                    for item in ticks(e, O, peel):
                        if it := item(L + 2):
                            pe_scoresT(e, it, 0)
                        if it := item(L):
                            pe_turn(e, it)
                        if it := item(L + 3):
                            pe_values(e, it, 0)
                        if it := item(L + 1):
                            pe_stack_q(e, it)
                            pe_stack_k(e, it)
                        if it := item(L):
                            pe_scores(e, it, 0)
                        if it := item(L + 3):
                            pe_values(e, it, 1)
                        if it := item(F):
                            pe_hT(e, it)
                        if it := item(L):
                            pe_scores(e, it, 1)
                        if it := item(G):
                            pe_gate(e, it)
                        if it := item(L + 2):
                            pe_scoresT(e, it, 1)
                        if it := item(F):
                            pe_qkv(e, it)
                        if it := item(O):
                            pe_out(e, it)
                else:
                    for item in ticks(e, O, peel):
                        if it := item(L):
                            pe_turn(e, it)
                        if it := item(L + 1):
                            pe_stack_k(e, it)
                            pe_stack_q(e, it)
                        if it := item(L + 3):
                            pe_values(e, it, 0)
                        if it := item(F):
                            pe_hT(e, it)
                        if it := item(L + 2):
                            pe_scoresT(e, it, 0)
                        if it := item(L):
                            pe_scores(e, it, 0)
                        if it := item(L + 3):
                            pe_values(e, it, 1)
                        if it := item(F):
                            pe_qkv(e, it)
                        if it := item(O):
                            pe_out(e, it)
                        if it := item(L):
                            pe_scores(e, it, 1)
                        if it := item(L + 2):
                            pe_scoresT(e, it, 1)

            def v_qkv(e, it):
                if due(2 * (it.n - 1)):
                    e.wait_ge(s_lo, at(s_lo, 2 * (it.n - 1)))
                if due(it.n - 1):
                    e.wait_ge(s_turn, at(s_turn, it.n - 1))
                e.wait_ge(s_qkv, at(s_qkv, it.n + 1))
                src = FR[:, 0:2 * D]
                dst = qk[:, it.s % 2].rearrange("p a h d -> p (a h d)")
                if has_bias:
                    e.tensor_tensor(dst, src, w[p + "bqk"][:, :], ALU.add).then_inc(s_qkf, 1)
                if masked:
                    e.tensor_scalar(qk[:, it.s % 2, 0].rearrange("p h d -> p (h d)"), FR[:, 0:D],
                                    keep[:, it.g, it.s:it.s + 1], None, ALU.mult)
                    e.tensor_copy(qk[:, it.s % 2, 1].rearrange("p h d -> p (h d)"), FR[:, D:2 * D])\
                     .then_inc(s_qkf, 1)
                if due(it.n - RING + 1):
                    e.wait_ge(s_av, at(s_av, it.n - RING + 1))
                vsrc = FR[:, 2 * D:3 * D].rearrange("p (g j d) -> p j g d", g=4, j=4)
                vdst = vx[:, it.s, :].rearrange("p (j n) -> p j n", j=4)[:, :, 0:128]\
                    .rearrange("p j (g n) -> p j g n", g=4)[:, :, :, 0:DH]
                if has_bias:
                    e.tensor_tensor(vdst, vsrc, w[p + "bv"][:, :].rearrange("p (g j d) -> p j g d", g=4, j=4),
                                    ALU.add).then_inc(s_v, 1)
                if masked:
                    e.tensor_copy(vdst, vsrc).then_inc(s_v, 1)

            def v_rotate(e, it):
                n = [0]

                def step(m):
                    n[0] += 1
                    m.then_inc(s_rope, 1)
                    e.wait_ge(s_rope, at(s_rope, 5 * it.n + n[0]))
                e.wait_ge(s_qkv, at(s_qkv, it.n + 1))
                if due(it.n):
                    e.wait_ge(s_qkf, at(s_qkf, 2 * it.n))
                    e.wait_ge(s_v, at(s_v, it.n))
                e.tensor_tensor(qkv[:, :], FR[:, 0:192], w[p + "bqkv"][:, :], ALU.add).then_inc(s_fr, 1)
                e.wait_ge(s_fr, at(s_fr, it.n + 1))
                x = qkv[:, 0:160].rearrange("p (h d) -> p h d", d=DH)
                cos, sin, neg_sin = (w[p + "rope"][:, i, :].unsqueeze(1).broadcast_to([T, n_heads, DH // 2])
                                     for i in range(3))
                low, high = x[:, :, 0:4], x[:, :, 4:8]
                e.tensor_tensor(ra[:, :, 0:4], low, cos, ALU.mult)
                e.tensor_tensor(ra[:, :, 4:8], high, cos, ALU.mult)
                e.tensor_tensor(rb[:, :, 0:4], high, neg_sin, ALU.mult)
                step(e.tensor_tensor(rb[:, :, 4:8], low, sin, ALU.mult))
                step(e.tensor_tensor(ra[:, :, :], ra[:, :, :], rb[:, :, :], ALU.add))
                step(e.tensor_tensor(rb[:, :, :], ra[:, :, :], ra[:, :, :], ALU.mult))
                step(e.tensor_reduce(rsq[:, :], rb[:, :, :], AXX, ALU.add))
                e.tensor_scalar(rsq[:, :], rsq[:, :], 1.0 / DH, RMS_EPS, ALU.mult, ALU.add).then_inc(s_sum, 1)

            def v_qk_norm(e, it):
                if due(it.n - RING + 1):
                    e.wait_ge(s_av, at(s_av, it.n - RING + 1))
                vdst = vx[:, it.s, :].rearrange("p (j n) -> p j n", j=4)[:, :, 0:128]\
                    .rearrange("p j (g n) -> p j g n", g=4)[:, :, :, 0:DH]
                e.tensor_copy(vdst, qkv[:, 160:192].rearrange("p (g d) -> p g d", g=4).unsqueeze(1)
                              .broadcast_to([T, 4, 4, DH])).then_inc(s_v, 1)
                e.wait_ge(s_rs3, at(s_rs3, it.n + 1))
                e.tensor_tensor(ra[:, :, :], ra[:, :, :], rrs[:, :].unsqueeze(2).broadcast_to([T, n_heads, DH]),
                                ALU.mult).then_inc(s_rope, 1)
                e.wait_ge(s_rope, at(s_rope, 5 * it.n + 5))
                if due(2 * (it.n - 1)):
                    e.wait_ge(s_lo, at(s_lo, 2 * (it.n - 1)))
                if due(it.n - 1):
                    e.wait_ge(s_turn, at(s_turn, it.n - 1))
                e.tensor_tensor(qk[:, it.s % 2, 0], ra[:, 0:H16, :],
                                w[p + "norm"][:, 0, :].unsqueeze(1).broadcast_to([T, H16, DH]), ALU.mult)\
                 .then_inc(s_qkf, 1)
                e.tensor_tensor(qk[:, it.s % 2, 1].rearrange("p (g j) d -> p g j d", g=4),
                                ra[:, H16:n_heads, :].unsqueeze(2).broadcast_to([T, 4, 4, DH]),
                                w[p + "norm"][:, 1, :].unsqueeze(1).unsqueeze(1).broadcast_to([T, 4, 4, DH]),
                                ALU.mult).then_inc(s_qkf, 1)

            def v_y(e, it):
                e.wait_ge(s_bn, at(s_bn, following(it, 2)))
                e.wait_ge(s_rs, at(s_rs, it.n + 1))
                e.tensor_scalar(Y[:, it.g, it.s, :], X[:, it.g, it.s, :], mv[:, it.s, 0:1], rstd[:, it.s, :],
                                ALU.subtract, ALU.mult).then_inc(s_y, 1)

            def v_h2(e, it):
                if due(it.n - RING + 1):
                    e.wait_ge(s_hps, at(s_hps, it.n - RING + 1))
                e.wait_ge(s_ms, at(s_ms, 4 * it.n + 4))
                e.tensor_scalar(h[:, it.s, :], Y[:, it.g, it.s, :], rstd2[:, it.s, :], None, ALU.mult)\
                 .then_inc(s_h, 1)

            def v_gate(e, it):
                e.wait_ge(s_eg, at(s_eg, it.n + 1))
                e.tensor_scalar(eg[:, 1, :], eg[:, 0, :], 1.0, None, ALU.add).then_inc(s_gt2, 1)
                e.wait_ge(s_gt2, at(s_gt2, 2 * it.n + 1))
                e.reciprocal(eg[:, 2, :], eg[:, 1, :]).then_inc(s_gt2, 1)
                e.wait_ge(s_gt2, at(s_gt2, 2 * it.n + 2))
                e.tensor_tensor(ogT[:, it.s, :], oT[:, it.s, :], eg[:, 2, :], ALU.mult).then_inc(s_gt, 1)

            def v_residual_self(e, it):
                e.wait_ge(s_yb, at(s_yb, it.n + 1))
                e.wait_ge(s_out, at(s_out, it.n + 1))
                e.tensor_tensor(Y[:, it.g, it.s, :], Y[:, it.g, it.s, :], TP[1][:, 0:D], ALU.add).then_inc(s_yd, 1)

            def high(e, it):
                if due(it.n - RING + 1):
                    e.wait_ge(s_tq, at(s_tq, it.n - RING + 1))
                e.wait_ge(s_qkf, at(s_qkf, (2 if causal else 1) * (it.n + 1)))
                src = qk[:, it.s % 2].rearrange("p a h d -> p (a h) d").unsqueeze(2).broadcast_to([T, 2 * H16, 3, DH])
                dst = parts[:, it.s, :, :, 0:3, :].rearrange("p a h c d -> p (a h) c d")
                (e.copy if causal else e.tensor_copy)(dst, src).then_inc(s_hi, 1)

            def v_kx(e, it):
                e.wait_ge(s_turn, at(s_turn, it.n + 1))
                e.tensor_tensor(kx[:, it.s % 2, :, :], FR[:, T:2 * T].unsqueeze(1).broadcast_to([D, 4, T]),
                                jmask[:, :].unsqueeze(2).broadcast_to([D, 4, T]), ALU.mult).then_inc(s_kx, 1)

            def v_max(e, it, half):
                if half == 0 and due(it.n - RING + 1):
                    e.wait_ge(s_tq, at(s_tq, it.n - RING + 1))
                e.wait_ge(s_s, at(s_s, 2 * it.n + half + 1))
                e.tensor_reduce(parts[:, it.s, 0, 8 * half:8 * half + 8, 3, 0],
                                S_ps[:, :, :].rearrange("p i (j t) -> p (i j) t", t=T), AXX, ALU.max)\
                 .then_inc(s_mx, 1)

            def v_heads(e, it):
                if due(it.n):
                    e.wait_ge(s_o, at(s_o, it.n))
                e.wait_ge(s_av, at(s_av, it.n + 1))
                e.reciprocal(rec[:, :], OB[:, T:2 * T]).then_inc(s_rec, 1)
                if due(it.n - RING + 1):
                    e.wait_ge(s_out, at(s_out, it.n - RING + 1))
                e.wait_ge(s_rec, at(s_rec, it.n + 1))
                e.tensor_tensor(oT[:, it.s, :], OB[:, 0:T], rec[:, :], ALU.mult).then_inc(s_o, 1)

            def v_residual(e, it):
                if projected:
                    e.wait_ge(s_xb, at(s_xb, it.n + 1))
                e.wait_ge(s_out, at(s_out, it.n + 1))
                e.tensor_tensor(X[:, it.g, it.s, :], X[:, it.g, it.s, :], TP[1][:, 0:D], ALU.add).then_inc(s_done, 1)

            def vector(e):
                before(e)
                e.wait_ge(s_pad, at(s_pad, n_pad))
                e.wait_ge(sem(p + "weights"), 16 * n_loads[p[:2]])
                if causal:
                    for item in ticks(e, O, peel):
                        if it := item(0):
                            stats(e, it)
                        if it := item(F):
                            v_h2(e, it)
                        if it := item(L):
                            v_max(e, it, 0)
                        if it := item(1):
                            v_y(e, it)
                        if it := item(0):
                            aggregate(e, it)
                        if it := item(F + 1):
                            v_qk_norm(e, it)
                        if it := item(L + 3):
                            v_heads(e, it)
                        if it := item(L):
                            v_max(e, it, 1)
                        if it := item(F):
                            v_rotate(e, it)
                        if it := item(O):
                            v_residual_self(e, it)
                        if it := item(G):
                            v_gate(e, it)
                else:
                    for item in ticks(e, O, peel):
                        if it := item(L):
                            v_kx(e, it)
                        if it := item(0):
                            stats(e, it)
                        if it := item(F + 1):
                            high(e, it)
                        if it := item(1):
                            norm(e, it, h[:, it.s, :])
                        if it := item(L):
                            v_max(e, it, 0)
                        if it := item(0):
                            aggregate(e, it)
                        if it := item(L + 3):
                            v_heads(e, it)
                        if it := item(F):
                            v_qkv(e, it)
                        if it := item(O):
                            v_residual(e, it)
                        if it := item(L):
                            v_max(e, it, 1)

            def g_low(e, it):
                e.wait_ge(s_hi, at(s_hi, it.n + 1))
                for which, place in ((0, 2), (1, 1)):
                    e.tensor_tensor(parts[:, it.s, which, :, place, :], qk[:, it.s % 2, which, :, :],
                                    parts[:, it.s, which, :, 0, :].bitcast(F32), ALU.subtract).then_inc(s_lo, 1)

            def g_rsqrt2(e, it):
                n = 4 * it.n
                if due(it.n - RING + 1):
                    e.wait_ge(s_h, at(s_h, it.n - RING + 1))
                e.wait_ge(s_rs, at(s_rs, it.n + 1))
                e.tensor_tensor(ms2[:, it.s, :], mv[:, it.s, 1:2], rstd[:, it.s, :], ALU.mult).then_inc(s_ms, 1)
                e.wait_ge(s_ms, at(s_ms, n + 1))
                e.tensor_tensor(ve3[:, it.s, :], ms2[:, it.s, :], rstd[:, it.s, :], ALU.mult).then_inc(s_ms, 1)
                e.wait_ge(s_ms, at(s_ms, n + 2))
                e.tensor_tensor(ms2[:, it.s, :], ve3[:, it.s, :], eps_t[:, 1:2], ALU.add).then_inc(s_ms, 1)
                e.wait_ge(s_ms, at(s_ms, n + 3))
                e.tensor_tensor(rstd2[:, it.s, :], ms2[:, it.s, :], neg_half[:, 0:1], ALU.pow).then_inc(s_ms, 1)

            def g_rsqrt3(e, it):
                e.wait_ge(s_sum, at(s_sum, it.n + 1))
                e.tensor_tensor(rrs[:, :], rsq[:, :], neg_half[:, 0:n_heads], ALU.pow).then_inc(s_rs3, 1)

            def g_bias_y(e, it):
                e.wait_ge(s_h, at(s_h, it.n + 1))
                e.tensor_tensor(Y[:, it.g, it.s, :], Y[:, it.g, it.s, :], w[p + "bo"][:, :], ALU.add)\
                 .then_inc(s_yb, 1)

            def g_add_y(e, it):
                e.wait_ge(s_yd, at(s_yd, it.n + 1))
                e.tensor_tensor(X[:, it.g, it.s, :], X[:, it.g, it.s, :], Y[:, it.g, it.s, :], ALU.add)\
                 .then_inc(s_done, 1)

            def g_bias(e, it):
                e.wait_ge(s_h, at(s_h, it.n + 1))
                e.tensor_tensor(X[:, it.g, it.s, :], X[:, it.g, it.s, :], w[p + "bo"][:, :], ALU.add)\
                 .then_inc(s_xb, 1)

            def pool(e):
                if kind != "cross":
                    before(e)
                if n_pad >= 2:
                    e.memset(parts[:, :, :, :, 3, :].rearrange("p r a h d -> p (r a h) d").bitcast(F32), 0.0)\
                     .then_inc(s_pad, 1)
                    e.wait_ge(s_pad, at(s_pad, 1))
                    e.memset(parts[:, :, 1, :, 3, 0:1].rearrange("p r h o -> p r (h o)").bitcast(F32), -1.0)\
                     .then_inc(s_pad, 1)
                if kind == "cross":
                    e.memset(qS[:].bitcast(F32), 0.0).then_inc(s_pad, 1)
                    before(e)
                    e.wait_ge(consts_ready, N_CONSTS)
                e.wait_ge(sem(p + "weights"), 16 * n_loads[p[:2]])
                if causal:
                    for item in ticks(e, O, peel):
                        if it := item(0):
                            rsqrt(e, it)
                        if it := item(1):
                            g_rsqrt2(e, it)
                        if it := item(F + 2):
                            g_low(e, it)
                        if it := item(F):
                            g_rsqrt3(e, it)
                        if it := item(O):
                            g_add_y(e, it)
                        if it := item(F):
                            g_bias_y(e, it)
                    return
                for item in ticks(e, F + 1, peel):
                    if it := item(0):
                        rsqrt(e, it)
                    if projected and (it := item(1)):
                        g_bias(e, it)
                    if it := item(F + 1):
                        g_low(e, it)

            def a_kx(e, it):
                e.wait_ge(s_turn, at(s_turn, it.n + 1))
                for j in range(4):
                    m = e.activation(kx[:, it.s % 2, j, :], FR[:, T:2 * T], ACT.Copy, scale=jmask[:, j:j + 1])
                m.then_inc(s_kx, 1)

            def a_qT(e, it):
                e.wait_ge(s_kx, at(s_kx, it.n + 1))
                e.copy(qT[:, it.s, :], FR[:, 0:T]).then_inc(s_qT, 1)

            def a_kS(e, it):
                if due(2 * (it.n - 1)):
                    e.wait_ge(s_st, at(s_st, 2 * (it.n - 1)))
                e.wait_ge(s_tk, at(s_tk, it.n + 1))
                e.copy(kS[:, it.s % 2].rearrange("p g t -> p (g t)"), TP[1]).then_inc(s_kS, 1)

            def a_qS(e, it):
                if due(2 * (it.n - 1)):
                    e.wait_ge(s_st, at(s_st, 2 * (it.n - 1)))
                e.wait_ge(s_tq, at(s_tq, it.n + 1))
                for j in range(4):
                    r = slice(32 * j, 32 * j + 32)
                    m = e.copy(qS[r, it.s % 2, :, j, :], TP[0][r, :].rearrange("p (g t) -> p g t", g=4))
                m.then_inc(s_qS, 1)

            def a_hT(e, it):
                if due(it.n - RING + 1):
                    e.wait_ge(s_qkv, at(s_qkv, it.n - RING + 1))
                e.wait_ge(s_hps, at(s_hps, it.n + 1))
                if causal:
                    e.activation(hT[:, it.s, :], FR[:, 0:T], ACT.Identity, scale=w[p + "ln"][:, 0:1]).then_inc(s_hT, 1)
                else:
                    e.copy(hT[:, it.s, :], FR[:, 0:T]).then_inc(s_hT, 1)

            def a_gate(e, it):
                if due(it.n):
                    e.wait_ge(s_gt, at(s_gt, it.n))
                e.wait_ge(s_gate, at(s_gate, it.n + 1))
                e.activation(eg[:, 0, :], TP[1][:, 0:T], ACT.Exp, bias=neg_bgate[:, 0:1], scale=-1.0).then_inc(s_eg, 1)

            def a_exp(e, it, half):
                if due(it.n - 1):
                    e.wait_ge(s_av, at(s_av, it.n - 1))
                e.wait_ge(s_st, at(s_st, 2 * it.n + half + 1))
                e.activation(P[:, it.s % 2, 8 * half:8 * half + 8, :].rearrange("p h t -> p (h t)"),
                             ST_ps[:, :, :].rearrange("p j n -> p (j n)"), ACT.Exp,
                             scale=float(DH) ** -0.5).then_inc(s_exp, 1)

            def scalar(e):
                before(e)
                e.wait_ge(s_pad, at(s_pad, n_pad))
                if causal:
                    for item in ticks(e, G, peel):
                        if it := item(L):
                            a_kx(e, it)
                            a_qT(e, it)
                        if it := item(L + 1):
                            a_kS(e, it)
                        if it := item(F + 2):
                            high(e, it)
                        if it := item(L + 2):
                            a_exp(e, it, 0)
                        if it := item(L + 1):
                            a_qS(e, it)
                        if it := item(F):
                            a_hT(e, it)
                        if it := item(G):
                            a_gate(e, it)
                        if it := item(L + 2):
                            a_exp(e, it, 1)
                else:
                    for item in ticks(e, L + 3, peel):
                        if it := item(L):
                            a_qT(e, it)
                        if it := item(L + 1):
                            a_qS(e, it)
                            a_kS(e, it)
                        if it := item(L + 2):
                            a_exp(e, it, 0)
                        if it := item(F):
                            a_hT(e, it)
                        if it := item(L + 2):
                            a_exp(e, it, 1)
            totals(stats=B, rstd=B, h=B, bn=B, ve=B, hps=B, hT=B, qkv=B, qkf=B * (2 if causal else 1), v=B,
                   hi=B, lo=2 * B, turn=B, kx=B, qT=B, tk=B, kS=B, tq=B, qS=B, s=2 * B, mx=2 * B,
                   st=2 * B, exp=2 * B, av=B, rec=B, o=B, out=B, done=B, pad=n_pad)
            if projected and not causal:
                totals(xb=B)
            if causal:
                totals(h2=B, ms=4 * B, rope=5 * B, fr_read=B, sum=B, rs3=B, gate=B, eg=B, gt=B, yb=B,
                       yd=B, gt2=2 * B)
            else:
                totals(**{f"ctx{i}": 16 * GROUPS for i in range(RING)})
            return dict(ahead=ahead, sync=sync, tensor=tensor, vector=vector, gpsimd=pool, scalar=scalar,
                        done=(s_done, reached["done"]))

        def attention1(p, before):
            at = counted_from(dict(reached))
            s_ctx = [sem(f"ctx{i}") for i in range(RING)]
            s_hps, s_hT, s_qkv, s_qk, s_v = (sem(n) for n in ("hps", "hT", "qkv", "qk", "v"))
            s_s, s_mx, s_nb, s_exp, s_pps, s_pT = (sem(n) for n in ("s", "mx", "nb", "exp", "pps", "pT"))
            s_av, s_rec, s_done = (sem(n) for n in ("av", "rec", "done"))
            stats, aggregate, rsqrt, norm, s_h = stat_stages(at)
            pool_f = P[:].rearrange("p b h t -> p (b h t)")
            q1, k1, v1, p1, pT1 = (pool_f[:, 512 * i:512 * i + 512].rearrange("p (r t) -> p r t", r=RING)
                                   for i in range(5))
            scale = float(D) ** -0.5
            QKV = [FR, PS[:, 3, :]]

            def ahead(e):
                for s in range(RING):
                    e.dma_start(ctxT[:, s, :], ctx_dram[:, 0, s, :]).then_inc(s_ctx[s], 16)

            def sync(e):
                with e.Fori(1, GROUPS, 1) as g:
                    for s in range(RING):
                        e.wait_ge(s_qkv, at(s_qkv, (g - 1) * RING + s + 1))
                        e.dma_start(ctxT[:, s, :], ctx_dram[:, g, s, :]).then_inc(s_ctx[s], 16)

            def tensor(e):
                def pe_hT(it):
                    e.wait_ge(s_h, at(s_h, it.n + 1))
                    if due(it.n):
                        e.wait_ge(s_hT, at(s_hT, it.n))
                    e.transpose(PS[:, 2, 0:T], h[:, it.s, :], ident[:, :]).then_inc(s_hps, 1)

                def pe_qkv(it):
                    e.wait_ge(s_hT, at(s_hT, it.n + 1))
                    if due(it.n - 1):
                        e.wait_ge(s_v, at(s_v, it.n - 1))
                    bank = QKV[it.s % 2]
                    e.wait_ge(s_ctx[it.s], at(s_ctx[it.s], 16 * (it.g + 1)))
                    e.matmul(bank[:, 0:T], w[p + "wq"][:, :], hT[:, it.s, :], start=True, stop=True)
                    e.matmul(bank[:, T:2 * T], w[p + "wk"][:, :], ctxT[:, it.s, :], start=True, stop=True)
                    e.matmul(bank[:, 2 * T:3 * T], ctxT[:, it.s, :], w[p + "wv"][:, :], start=True, stop=True)\
                     .then_inc(s_qkv, 1)

                def pe_scores(it):
                    e.wait_ge(s_qk, at(s_qk, 2 * it.n + 2))
                    if due(it.n):
                        e.wait_ge(s_exp, at(s_exp, it.n))
                    e.matmul(PS[:, 0, 0:T], q1[:, it.s, :], k1[:, it.s, :], start=True, stop=True).then_inc(s_s, 1)

                def pe_pT(it):
                    e.wait_ge(s_exp, at(s_exp, it.n + 1))
                    if due(it.n):
                        e.wait_ge(s_pT, at(s_pT, it.n))
                    e.transpose(PS[:, 4, 0:T], p1[:, it.s, :], ident[:, :]).then_inc(s_pps, 1)

                def pe_values(it):
                    e.wait_ge(s_pT, at(s_pT, it.n + 1))
                    if due(it.n):
                        e.wait_ge(s_done, at(s_done, it.n))
                    e.matmul(OB[:, 0:T], pT1[:, it.s, :], v1[:, it.s, :], start=True, stop=True).then_inc(s_av, 1)
                before(e)
                e.wait_ge(sem(p + "weights"), 16 * n_loads[p[:2]])
                e.wait_ge(consts_ready, N_CONSTS)
                for item in ticks(e, 5):
                    if it := item(5):
                        pe_values(it)
                    if it := item(2):
                        pe_qkv(it)
                    if it := item(4):
                        pe_pT(it)
                    if it := item(3):
                        pe_scores(it)
                    if it := item(1):
                        pe_hT(it)

            def vector(e):
                def v_qkv(it):
                    if due(it.n - RING + 1):
                        e.wait_ge(s_done, at(s_done, it.n - RING + 1))
                    e.wait_ge(s_qkv, at(s_qkv, it.n + 1))
                    bank = QKV[it.s % 2]
                    e.tensor_scalar(q1[:, it.s, :], bank[:, 0:T], w[p + "bq"][:, 0:1], None, ALU.add).then_inc(s_qk, 1)
                    e.tensor_scalar(k1[:, it.s, :], bank[:, T:2 * T], w[p + "bk"][:, 0:1], None, ALU.add)\
                     .then_inc(s_qk, 1)
                    e.tensor_tensor(v1[:, it.s, :], bank[:, 2 * T:3 * T], w[p + "bv"][:, :], ALU.add).then_inc(s_v, 1)

                def v_max(it):
                    e.wait_ge(s_s, at(s_s, it.n + 1))
                    e.tensor_reduce(mx[:, it.s, 0:1], PS[:, 0, 0:T], AXX, ALU.max).then_inc(s_mx, 1)
                    e.wait_ge(s_mx, at(s_mx, it.n + 1))
                    e.tensor_scalar(mx[:, it.s, 1:2], mx[:, it.s, 0:1], -scale, None, ALU.mult).then_inc(s_nb, 1)

                def v_out(it):
                    e.wait_ge(s_av, at(s_av, it.n + 1))
                    e.reciprocal(mx[:, it.s, 3:4], mx[:, it.s, 2:3]).then_inc(s_rec, 1)
                    e.wait_ge(s_rec, at(s_rec, it.n + 1))
                    e.scalar_tensor_tensor(out=X[:, it.g, it.s, :], in0=OB[:, 0:T], scalar=mx[:, it.s, 3:4],
                                           in1=X[:, it.g, it.s, :], op0=ALU.mult, op1=ALU.add).then_inc(s_done, 1)
                before(e)
                e.wait_ge(sem(p + "weights"), 16 * n_loads[p[:2]])
                for item in ticks(e, 5):
                    if it := item(0):
                        stats(e, it)
                    if it := item(1):
                        norm(e, it, h[:, it.s, :])
                    if it := item(5):
                        v_out(it)
                    if it := item(3):
                        v_max(it)
                    if it := item(0):
                        aggregate(e, it)
                    if it := item(2):
                        v_qkv(it)

            def pool(e):
                before(e)
                e.memset(qS[:].bitcast(F32), 0.0).then_inc(sem("pad"), 1)
                for item in ticks(e, 0):
                    if it := item(0):
                        rsqrt(e, it)

            def scalar(e):
                def a_hT(it):
                    if due(it.n - RING + 1):
                        e.wait_ge(s_qkv, at(s_qkv, it.n - RING + 1))
                    e.wait_ge(s_hps, at(s_hps, it.n + 1))
                    e.copy(hT[:, it.s, :], PS[:, 2, 0:T]).then_inc(s_hT, 1)

                def a_exp(it):
                    e.wait_ge(s_nb, at(s_nb, it.n + 1))
                    e.activation(p1[:, it.s, :], PS[:, 0, 0:T], ACT.Exp, scale=scale, bias=mx[:, it.s, 1:2],
                                 accum_out=mx[:, it.s, 2:3]).then_inc(s_exp, 1)

                def a_pT(it):
                    e.wait_ge(s_pps, at(s_pps, it.n + 1))
                    e.copy(pT1[:, it.s, :], PS[:, 4, 0:T]).then_inc(s_pT, 1)
                before(e)
                for item in ticks(e, 4):
                    if it := item(4):
                        a_pT(it)
                    if it := item(1):
                        a_hT(it)
                    if it := item(3):
                        a_exp(it)
            totals(stats=B, rstd=B, h=B, bn=B, ve=B, hps=B, hT=B, qkv=B, qk=2 * B, v=B, s=B, mx=B, nb=B,
                   exp=B, pps=B, pT=B, av=B, rec=B, done=B, pad=1)
            totals(**{f"ctx{i}": 16 * GROUPS for i in range(RING)})
            return dict(ahead=ahead, sync=sync, tensor=tensor, vector=vector, gpsimd=pool, scalar=scalar,
                        done=(s_done, reached["done"]))

        def attention8(p, before):
            at = counted_from(dict(reached))
            NH, HD = 8, 64
            s_ctx = [sem(f"ctx{i}") for i in range(RING)]
            s_hps, s_hT, s_q, s_k, s_vps, s_v = (sem(n) for n in ("hps", "hT", "q", "k", "vps", "v"))
            s_qH, s_kH, s_qL, s_kL = (sem(n) for n in ("qH", "kH", "qL", "kL"))
            s_s, s_mx, s_md, s_st, s_exp = (sem(n) for n in ("s", "mx", "md", "st", "exp"))
            s_av, s_rec, s_o, s_ops, s_oT = (sem(n) for n in ("av", "rec", "o", "ops", "oT"))
            s_out, s_xb, s_done, s_pad = (sem(n) for n in ("out", "xb", "done", "pad"))
            stats, aggregate, rsqrt, norm, s_h = stat_stages(at)
            flat = P[:].rearrange("p b h t -> p (b h t)")
            P8 = flat[:, 0:2048].rearrange("p (b h t) -> p b h t", b=2, h=NH)
            VW = 584
            v8 = flat[:, 2048:2048 + 2 * VW].rearrange("p (b n) -> p b n", b=2)
            q8 = qS[:].rearrange("p b g j t -> p (b g j t)").rearrange("p (b a u t) -> p b a u t", b=2, a=2, t=2 * T)
            kH, kL = kx, kS
            md = parts[:].rearrange("p r a h c d -> p (r a h c d)")[:, 0:2048]\
                .rearrange("p (b h t) -> p b h t", b=2, h=NH)
            vflat = vx[:].rearrange("p r n -> p (r n)")
            o8 = vflat[:, 0:1024].rearrange("p (b n) -> p b n", b=2)
            oT8 = vflat[:, 1024:2048].rearrange("p (b n) -> p b n", b=2)

            def ahead(e):
                for s in range(RING):
                    e.dma_start(ctxT[:, s, :], ctx_dram[:, 0, s, :]).then_inc(s_ctx[s], 16)

            def sync(e):
                with e.Fori(1, GROUPS, 1) as g:
                    for s in range(RING):
                        e.wait_ge(s_vps, at(s_vps, (g - 1) * RING + s + 1))
                        e.dma_start(ctxT[:, s, :], ctx_dram[:, g, s, :]).then_inc(s_ctx[s], 16)

            def tensor(e):
                def pe_hT(it):
                    e.wait_ge(s_h, at(s_h, it.n + 1))
                    if due(it.n - 2):
                        e.wait_ge(s_v, at(s_v, it.n - 2))
                    e.transpose(FR[:, 0:T], h[:, it.s, :], ident[:, :]).then_inc(s_hps, 1)

                def pe_qk(it):
                    e.wait_ge(s_hT, at(s_hT, it.n + 1))
                    if due(2 * it.n):
                        e.wait_ge(s_qL, at(s_qL, 2 * it.n))
                    for t in range(4):
                        m = e.matmul(TP[0][:, t * T:(t + 1) * T], w[p + "wq"][:, t * 128:(t + 1) * 128],
                                     hT[:, it.s, :], start=True, stop=True)
                    m.then_inc(s_q, 1)
                    e.wait_ge(s_ctx[it.s], at(s_ctx[it.s], 16 * (it.g + 1)))
                    if due(it.n):
                        e.wait_ge(s_kL, at(s_kL, it.n))
                    for t in range(4):
                        m = e.matmul(TP[1][:, t * T:(t + 1) * T], w[p + "wk"][:, t * 128:(t + 1) * 128],
                                     ctxT[:, it.s, :], start=True, stop=True)
                    m.then_inc(s_k, 1)

                def pe_v(it):
                    e.wait_ge(s_hT, at(s_hT, following(it, 3)))
                    e.matmul(FR[:, :], ctxT[:, it.s, :], w[p + "wv"][:, :], start=True, stop=True).then_inc(s_vps, 1)

                def pe_scores(it):
                    e.wait_ge(s_qH, at(s_qH, 2 * it.n + 2))
                    e.wait_ge(s_kH, at(s_kH, it.n + 1))
                    if due(it.n):
                        e.wait_ge(s_mx, at(s_mx, it.n))
                    for hd in range(NH):
                        t, u = hd // 2, hd % 2
                        m = e.matmul(S_ps[:, hd // 4, (hd % 4) * T:(hd % 4 + 1) * T],
                                     q8[:, it.s % 2, 0, t, u * T:(u + 1) * T], kH[:, it.s % 2, t, :],
                                     start=True, stop=True)
                    m.then_inc(s_s, 1)

                def pe_scoresT(it):
                    e.wait_ge(s_md, at(s_md, it.n + 1))
                    e.wait_ge(s_qL, at(s_qL, 2 * it.n + 2))
                    e.wait_ge(s_kL, at(s_kL, it.n + 1))
                    if due(it.n):
                        e.wait_ge(s_exp, at(s_exp, it.n))
                    for b in range(2):
                        e.matmul(ST_ps[:, b, :], minus_ones[:, :],
                                 md[:, it.s % 2, 4 * b:4 * b + 4, :].rearrange("p h t -> p (h t)"),
                                 start=True, stop=False)
                        for t in (2 * b, 2 * b + 1):
                            dst = ST_ps[:, b, (t % 2) * 2 * T:(t % 2 + 1) * 2 * T]
                            for kk, a_ in ((kH, 0), (kL, 0), (kH, 1)):
                                m = e.matmul(dst, kk[:, it.s % 2, t, :], q8[:, it.s % 2, a_, t, :],
                                             start=False, stop=(t == 2 * b + 1 and kk is kH and a_ == 1))
                    m.then_inc(s_st, 1)

                def pe_values(it, half):
                    if half == 0:
                        e.wait_ge(s_exp, at(s_exp, it.n + 1))
                        e.wait_ge(s_v, at(s_v, it.n + 1))
                        if due(it.n):
                            e.wait_ge(s_done, at(s_done, it.n))
                    else:
                        e.wait_ge(s_o, at(s_o, 2 * it.n + 1))
                    for i in range(4):
                        hd = 4 * half + i
                        m = e.matmul(OB[:, i * T:(i + 1) * T], P8[:, it.s % 2, hd, :],
                                     v8[:, it.s % 2, hd * (HD + 1):hd * (HD + 1) + T], start=True, stop=True)
                    m.then_inc(s_av, 1)

                def pe_oT(it):
                    e.wait_ge(s_o, at(s_o, 2 * it.n + 2))
                    for t in range(4):
                        m = e.transpose(OB[:, t * T:(t + 1) * T], o8[:, it.s % 2, t * 128:(t + 1) * 128], ident[:, :])
                    m.then_inc(s_ops, 1)

                def pe_out(it):
                    e.wait_ge(s_oT, at(s_oT, it.n + 1))
                    for t in range(4):
                        m = e.matmul(OB[:, 0:D], oT8[:, it.s % 2, t * T:(t + 1) * T], w[p + "wo"][:, t, :],
                                     start=(t == 0), stop=(t == 3))
                    m.then_inc(s_out, 1)
                before(e)
                e.wait_ge(sem(p + "weights"), 16 * n_loads[p[:2]])
                e.wait_ge(consts_ready, N_CONSTS)
                e.wait_ge(s_pad, at(s_pad, 2))
                for item in ticks(e, 5):
                    if it := item(5):
                        pe_out(it)
                    if it := item(3):
                        pe_scoresT(it)
                    if it := item(4):
                        pe_values(it, 0)
                    if it := item(2):
                        pe_scores(it)
                    if it := item(1):
                        pe_hT(it)
                    if it := item(4):
                        pe_values(it, 1)
                    if it := item(3):
                        pe_v(it)
                    if it := item(4):
                        pe_oT(it)
                    if it := item(1):
                        pe_qk(it)

            def vector(e):
                def v_low(it):
                    e.wait_ge(s_qH, at(s_qH, 2 * it.n + 2))
                    for u in range(2):
                        r = slice(64 * u, 64 * u + 64)
                        e.tensor_tensor(q8[r, it.s % 2, 1, :, u * T:(u + 1) * T],
                                        TP[0][r, :].rearrange("p (t n) -> p t n", t=4),
                                        q8[r, it.s % 2, 0, :, u * T:(u + 1) * T].bitcast(F32),
                                        ALU.subtract).then_inc(s_qL, 1)
                    e.wait_ge(s_kH, at(s_kH, it.n + 1))
                    e.tensor_tensor(kL[:, it.s % 2, :, :].rearrange("p t n -> p (t n)"), TP[1][:, :],
                                    kH[:, it.s % 2, :, :].rearrange("p t n -> p (t n)").bitcast(F32),
                                    ALU.subtract).then_inc(s_kL, 1)

                def v_max(it):
                    e.wait_ge(s_s, at(s_s, it.n + 1))
                    e.tensor_reduce(mx[:, it.s, 0:NH], S_ps[:, :, :].rearrange("p i (j t) -> p (i j) t", t=T),
                                    AXX, ALU.max).then_inc(s_mx, 1)

                def v_heads(it, half):
                    e.wait_ge(s_av, at(s_av, 2 * it.n + half + 1))
                    ob = OB[:, :].rearrange("p (h n) -> p h n", n=T)
                    e.reciprocal(rec[:, 0:4].unsqueeze(2), ob[:, :, HD:HD + 1]).then_inc(s_rec, 1)
                    if half == 0:
                        if due(it.n - 1):
                            e.wait_ge(s_ops, at(s_ops, it.n - 1))
                    e.wait_ge(s_rec, at(s_rec, 2 * it.n + half + 1))
                    e.tensor_tensor(o8[:, it.s % 2, 256 * half:256 * half + 256].rearrange("p (h n) -> p h n", h=4),
                                    ob[:, :, 0:HD], rec[:, 0:4].unsqueeze(2).broadcast_to([T, 4, HD]),
                                    ALU.mult).then_inc(s_o, 1)

                def v_residual(it):
                    e.wait_ge(s_xb, at(s_xb, it.n + 1))
                    e.wait_ge(s_out, at(s_out, it.n + 1))
                    e.tensor_tensor(X[:, it.g, it.s, :], X[:, it.g, it.s, :], OB[:, 0:D], ALU.add).then_inc(s_done, 1)
                before(e)
                e.wait_ge(sem(p + "weights"), 16 * n_loads[p[:2]])
                for item in ticks(e, 5):
                    if it := item(0):
                        stats(e, it)
                    if it := item(5):
                        v_residual(it)
                    if it := item(2):
                        v_low(it)
                    if it := item(1):
                        norm(e, it, h[:, it.s, :])
                    if it := item(4):
                        v_heads(it, 0)
                    if it := item(2):
                        v_max(it)
                    if it := item(4):
                        v_heads(it, 1)
                    if it := item(0):
                        aggregate(e, it)

            def pool(e):
                def g_bias(it):
                    e.wait_ge(s_h, at(s_h, it.n + 1))
                    e.tensor_tensor(X[:, it.g, it.s, :], X[:, it.g, it.s, :], w[p + "bo"][:, :], ALU.add)\
                     .then_inc(s_xb, 1)

                def g_diagonals(it):
                    if due(it.n - 1):
                        e.wait_ge(s_st, at(s_st, it.n - 1))
                    e.wait_ge(s_mx, at(s_mx, it.n + 1))
                    e.tensor_tensor(md[:, it.s % 2], ident[:, :].unsqueeze(1).broadcast_to([T, NH, T]),
                                    mx[:, it.s, 0:NH].unsqueeze(2).broadcast_to([T, NH, T]),
                                    ALU.mult).then_inc(s_md, 1)
                before(e)
                e.wait_ge(sem(p + "weights"), 16 * n_loads[p[:2]])
                e.memset(qS[:].bitcast(F32), 0.0).then_inc(s_pad, 1)
                e.memset(v8[:, :, :], 1.0).then_inc(s_pad, 1)
                for item in ticks(e, 2):
                    if it := item(1):
                        g_bias(it)
                    if it := item(2):
                        g_diagonals(it)
                    if it := item(0):
                        rsqrt(e, it)

            def scalar(e):
                def a_high(it):
                    if due(it.n - 1):
                        e.wait_ge(s_st, at(s_st, it.n - 1))
                    e.wait_ge(s_q, at(s_q, it.n + 1))
                    for u in range(2):
                        r = slice(64 * u, 64 * u + 64)
                        e.copy(q8[r, it.s % 2, 0, :, u * T:(u + 1) * T],
                               TP[0][r, :].rearrange("p (t n) -> p t n", t=4)).then_inc(s_qH, 1)
                    e.wait_ge(s_k, at(s_k, it.n + 1))
                    e.copy(kH[:, it.s % 2, :, :].rearrange("p t n -> p (t n)"), TP[1][:, :]).then_inc(s_kH, 1)

                def a_hT(it):
                    if due(it.n - RING + 1):
                        e.wait_ge(s_q, at(s_q, it.n - RING + 1))
                    e.wait_ge(s_hps, at(s_hps, it.n + 1))
                    e.copy(hT[:, it.s, :], FR[:, 0:T]).then_inc(s_hT, 1)

                def a_exp(it):
                    if due(2 * (it.n - 1)):
                        e.wait_ge(s_av, at(s_av, 2 * (it.n - 1)))
                    e.wait_ge(s_st, at(s_st, it.n + 1))
                    e.activation(P8[:, it.s % 2, :, :].rearrange("p h t -> p (h t)"),
                                 ST_ps[:, :, :].rearrange("p j n -> p (j n)"), ACT.Exp,
                                 scale=float(HD) ** -0.5).then_inc(s_exp, 1)

                def a_v(it):
                    if due(2 * (it.n - 1)):
                        e.wait_ge(s_av, at(s_av, 2 * (it.n - 1)))
                    e.wait_ge(s_vps, at(s_vps, it.n + 1))
                    e.copy(v8[:, it.s % 2, 0:NH * (HD + 1)].rearrange("p (h n) -> p h n", h=NH)[:, :, 0:HD],
                           FR[:, :].rearrange("p (h n) -> p h n", h=NH)).then_inc(s_v, 1)

                def a_oT(it):
                    if due(it.n - 1):
                        e.wait_ge(s_out, at(s_out, it.n - 1))
                    e.wait_ge(s_ops, at(s_ops, it.n + 1))
                    e.copy(oT8[:, it.s % 2, :], OB[:, :]).then_inc(s_oT, 1)
                before(e)
                e.wait_ge(s_pad, at(s_pad, 2))
                for item in ticks(e, 4):
                    if it := item(2):
                        a_high(it)
                    if it := item(3):
                        a_exp(it)
                    if it := item(1):
                        a_hT(it)
                    if it := item(4):
                        a_oT(it)
                    if it := item(3):
                        a_v(it)
            totals(stats=B, rstd=B, h=B, bn=B, ve=B, hps=B, hT=B, q=B, k=B, vps=B, v=B, qH=2 * B, kH=B,
                   qL=2 * B, kL=B, s=B, mx=B, md=B, st=B, exp=B, av=2 * B, rec=2 * B, o=2 * B, ops=B,
                   oT=B, out=B, xb=B, done=B, pad=2)
            totals(**{f"ctx{i}": 16 * GROUPS for i in range(RING)})
            return dict(ahead=ahead, sync=sync, tensor=tensor, vector=vector, gpsimd=pool, scalar=scalar,
                        done=(s_done, reached["done"]))

        def experts(p, before, E, tiles, kind, top_k, source, shared=False):
            at = counted_from(dict(reached))
            n_exp = E + (1 if shared else 0)
            n_z = {"gelu": tiles, "relu": tiles, "glu": 2 * tiles, "linear": 0}[kind] * n_exp
            per_e = n_z // n_exp
            s_bn, s_st, s_ms = sem("bn"), sem("stats"), sem("ms")
            s_ve, s_rs, s_h = sem("ve"), sem("rstd"), sem("h")
            s_hps, s_hT, s_lg = sem("hps"), sem("hT"), sem("logits")
            s_r, s_e = sem("route"), sem("exp")
            s_wt, s_wps, s_wT = sem("wt"), sem("wps"), sem("wT")
            s_loc, s_locr = sem("loc"), sem("loc_read")
            s_z, s_g, s_sig = sem("z"), sem("g"), sem("sig")
            s_y, s_acc, s_done = sem("y"), sem("acc"), sem("done")
            rms = kind == "glu"
            wg, b2 = w[p + "wg"], w.get(p + "b2")
            w1, b1, w2 = w.get(p + "w1"), w.get(p + "b1"), w[p + "w2"]
            STATS, NORM, TURN, LOGITS, ROUTE = 1, 2, 3, 5, 6
            n_steps = n_exp + (1 if b2 is not None else 0)
            ZP = [PS[:, bank, :] for bank in (0, 1, 6, 7)]
            YP = [PS[:, 2, :], PS[:, 3, :]]
            HP, LP = PS[:, 4, :], PS[:, 5, :]
            WP = HP if n_z else PS[:, 6, :]
            if n_z:
                s_wh, s_wl, s_hH, s_hL = (sem(n) for n in ("w_high", "w_low", "rows_high", "rows_low"))
                n_cuts = n_z // 4
                w_in = w1.rearrange("p x n -> p (x n)").rearrange("p (c n) -> p c n", n=512)
                w_high = parts[:].rearrange("p r a h c d -> p (r a h c d)").rearrange("p (c n) -> p c n", n=512)
                w_low = w_high[:, n_cuts:2 * n_cuts] if n_cuts <= 4 else \
                    qS[:].rearrange("p b g j t -> p (b g j t)").rearrange("p (c n) -> p c n", n=512)
                hH, hL = (buf[:].rearrange("p b j t -> p b (j t)") for buf in (kx, kS))

            def groups(e, prologue, body):
                before(e)
                e.wait_ge(sem(p + "weights"), 16 * n_loads[p[:2]])
                e.wait_ge(consts_ready, N_CONSTS)
                prologue()
                body(0, 0, True)
                with e.Fori(0, GROUPS // 2 - 1, 1) as pair:
                    body(2 * pair + 1, 1, True)
                    body(2 * pair + 2, 0, True)
                body(GROUPS - 1, (GROUPS - 1) % 2, False)

            def tensor(e):
                def prep(g, b):
                    for s in range(RING):
                        e.wait_ge(s_h, at(s_h, RING * g + s + 1))
                        if s == 0 and due(g):
                            e.wait_ge(s_hT, at(s_hT, g))
                            if b2 is not None and n_z:
                                e.wait_ge(s_wT, at(s_wT, g))
                        m = e.transpose(HP[:, s * T:(s + 1) * T], h[:, s, :], ident[:, :])
                        m.then_inc(s_hps, 1)

                def logits(g, b):
                    if due(n_route * (g - 1) + 1):
                        e.wait_ge(s_r, at(s_r, n_route * (g - 1) + 1))
                    e.wait_ge(s_hT, at(s_hT, g + 1))
                    for s in range(RING):
                        m = e.matmul(LP[:, s * E:(s + 1) * E], hT4[:, b, s * T:(s + 1) * T], wg[:, :],
                                     start=True, stop=True)
                    m.then_inc(s_lg, 1)

                def z(g, b, i):
                    if due(zfree(g, i)):
                        e.wait_ge(s_g, at(s_g, zfree(g, i)))
                    if i == 0:
                        e.wait_ge(s_hL, at(s_hL, g + 1))
                    if isinstance(g, int) and g == 0 and i % 4 == 0:
                        e.wait_ge(s_wl, at(s_wl, i // 4 + 1))
                    c, n = i // 4, slice(i % 4 * 128, i % 4 * 128 + 128)
                    e.matmul(ZP[i % 4][:, :], w_high[:, c, n], hH[:, b], start=True, stop=False)
                    e.matmul(ZP[i % 4][:, :], w_low[:, c, n], hH[:, b], start=False, stop=False)
                    e.matmul(ZP[i % 4][:, :], w_high[:, c, n], hL[:, b], start=False, stop=True)\
                     .then_inc(s_z, 1)

                def zfree(g, i):
                    if kind == "glu":
                        return tiles * n_exp * g + i // 2 - 1
                    return n_z * g + i - 3

                def y(g, b, x):
                    k = n_exp * g + x
                    if due(RING * (n_steps * g + x - 1)):
                        e.wait_ge(s_acc, at(s_acc, RING * (n_steps * g + x - 1)))
                    if kind != "linear":
                        e.wait_ge(s_g, at(s_g, tiles * (k + 1)))
                    for s in range(RING):
                        for t in range(tiles):
                            lhs = hT4[:, b, s * T:(s + 1) * T] if kind == "linear" else \
                                gt[:, (x % 2) * tiles + t, s * T:(s + 1) * T]
                            m = e.matmul(YP[(n_steps * b + x) % 2][:, s * T:(s + 1) * T], lhs, w2[:, x, t * D:(t + 1) * D],
                                         start=(t == 0), stop=(t == tiles - 1))
                    m.then_inc(s_y, 1)

                def bias(g, b):
                    if due(g):
                        e.wait_ge(s_wT, at(s_wT, g))
                    e.wait_ge(s_wt, at(s_wt, g + 1))
                    for s in range(RING):
                        m = e.transpose(WP[0:n_exp, s * T:(s + 1) * T], wt[:, b, s, 0:n_exp], ident[:, :])
                    m.then_inc(s_wps, 1)

                def bias_rows(g, b):
                    e.wait_ge(s_wT, at(s_wT, g + 1))
                    if due(RING * (n_steps * g + n_exp - 1)):
                        e.wait_ge(s_acc, at(s_acc, RING * (n_steps * g + n_exp - 1)))
                    for s in range(RING):
                        m = e.matmul(YP[(n_steps * b + n_exp) % 2][:, s * T:(s + 1) * T], wT[0:n_exp, s * T:(s + 1) * T],
                                     b2[:, :], start=True, stop=True)
                    m.then_inc(s_y, 1)

                def positions(g):
                    if due(g):
                        e.wait_ge(s_wT, at(s_wT, g))
                    e.wait_ge(s_r, at(s_r, n_route * g + n_before_loc))
                    for s in range(RING):
                        e.matmul(WP[:, s * E:(s + 1) * E], earlier[:, :], sel[:, s, 0:E], start=True, stop=False)
                        m = e.matmul(WP[:, s * E:(s + 1) * E], ones[:, :], run[:, s, :], start=False, stop=True)
                    m.then_inc(s_loc, 1)

                def prologue():
                    prep(0, 0)
                    logits(0, 0)
                    if kind == "linear":
                        positions(0)

                def body(g, b, more):
                    for x in range(n_exp + 1):
                        if x < n_exp:
                            for t in range(per_e):
                                z(g, b, x * per_e + t)
                        if x == TURN and more:
                            prep(g + 1, 1 - b)
                        if x == LOGITS and more:
                            logits(g + 1, 1 - b)
                        if kind == "linear" and x == ROUTE + 1 and more:
                            positions(g + 1)
                        if x >= 1:
                            y(g, b, x - 1)
                        if b2 is not None and x == 1:
                            bias(g, b)
                    if b2 is not None:
                        bias_rows(g, b)
                groups(e, prologue, body)

            def vector(e):
                def statistics(g):
                    for s in range(RING):
                        if due(RING * (g - 1) + s + 1):
                            e.wait_ge(s_hps, at(s_hps, RING * (g - 1) + s + 1))
                        e.bn_stats(bn[:, s, :], source[:, g, s, :]).then_inc(s_bn, 1)
                    e.wait_ge(s_bn, at(s_bn, RING * (g + 1)))
                    e.tensor_copy(scratch[:, 0:1], neg_half[:, 0:1])
                    for s in range(RING):
                        m = e.bn_aggr(mv[:, s, :], bn[:, s, :])
                        m.then_inc(s_st, 1)
                    if rms:
                        e.wait_ge(s_st, at(s_st, RING * (g + 1)))
                        e.tensor_tensor(ve[:, :, :], mv[:, :, 0:1], mv[:, :, 0:1], ALU.mult).then_inc(s_ms, 1)
                        e.wait_ge(s_ms, at(s_ms, 2 * g + 1))
                        e.tensor_tensor(mv[:, :, 1:2], mv[:, :, 1:2], ve[:, :, :], ALU.add).then_inc(s_ms, 1)

                def norm(g):
                    e.wait_ge(s_rs, at(s_rs, g + 1))
                    for s in range(RING):
                        if rms:
                            m = e.tensor_scalar(h[:, s, :], source[:, g, s, :], rstd[:, s, :], None, ALU.mult)
                        else:
                            m = e.tensor_scalar(h[:, s, :], source[:, g, s, :], mv[:, s, 0:1], rstd[:, s, :],
                                                ALU.subtract, ALU.mult)
                        m.then_inc(s_h, 1)

                def bc(t):
                    return t[:, :].unsqueeze(2).broadcast_to([T, RING, E])

                def route(g, b):
                    n = [0]

                    def step(m):
                        n[0] += 1
                        m.then_inc(s_r, 1)
                        e.wait_ge(s_r, at(s_r, n_route * g + n[0]))
                    e.wait_ge(s_lg, at(s_lg, g + 1))
                    lp = LP[:, 0:RING * E].rearrange("p (s x) -> p s x", s=RING)
                    if p + "bg" in w:
                        step(e.tensor_tensor(lg[:, :, 0:E], lp,
                                             w[p + "bg"][:, :].unsqueeze(1).broadcast_to([T, RING, E]), ALU.add))
                    else:
                        step(e.tensor_copy(lg[:, :, 0:E], lp))
                    L, SEL, TMP = lg[:, :, 0:E], sel[:, :, 0:E], tmp[:, :, 0:E]
                    for k in range(top_k):
                        step(e.tensor_reduce(rmax[:, :], L, AXX, ALU.max))
                        if k == 0 and kind != "glu":
                            step(e.tensor_tensor(pr[:, :, 0:E], L, bc(rmax), ALU.subtract))
                        step(e.tensor_tensor(TMP, L, bc(rmax), ALU.is_equal))
                        step(e.tensor_tensor(TMP, TMP, rank[:, 0:E].unsqueeze(1).broadcast_to([T, RING, E]), ALU.mult))
                        step(e.tensor_reduce(rmax[:, :], TMP, AXX, ALU.max))
                        if top_k > 1:
                            yield
                        if k == 0:
                            step(e.tensor_tensor(SEL, TMP, bc(rmax), ALU.is_equal))
                            one = SEL
                        else:
                            step(e.tensor_tensor(TMP, TMP, bc(rmax), ALU.is_equal))
                            step(e.tensor_tensor(SEL, SEL, TMP, ALU.add))
                            one = TMP
                        if k < top_k - 1:
                            step(e.scalar_tensor_tensor(out=L, in0=one, scalar=-BIG, in1=L, op0=ALU.mult, op1=ALU.add))
                            yield
                    if kind == "linear":
                        for s in range(RING):
                            step(e.tensor_tensor(run[:, s + 1, :], run[:, s, :], sel[:, s, 0:E], ALU.add))
                        assert n[0] == n_before_loc
                        yield
                        e.wait_ge(s_loc, at(s_loc, g + 1))
                        loc = WP[:, 0:RING * E].rearrange("p (s x) -> p s x", s=RING)
                        e.tensor_scalar(tmp[:, :, 0:E], loc, float(B * T // E), None, ALU.is_lt).then_inc(s_locr, 1)
                        e.wait_ge(s_locr, at(s_locr, g + 1))
                        step(e.tensor_tensor(SEL, SEL, TMP, ALU.mult))
                        step(e.tensor_copy(run[:, 0, :], run[:, RING, :]))
                    if kind != "glu":
                        e.wait_ge(s_e, at(s_e, g + 1))
                        step(e.tensor_reduce(rsum[:, :], pr[:, :, 0:E], AXX, ALU.add))
                        step(e.reciprocal(rsum[:, :], rsum[:, :]))
                        step(e.tensor_tensor(pr[:, :, 0:E], pr[:, :, 0:E], bc(rsum), ALU.mult))
                        e.tensor_tensor(wt[:, b, :, 0:E], SEL, pr[:, :, 0:E], ALU.mult).then_inc(s_wt, 1)
                    else:
                        e.tensor_copy(wt[:, b, :, 0:E], SEL).then_inc(s_wt, 1)
                    assert n[0] == n_route, n[0]

                def add(g, b, x):
                    k = n_steps * g + x
                    e.wait_ge(s_y, at(s_y, k + 1))
                    if x == 0:
                        e.wait_ge(s_wt, at(s_wt, g + 1))
                    for s in range(RING):
                        if due(RING * (k - 1) + s + 1):
                            e.wait_ge(s_acc, at(s_acc, RING * (k - 1) + s + 1))
                        X_s = X[:, g, s, :]
                        rows = YP[(n_steps * b + x) % 2][:, s * T:(s + 1) * T]
                        if x < E:
                            m = e.scalar_tensor_tensor(out=X_s, in0=rows, scalar=wt[:, b, s, x:x + 1], in1=X_s,
                                                       op0=ALU.mult, op1=ALU.add)
                        else:
                            m = e.tensor_tensor(X_s, X_s, rows, ALU.add)
                        m.then_inc(s_acc, 1)

                def product(g, i):
                    x, t = i // tiles, i % tiles
                    if due(n_steps * g + x - 1):
                        e.wait_ge(s_y, at(s_y, n_steps * g + x - 1))
                    e.wait_ge(s_sig, at(s_sig, tiles * n_exp * g + i + 1))
                    e.scalar_tensor_tensor(out=gt[:, (x % 2) * tiles + t, :], in0=ZP[2 * (i % 2)][:, :],
                                           scalar=b1[:, x, t:t + 1], in1=sg[:, i % 2, :],
                                           op0=ALU.add, op1=ALU.mult).then_inc(s_g, 1)

                def prologue():
                    if kind == "linear":
                        e.memset(run[:, 0, :], 0.0).then_inc(s_ms, 1)
                        e.wait_ge(s_ms, at(s_ms, 1))
                    if shared:
                        e.memset(wt[:, :, :, E:E + 1], 1.0).then_inc(s_ms, 1)
                    statistics(0)
                    norm(0)
                    if n_z:
                        for c in range(n_cuts):
                            e.wait_ge(s_wh, at(s_wh, c + 1))
                            e.tensor_tensor(w_low[:, c, :], w_in[:, c, :], w_high[:, c, :].bitcast(F32),
                                            ALU.subtract).then_inc(s_wl, 1)
                    for _ in route(0, 0):
                        pass

                def body(g, b, more):
                    pieces = route(g + 1, 1 - b)
                    for x in range(n_steps + 1):
                        if kind == "glu" and x < n_exp:
                            for t in range(tiles):
                                product(g, x * tiles + t)
                        if x == STATS and more:
                            statistics(g + 1)
                        if x == NORM and more:
                            norm(g + 1)
                        if x >= ROUTE and more:
                            next(pieces, None)
                        if x >= 1:
                            add(g, b, x - 1)
                groups(e, prologue, body)

            def pool(e):
                def rs(g):
                    if rms:
                        e.wait_ge(s_ms, at(s_ms, 2 * (g + 1)))
                    else:
                        e.wait_ge(s_st, at(s_st, RING * (g + 1)))
                    e.tensor_tensor(ve2[:, :, :], mv[:, :, 1:2],
                                    eps_t[:, int(rms):int(rms) + 1].unsqueeze(1).broadcast_to([T, RING, 1]),
                                    ALU.add).then_inc(s_ve, 1)
                    e.wait_ge(s_ve, at(s_ve, g + 1))
                    if due(RING * g):
                        e.wait_ge(s_h, at(s_h, RING * g))
                    e.tensor_tensor(rstd[:, :, :], ve2[:, :, :], neg_half[:, 0:RING].unsqueeze(2), ALU.pow)\
                     .then_inc(s_rs, 1)

                def low_rows(g, b):
                    e.wait_ge(s_hH, at(s_hH, g + 1))
                    e.tensor_tensor(hL[:, b], hT4[:, b], hH[:, b].bitcast(F32), ALU.subtract).then_inc(s_hL, 1)

                def prologue():
                    rs(0)
                    if n_z:
                        low_rows(0, 0)

                def body(g, b, more):
                    if more:
                        rs(g + 1)
                        if n_z:
                            low_rows(g + 1, 1 - b)
                groups(e, prologue, body)

            def scalar(e):
                def turn(g, b):
                    if due(g - 1):
                        e.wait_ge(s_lg, at(s_lg, g - 1))
                        if n_z:
                            e.wait_ge(s_hL, at(s_hL, g - 1))
                            e.wait_ge(s_z, at(s_z, n_z * (g - 1)))
                        else:
                            e.wait_ge(s_y, at(s_y, n_steps * (g - 1)))
                    e.wait_ge(s_hps, at(s_hps, RING * (g + 1)))
                    if rms:
                        m = e.activation(hT4[:, b], HP[:, :], ACT.Identity, scale=w[p + "ln"][:, 0:1])
                    else:
                        m = e.copy(hT4[:, b], HP[:, :])
                    m.then_inc(s_hT, 1)
                    if n_z:
                        e.wait_ge(s_hT, at(s_hT, g + 1))
                        e.copy(hH[:, b], hT4[:, b]).then_inc(s_hH, 1)

                def round_weights():
                    for c in range(n_cuts):
                        e.copy(w_high[:, c, :], w_in[:, c, :]).then_inc(s_wh, 1)

                def prologue():
                    if n_z:
                        round_weights()
                    turn(0, 0)
                    if kind != "glu":
                        route_exp(0)

                def route_exp(g):
                    e.wait_ge(s_r, at(s_r, n_route * g + 3))
                    e.activation(pr[:, :, 0:E], pr[:, :, 0:E], ACT.Exp).then_inc(s_e, 1)

                def hidden(g, i):
                    x, t = i // per_e, i % per_e
                    if kind == "glu":
                        if t % 2 == 0:
                            return
                        j = i // 2
                        if due(tiles * n_exp * g + j - 1):
                            e.wait_ge(s_g, at(s_g, tiles * n_exp * g + j - 1))
                        e.wait_ge(s_z, at(s_z, n_z * g + i + 1))
                        e.activation(sg[:, j % 2, :], ZP[i % 4][:, :], ACT.Sigmoid,
                                     bias=b1[:, x, tiles + t // 2:tiles + t // 2 + 1]).then_inc(s_sig, 1)
                        return
                    if due(n_steps * g + x - 1 if x >= 2 else bound(g, x)):
                        e.wait_ge(s_y, at(s_y, n_steps * g + x - 1 if x >= 2 else bound(g, x)))
                    e.wait_ge(s_z, at(s_z, n_z * g + i + 1))
                    e.activation(gt[:, (x % 2) * tiles + t, :], ZP[i % 4][:, :],
                                 ACT.Gelu if kind == "gelu" else ACT.Relu,
                                 bias=b1[:, x, t:t + 1]).then_inc(s_g, 1)

                def bound(g, x):
                    last = n_exp - 2 + x
                    same = last if last % 2 == x % 2 else last + 1
                    return n_steps * (g - 1) + min(same, n_exp - 1) + 1

                def turn_weights(g):
                    if due(n_steps * g):
                        e.wait_ge(s_y, at(s_y, n_steps * g))
                    e.wait_ge(s_wps, at(s_wps, g + 1))
                    e.copy(wT[0:n_exp, :], WP[0:n_exp, :]).then_inc(s_wT, 1)

                def body(g, b, more):
                    for x in range(n_exp):
                        for t in range(per_e):
                            hidden(g, x * per_e + t)
                        if b2 is not None and x == 1:
                            turn_weights(g)
                        if x == TURN and more:
                            turn(g + 1, 1 - b)
                        if x == ROUTE and more and kind != "glu":
                            route_exp(g + 1)
                groups(e, prologue, body)

            n_route = 1
            for k in range(top_k):
                n_route += 1 + (1 if k == 0 and kind != "glu" else 0) + 3
                n_route += 1 if k == 0 else 2
                n_route += 1 if k < top_k - 1 else 0
            n_before_loc = n_route + RING
            if kind == "linear":
                n_route += RING + 2
            if kind != "glu":
                n_route += 3

            hidden_steps = n_z // 2 if kind == "glu" else n_z
            totals(bn=B, stats=B, h=B, hps=B, ve=GROUPS, rstd=GROUPS, hT=GROUPS, logits=GROUPS,
                   route=n_route * GROUPS, wt=GROUPS, z=n_z * GROUPS, g=hidden_steps * GROUPS,
                   y=n_steps * GROUPS, acc=RING * n_steps * GROUPS)
            if kind == "glu":
                totals(ms=2 * GROUPS, sig=hidden_steps * GROUPS)
            else:
                totals(exp=GROUPS)
            totals(ms=int(kind == "linear") + int(shared))
            if n_z:
                totals(w_low=n_cuts, w_high=n_cuts, rows_high=GROUPS, rows_low=GROUPS)
            if kind == "linear":
                totals(loc=GROUPS, loc_read=GROUPS)
            if b2 is not None:
                totals(wps=GROUPS, wT=GROUPS)

            def sync(e):
                if kind == "linear":
                    with e.Fori(0, GROUPS, 1) as g:
                        e.wait_ge(s_acc, at(s_acc, RING * n_steps * (g + 1)))
                        e.dma_start(out_dram[:, g], X[:, g]).then_inc(stored, 16)
            return dict(ahead=lambda e: None, sync=sync, tensor=tensor, vector=vector, gpsimd=pool, scalar=scalar,
                        done=(s_acc, reached["acc"]))

        n_loads = {}
        for ph, _, _ in loads:
            n_loads[ph] = n_loads.get(ph, 0) + 1

        def first(e):
            e.wait_ge(x_begin, 16)
            e.wait_ge(sem("a0_weights"), 16 * n_loads["a0"])

        phases = []

        def follow(make, *args, **kw):
            if phases:
                s_before, count = phases[-1]["done"]
                phases.append(make(args[0], lambda e: e.wait_ge(s_before, count), *args[1:], **kw))
            else:
                phases.append(make(args[0], first, *args[1:], **kw))

        follow(attention16, "a0_", "cross")
        follow(experts, "f0_", 8, 4, "gelu", 1, X)
        follow(attention1, "a1_")
        follow(experts, "f1_", 15, 1, "relu", 3, X, shared=True)
        follow(attention16, "a2_", "masked")
        follow(attention16, "b2_", "self")
        follow(experts, "f2_", 8, 2, "glu", 1, Y)
        follow(attention8, "a3_")
        follow(experts, "f3_", 8, 1, "linear", 1, X)
        late = {1: "f2", 3: "f3"}
        block = ctx.enter_context(nc.Block())

        @block.sync
        def _(e):
            def load(name):
                for ph, tile, arr in loads:
                    if ph == name:
                        e.dma_start(tile, arr).then_inc(sem(ph + "_weights"), 16)
            e.dma_start(X[:, 0:X_BEGIN], x_dram[:, 0:X_BEGIN]).then_inc(x_begin, 16)
            phases[0]["ahead"](e)
            load("a0")
            e.wait_ge(x_begin, 16)
            e.wait_ge(sem("a0_weights"), 16 * n_loads["a0"])
            e.dma_start(X[:, X_BEGIN:], x_dram[:, X_BEGIN:]).then_inc(x_rest, 16)
            for ph, tile, arr in loads:
                if ph not in ("a0", "f2", "f3"):
                    e.dma_start(tile, arr).then_inc(sem(ph + "_weights"), 16)
            for n, p in enumerate(phases):
                p["sync"](e)
                if n + 1 < len(phases):
                    if n > 0:
                        e.wait_ge(*phases[n - 1]["done"])
                    phases[n + 1]["ahead"](e)
                if n in late:
                    e.wait_ge(*p["done"])
                    load(late[n])
            e.wait_ge(stored, 16 * GROUPS)

        @block.tensor
        def _(e):
            for p in phases:
                p["tensor"](e)

        @block.vector
        def _(e):
            e.memset(neg_half[:], -0.5).then_inc(consts_ready, 1)
            e.memset(vx[:], 0.0).then_inc(consts_ready, 1)
            e.memset(ones_x[:], 0.0).then_inc(consts_ready, 1)
            e.memset(ones[:], 1.0).then_inc(consts_ready, 1)
            e.wait_ge(consts_ready, 4)
            for j in range(4):
                e.memset(ones_x[:, j, j, :], 1.0).then_inc(consts_ready, 1)
            e.wait_ge(sem("a0_weights"), 16 * n_loads["a0"])
            e.tensor_copy(ident_r[:], ident[:]).then_inc(consts_ready, 1)
            e.tensor_scalar(minus_ones[:], ones[:], -1.0, None, ALU.mult).then_inc(consts_ready, 1)
            e.tensor_copy(keep[:].rearrange("p g s -> p (g s)"), keep_words[:].bitcast(U8)).then_inc(consts_ready, 1)
            for i, dst in enumerate((causal_q, causal_k)):
                e.tensor_copy(dst[:].rearrange("p (j t) -> p j t", j=4),
                              causal_in[:, i, :].unsqueeze(1).broadcast_to([T, 4, T])).then_inc(consts_ready, 1)
            e.tensor_scalar(neg_bgate[:], w["b2_bgate"][:], -1.0, None, ALU.mult).then_inc(consts_ready, 1)
            for p in phases:
                p["vector"](e)

        @block.gpsimd
        def _(e):
            e.memset(eps_t[:, 0:1], EPS).then_inc(eps_ready, 1)
            e.memset(eps_t[:, 1:2], RMS_EPS).then_inc(eps_ready, 1)
            e.wait_ge(eps_ready, 2)
            for p in phases:
                p["gpsimd"](e)

        @block.scalar
        def _(e):
            for p in phases:
                p["scalar"](e)


def layout(i):
    def rows(v, n=128):
        return np.broadcast_to(v, (n,) + v.shape).reshape(n, -1)
    a = {}
    a["x"] = i["x"]
    a["ctxT"] = i["ctx_768"].transpose(0, 2, 1)
    a["ident"] = np.eye(128, dtype=np.float32)
    a["jmask"] = np.tile(np.repeat(np.eye(4, dtype=np.float32), DH, 0), (4, 1))
    a["a0_wq"] = i["L0_xattn_wq"].T
    a["a0_wkv"] = np.concatenate([i["L0_xattn_wk"].T, i["L0_xattn_wv"].T], 1)
    a["a0_bqk"] = rows(np.concatenate([i["L0_xattn_bq"], i["L0_xattn_bk"]]))
    a["a0_bv"] = rows(i["L0_xattn_bv"])
    a["a0_wo"] = i["L0_xattn_wo"].T
    a["a0_bo"] = rows(i["L0_xattn_bo"])
    a["a1_wq"], a["a1_wk"], a["a1_wv"] = i["L1_xattn_Wq"], i["L1_xattn_Wk"], i["L1_xattn_Wv"]
    a["a1_bq"], a["a1_bk"] = i["L1_xattn_bq"].reshape(D, 1), i["L1_xattn_bk"].reshape(D, 1)
    a["a1_bv"] = rows(i["L1_xattn_bv"])
    a["a3_wq"], a["a3_wk"], a["a3_wv"] = i["L3_xattn_Wq"], i["L3_xattn_Wk"], i["L3_xattn_Wv"]
    a["a3_wo"] = i["L3_xattn_Wo"].reshape(4, 128, D).transpose(1, 0, 2)
    a["a3_bo"] = rows(i["L3_xattn_bo"])
    a["keep"] = np.ascontiguousarray(i["mask_BxS_bk0"].T).view(np.int32)
    q, k = np.arange(T)[:, None], np.arange(T)[None, :]
    a["causal"] = np.stack([np.where(k > q, -BIG, 0), np.where(q > k, -BIG, 0)], 1).astype(np.float32)
    a["a2_wq"], a["a2_wkv"] = i["L2_xattn_Wq"].T, i["L2_xattn_Wkv"].T
    a["b2_wqkv"] = np.concatenate([i["L2_ffn_Wq"], i["L2_ffn_Wk"], i["L2_ffn_Wv"]], 1)
    a["b2_bqkv"] = rows(np.concatenate([i["L2_ffn_bq"], i["L2_ffn_bk"], i["L2_ffn_bv"]]))
    freq = 1.0 / 10000.0 ** (np.arange(0, DH, 2, dtype=np.float32) / DH)
    angle = np.arange(T, dtype=np.float32)[:, None] * freq.astype(np.float32)[None, :]
    a["b2_rope"] = np.stack([np.cos(angle), np.sin(angle), -np.sin(angle)], 1).astype(np.float32)
    a["b2_norm"] = rows(np.concatenate([i["L2_ffn_qn_w"], i["L2_ffn_kn_w"]])).reshape(T, 2, DH)
    a["b2_ln"] = i["L2_ffn_ln1_w"].reshape(D, 1)
    gate = np.zeros((H16, DH, H16, DH), np.float32)
    for head in range(H16):
        gate[head, :, head, :] = i["L2_ffn_Wg"]
    a["b2_wgate"] = gate.reshape(D, D)
    a["b2_bgate"] = np.tile(i["L2_ffn_bg"], H16).reshape(D, 1)
    a["b2_wo"], a["b2_bo"] = i["L2_ffn_Wo"], rows(i["L2_ffn_bo"])
    a["rank"] = rows(16.0 - np.arange(16, dtype=np.float32))
    a["earlier"] = np.triu(np.ones((T, T), np.float32), 1)

    def hidden_bias(v):
        return v.reshape(v.shape[0], -1, 128).transpose(2, 0, 1)

    def down(v):
        return v.reshape(v.shape[0], -1, 128, D).transpose(2, 0, 1, 3).reshape(128, v.shape[0], -1)
    a["f0_wg"], a["f0_bg"] = i["L0_ffn_gate_w"], rows(i["L0_ffn_gate_b"])
    a["f0_w1"], a["f0_b1"] = i["L0_ffn_w1"].transpose(1, 0, 2), hidden_bias(i["L0_ffn_b1"])
    a["f0_w2"], a["f0_b2"] = down(i["L0_ffn_w2"]), i["L0_ffn_b2"]
    a["f1_wg"], a["f1_bg"] = i["L1_ffn_router_W"], rows(i["L1_ffn_router_b"])

    def with_shared(e, s):
        return np.concatenate([i["L1_ffn_" + e], i["L1_ffn_" + s][None]], 0)
    a["f1_w1"] = with_shared("eW1", "sW1").transpose(1, 0, 2)
    a["f1_b1"] = hidden_bias(with_shared("eb1", "sb1"))
    a["f1_w2"], a["f1_b2"] = down(with_shared("eW2", "sW2")), with_shared("eb2", "sb2")
    a["f2_ln"] = i["L2_ffn_ln2_w"].reshape(D, 1)
    a["f2_wg"], a["f2_bg"] = i["L2_ffn_Wr"], rows(i["L2_ffn_br"])
    order = [0, 2, 1, 3]
    a["f2_w1"] = i["L2_ffn_W1"].reshape(8, D, 4, 128)[:, :, order].reshape(8, D, 512).transpose(1, 0, 2)
    a["f2_b1"] = hidden_bias(i["L2_ffn_b1"])
    a["f2_w2"], a["f2_b2"] = down(i["L2_ffn_W2"]), i["L2_ffn_b2"]
    a["f3_wg"] = i["L3_ffn_wg"]
    a["f3_w2"], a["f3_b2"] = i["L3_ffn_W"].transpose(2, 0, 1), i["L3_ffn_b"]
    return a


def kernel(**inputs):
    import concourse.bacc as bacc
    from concourse.bass_utils import run_bass_kernel_spmd as run

    nc = bacc.Bacc("TRN2", target_bir_lowering=False, num_devices=1)
    laid = layout({k: np.asarray(v) for k, v in inputs.items()})
    arrays, aps = {}, {}
    for name, v in laid.items():
        v = np.ascontiguousarray(v)
        arrays["in_" + name] = v
        aps[name] = nc.dram_tensor("in_" + name, v.shape, mybir.dt.from_np(v.dtype), kind="ExternalInput").ap()
    out = nc.dram_tensor("out", (B, T, D), F32, kind="ExternalOutput").ap()
    build(nc, aps, out)
    r = run(nc, [arrays], core_ids=[0])
    return r.results[0]["out"]
```
